# Optimizing a Trainium2 kernel written in Bass

```python
import numpy as np
import jax
import jax.numpy as jnp

def _softmax(x, axis=-1):
    return jax.nn.softmax(x, axis=axis)

def _gelu(x):
    return jax.nn.gelu(x, approximate=True)

def _silu(x):
    return jax.nn.silu(x)

def _sigmoid(x):
    return jax.nn.sigmoid(x)

def _layernorm(x, axis=-1, eps=1e-05):
    m = jnp.mean(x, axis=axis, keepdims=True)
    v = jnp.var(x, axis=axis, keepdims=True)
    return (x - m) / jnp.sqrt(v + eps)

def _scatter_add(tgt, idx, src, axis=0):
    return tgt.at[idx].add(src)

def _segment_sum(src, seg, n):
    return jax.ops.segment_sum(src, seg, n)
kernel_name = 'mk_decoder_postln_d2_seqx_r4_03483b'

def setup_inputs(seed: int=0):
    np.random.seed(seed)
    _w = jnp.asarray

    def _rec_inputs():
        import jax
        import jax.numpy as jnp
        _rk = jax.random.key(seed)
        x = -0.0005207 + 1.001 * jax.random.normal(jax.random.fold_in(_rk, 1), (16, 128, 256), jnp.float32)
        _lenS = 128 - jax.random.randint(jax.random.fold_in(_rk, 7), (16,), 0, max(1, 128 // 4) + 1, jnp.int32)
        _lenS2 = 128 - jax.random.randint(jax.random.fold_in(_rk, 8), (16,), 0, max(1, 128 // 4) + 1, jnp.int32)
        _ctx_512P = jax.random.normal(jax.random.fold_in(_rk, 11), (16, 16, 128), jnp.float32)
        _ctx_512c = jax.random.dirichlet(jax.random.fold_in(_rk, 511), 0.3 * jnp.ones((16,), jnp.float32), (16, 128))
        _ctx_512t = jnp.einsum('bsk,bkd->bsd', _ctx_512c, _ctx_512P)
        _ctx_512t = _ctx_512t * jax.lax.rsqrt(jnp.mean(jnp.square(_ctx_512t)) + 1e-12) * 0.953939
        ctx_512 = 0.502058 + 0.29099 * (_ctx_512t + 0.3 * jax.random.normal(jax.random.fold_in(_rk, 611), (16, 128, 128), jnp.float32))
        itok_BxS2xS_0_7 = jax.random.randint(jax.random.fold_in(_rk, 12), (16, 128, 128), 0, 8, jnp.int32)
        return (x, ctx_512, itok_BxS2xS_0_7)
    x, ctx_512, itok_BxS2xS_0_7 = _rec_inputs()

    def _L0_attn_setup():
        import jax, jax.numpy as jnp
        import numpy as np
        B, S, D, H, DH = (4, 512, 256, 16, 64)
        INIT_STD = 0.02
        IGNORE = -100000.0
        key = jax.random.key(seed)
        ks = jax.random.split(key, 5)
        x = jax.random.normal(ks[0], (B, S, D), dtype=jnp.float32)
        W_Q = INIT_STD * jax.random.normal(ks[1], (H, D, DH), dtype=jnp.float32)
        W_K = INIT_STD * jax.random.normal(ks[2], (H, D, DH), dtype=jnp.float32)
        W_V = INIT_STD * jax.random.normal(ks[3], (H, D, DH), dtype=jnp.float32)
        W_O = INIT_STD * jax.random.normal(ks[4], (H, DH, D), dtype=jnp.float32)
        b_Q = jnp.zeros((H, DH), dtype=jnp.float32)
        b_K = jnp.zeros((H, DH), dtype=jnp.float32)
        b_V = jnp.zeros((H, DH), dtype=jnp.float32)
        b_O = jnp.zeros((D,), dtype=jnp.float32)
        return {'x': x, 'W_Q': W_Q, 'b_Q': b_Q, 'W_K': W_K, 'b_K': b_K, 'W_V': W_V, 'b_V': b_V, 'W_O': W_O, 'b_O': b_O}
    _L0_attn_all = _L0_attn_setup()
    _L0_attn_in = {k: v for k, v in _L0_attn_all.items() if k in ('W_Q', 'b_Q', 'W_K', 'b_K', 'W_V', 'b_V', 'W_O', 'b_O')}
    del _L0_attn_all

    def _L0_xattn_setup():
        import jax, jax.numpy as jnp
        import numpy as np
        key = jax.random.key(seed)
        k1, k2, k3, k4, k5 = jax.random.split(key, 5)
        B, K, S, E, I, D = (4, 2, 128, 8, 256, 512)
        x = jax.random.normal(k1, (B, S, I), dtype=jnp.float32)
        weights = jax.random.uniform(k2, (B, K, S), dtype=jnp.float32)
        ensembles = jax.random.randint(k3, (B, K, S), 0, E, dtype=jnp.int64)
        lim1 = float(np.sqrt(6.0 / (D + I)))
        proj_in = jax.random.uniform(k4, (E, D, I), dtype=jnp.float32, minval=-lim1, maxval=lim1)
        proj_out = jax.random.uniform(k5, (E, I, D), dtype=jnp.float32, minval=-lim1, maxval=lim1)
        return {'x': x, 'weights': weights, 'ensembles': ensembles, 'proj_in': proj_in, 'proj_out': proj_out}
    _L0_xattn_all = _L0_xattn_setup()
    _L0_xattn_in = {k: v for k, v in _L0_xattn_all.items() if k in ('proj_in', 'proj_out')}
    del _L0_xattn_all

    def _L0_ffn_setup():
        import jax, jax.numpy as jnp
        import numpy as np
        HIDDEN = 256
        N_ROUTED = 16
        N_SHARED = 2
        TOP_K = 2
        MID_R = HIDDEN // 4
        MID_S = HIDDEN // 2
        key = jax.random.key(seed)
        ks = jax.random.split(key, 8)
        s = 0.02
        return {'x': jax.random.normal(ks[0], (2, 256, HIDDEN), dtype=jnp.float32), 'router_w': jax.random.normal(ks[1], (HIDDEN, N_ROUTED), dtype=jnp.float32) * s, 'wg_r': jax.random.normal(ks[2], (N_ROUTED, HIDDEN, MID_R), dtype=jnp.float32) * s, 'wu_r': jax.random.normal(ks[3], (N_ROUTED, HIDDEN, MID_R), dtype=jnp.float32) * s, 'wd_r': jax.random.normal(ks[4], (N_ROUTED, MID_R, HIDDEN), dtype=jnp.float32) * s, 'wg_s': jax.random.normal(ks[5], (N_SHARED, HIDDEN, MID_S), dtype=jnp.float32) * s, 'wu_s': jax.random.normal(ks[6], (N_SHARED, HIDDEN, MID_S), dtype=jnp.float32) * s, 'wd_s': jax.random.normal(ks[7], (N_SHARED, MID_S, HIDDEN), dtype=jnp.float32) * s}
    _L0_ffn_all = _L0_ffn_setup()
    _L0_ffn_in = {k: v for k, v in _L0_ffn_all.items() if k in ('router_w', 'wg_r', 'wu_r', 'wd_r', 'wg_s', 'wu_s', 'wd_s')}
    del _L0_ffn_all

    def _L1_attn_setup():
        import jax, jax.numpy as jnp
        import numpy as np
        B, N, C, H, W = (2, 512, 256, 16, 8)
        HD = C // H
        SCALE = HD ** (-0.5)

        def band_mask(n, w):
            i = jnp.arange(n)[:, None]
            j = jnp.arange(n)[None, :]
            lo = jnp.where(i <= w, 0, i - w)
            hi = jnp.where(n - i <= w, n - 1, i + w)
            return (j >= lo) & (j <= hi)
        key = jax.random.key(seed)
        k1, k2, k3 = jax.random.split(key, 3)
        x = jax.random.normal(k1, (B, N, C), dtype=jnp.float32)
        Wqkv = jax.random.normal(k2, (C, 3 * C), dtype=jnp.float32) * C ** (-0.5)
        Wproj = jax.random.normal(k3, (C, C), dtype=jnp.float32) * C ** (-0.5)
        bproj = jnp.zeros((C,), dtype=jnp.float32)
        return {'x': x, 'Wqkv': Wqkv, 'Wproj': Wproj, 'bproj': bproj}
    _L1_attn_all = _L1_attn_setup()
    _L1_attn_in = {k: v for k, v in _L1_attn_all.items() if k in ('Wqkv', 'Wproj', 'bproj')}
    del _L1_attn_all

    def _L1_xattn_setup():
        import jax, jax.numpy as jnp
        import numpy as np
        HEADS = 16
        D_MODEL = 256
        IMG_MODEL = 128
        D_K = D_MODEL // HEADS
        key = jax.random.key(seed)
        ks = jax.random.split(key, 12)
        B, LQ, LKV = (8, 512, 256)
        s_dm = 1.0 / np.sqrt(D_MODEL)
        s_im = 1.0 / np.sqrt(IMG_MODEL)
        return {'q': jax.random.normal(ks[0], (B, LQ, D_MODEL), jnp.float32), 'k': jax.random.normal(ks[1], (B, LKV, IMG_MODEL), jnp.float32), 'v': jax.random.normal(ks[2], (B, LKV, IMG_MODEL), jnp.float32), 'Wq': jax.random.normal(ks[3], (D_MODEL, D_MODEL), jnp.float32) * s_dm, 'bq': jnp.zeros((D_MODEL,), jnp.float32), 'Wk': jax.random.normal(ks[4], (IMG_MODEL, D_MODEL), jnp.float32) * s_im, 'bk': jnp.zeros((D_MODEL,), jnp.float32), 'Wv': jax.random.normal(ks[5], (IMG_MODEL, D_MODEL), jnp.float32) * s_im, 'bv': jnp.zeros((D_MODEL,), jnp.float32), 'Wo': jax.random.normal(ks[6], (D_MODEL, D_MODEL), jnp.float32) * s_dm, 'bo': jnp.zeros((D_MODEL,), jnp.float32)}
    _L1_xattn_all = _L1_xattn_setup()
    _L1_xattn_in = {k: v for k, v in _L1_xattn_all.items() if k in ('Wq', 'bq', 'Wk', 'bk', 'Wv', 'bv', 'Wo', 'bo')}
    del _L1_xattn_all

    def _L1_ffn_setup():
        import jax, jax.numpy as jnp
        import numpy as np
        TEMPERATURE = 0.5
        CAPACITY_FACTOR = 1.25
        TOP_K = 1
        key = jax.random.key(seed)
        ks = jax.random.split(key, 5)
        B, S, D, H, E = (4, 512, 256, 512, 8)
        s = 0.02
        return {'x': jax.random.normal(ks[0], (B, S, D), jnp.float32), 'gate_w': jax.random.normal(ks[1], (E, D), jnp.float32) * s, 'gate_b': jnp.zeros((E,), jnp.float32), 'rms_w': jnp.ones((E,), jnp.float32), 'w1': jax.random.normal(ks[2], (E, D, H), jnp.float32) * s, 'b1': jnp.zeros((E, H), jnp.float32), 'w2': jax.random.normal(ks[3], (E, H, D), jnp.float32) * s, 'b2': jnp.zeros((E, D), jnp.float32)}
    _L1_ffn_all = _L1_ffn_setup()
    _L1_ffn_in = {k: v for k, v in _L1_ffn_all.items() if k in ('gate_w', 'gate_b', 'rms_w', 'w1', 'b1', 'w2', 'b2')}
    del _L1_ffn_all
    return {'x': x, 'ctx_512': ctx_512, 'itok_BxS2xS_0_7': itok_BxS2xS_0_7, 'L0_attn_W_Q': _L0_attn_in['W_Q'], 'L0_attn_b_Q': _L0_attn_in['b_Q'], 'L0_attn_W_K': _L0_attn_in['W_K'], 'L0_attn_b_K': _L0_attn_in['b_K'], 'L0_attn_W_V': _L0_attn_in['W_V'], 'L0_attn_b_V': _L0_attn_in['b_V'], 'L0_attn_W_O': _L0_attn_in['W_O'], 'L0_attn_b_O': _L0_attn_in['b_O'], 'L0_xattn_proj_in': _L0_xattn_in['proj_in'], 'L0_xattn_proj_out': _L0_xattn_in['proj_out'], 'L0_ffn_router_w': _L0_ffn_in['router_w'], 'L0_ffn_wg_r': _L0_ffn_in['wg_r'], 'L0_ffn_wu_r': _L0_ffn_in['wu_r'], 'L0_ffn_wd_r': _L0_ffn_in['wd_r'], 'L0_ffn_wg_s': _L0_ffn_in['wg_s'], 'L0_ffn_wu_s': _L0_ffn_in['wu_s'], 'L0_ffn_wd_s': _L0_ffn_in['wd_s'], 'L1_attn_Wqkv': _L1_attn_in['Wqkv'], 'L1_attn_Wproj': _L1_attn_in['Wproj'], 'L1_attn_bproj': _L1_attn_in['bproj'], 'L1_xattn_Wq': _L1_xattn_in['Wq'], 'L1_xattn_bq': _L1_xattn_in['bq'], 'L1_xattn_Wk': _L1_xattn_in['Wk'], 'L1_xattn_bk': _L1_xattn_in['bk'], 'L1_xattn_Wv': _L1_xattn_in['Wv'], 'L1_xattn_bv': _L1_xattn_in['bv'], 'L1_xattn_Wo': _L1_xattn_in['Wo'], 'L1_xattn_bo': _L1_xattn_in['bo'], 'L1_ffn_gate_w': _L1_ffn_in['gate_w'], 'L1_ffn_gate_b': _L1_ffn_in['gate_b'], 'L1_ffn_rms_w': _L1_ffn_in['rms_w'], 'L1_ffn_w1': _L1_ffn_in['w1'], 'L1_ffn_b1': _L1_ffn_in['b1'], 'L1_ffn_w2': _L1_ffn_in['w2'], 'L1_ffn_b2': _L1_ffn_in['b2']}

def reference(x, ctx_512, itok_BxS2xS_0_7, L0_attn_W_Q, L0_attn_b_Q, L0_attn_W_K, L0_attn_b_K, L0_attn_W_V, L0_attn_b_V, L0_attn_W_O, L0_attn_b_O, L0_xattn_proj_in, L0_xattn_proj_out, L0_ffn_router_w, L0_ffn_wg_r, L0_ffn_wu_r, L0_ffn_wd_r, L0_ffn_wg_s, L0_ffn_wu_s, L0_ffn_wd_s, L1_attn_Wqkv, L1_attn_Wproj, L1_attn_bproj, L1_xattn_Wq, L1_xattn_bq, L1_xattn_Wk, L1_xattn_bk, L1_xattn_Wv, L1_xattn_bv, L1_xattn_Wo, L1_xattn_bo, L1_ffn_gate_w, L1_ffn_gate_b, L1_ffn_rms_w, L1_ffn_w1, L1_ffn_b1, L1_ffn_w2, L1_ffn_b2):
    import jax
    import jax.numpy as jnp

    def _L0_attn_ref(x, W_Q, b_Q, W_K, b_K, W_V, b_V, W_O, b_O):
        import jax, jax.numpy as jnp
        import numpy as np
        B, S, D, H, DH = (4, 512, 256, 16, 64)
        INIT_STD = 0.02
        IGNORE = -100000.0
        Q = jnp.einsum('bqd,hde->bqhe', x, W_Q) + b_Q
        K = jnp.einsum('bkd,hde->bkhe', x, W_K) + b_K
        V = jnp.einsum('bkd,hde->bkhe', x, W_V) + b_V
        d_head = Q.shape[-1]
        scores = jnp.einsum('bqhe,bkhe->bhqk', Q, K) / np.sqrt(d_head).astype(np.float32)
        s = scores.shape[-1]
        causal = jnp.triu(jnp.ones((s, s), dtype=bool), k=1)
        scores = jnp.where(causal, jnp.float32(IGNORE), scores)
        A = jax.nn.softmax(scores, axis=-1)
        z = jnp.einsum('bhqk,bkhe->bqhe', A, V)
        attn_out = jnp.einsum('bqhe,hed->bqd', z, W_O) + b_O
        return attn_out

    def _L0_xattn_ref(x, weights, ensembles, proj_in, proj_out):
        import jax, jax.numpy as jnp
        import numpy as np
        E = proj_in.shape[0]
        h = jax.nn.relu(jnp.einsum('edi,bsi->bsed', proj_in, x))
        o = jnp.einsum('eid,bsed->bsei', proj_out, h)
        onehot = jax.nn.one_hot(ensembles, E, dtype=x.dtype)
        gate = jnp.einsum('bks,bkse->bse', weights, onehot)
        return jnp.einsum('bsei,bse->bsi', o, gate)

    def _L0_ffn_ref(x, router_w, wg_r, wu_r, wd_r, wg_s, wu_s, wd_s):
        import jax, jax.numpy as jnp
        import numpy as np
        HIDDEN = 256
        N_ROUTED = 16
        N_SHARED = 2
        TOP_K = 2
        MID_R = HIDDEN // 4
        MID_S = HIDDEN // 2
        orig_shape = x.shape
        flat = x.reshape(-1, orig_shape[-1])
        gs = jnp.einsum('td,ndm->tnm', flat, wg_s)
        us = jnp.einsum('td,ndm->tnm', flat, wu_s)
        out = jnp.einsum('tnm,nmd->td', jax.nn.silu(gs) * us, wd_s)
        logits = (flat @ router_w).astype(jnp.float32)
        probs = jax.nn.softmax(logits, axis=-1)
        weights, indices = jax.lax.top_k(probs, TOP_K)
        weights = weights / (weights.sum(axis=-1, keepdims=True) + 1e-09)
        weights = weights.astype(x.dtype)
        comb = jnp.sum(jax.nn.one_hot(indices, N_ROUTED, dtype=x.dtype) * weights[..., None], axis=1)
        g = jnp.einsum('td,edm->tem', flat, wg_r)
        u = jnp.einsum('td,edm->tem', flat, wu_r)
        h = jax.nn.silu(g) * u
        h = h * comb[:, :, None]
        out = out + jnp.einsum('tem,emd->td', h, wd_r)
        return out.reshape(orig_shape)

    def _L1_attn_ref(x, Wqkv, Wproj, bproj):
        import jax, jax.numpy as jnp
        import numpy as np
        B, N, C, H, W = (2, 512, 256, 16, 8)
        HD = C // H
        SCALE = HD ** (-0.5)

        def band_mask(n, w):
            i = jnp.arange(n)[:, None]
            j = jnp.arange(n)[None, :]
            lo = jnp.where(i <= w, 0, i - w)
            hi = jnp.where(n - i <= w, n - 1, i + w)
            return (j >= lo) & (j <= hi)
        b, n, c = x.shape
        qkv = (x @ Wqkv).reshape(b, n, 3, H, HD)
        qkv = jnp.transpose(qkv, (2, 0, 3, 1, 4))
        q, k, v = (qkv[0], qkv[1], qkv[2])
        attn = jnp.einsum('bhqd,bhkd->bhqk', q, k) * SCALE
        mask = band_mask(n, W)
        attn = jnp.where(mask[None, None], attn, jnp.float32(-1000000000.0))
        attn = jax.nn.softmax(attn, axis=-1)
        out = jnp.einsum('bhqk,bhkd->bhqd', attn, v)
        out = jnp.transpose(out, (0, 2, 1, 3)).reshape(b, n, c)
        return out @ Wproj + bproj

    def _L1_xattn_ref(q, k, v, Wq, bq, Wk, bk, Wv, bv, Wo, bo):
        import jax, jax.numpy as jnp
        import numpy as np
        HEADS = 16
        D_MODEL = 256
        IMG_MODEL = 128
        D_K = D_MODEL // HEADS
        B, LQ, _ = q.shape
        LKV = k.shape[1]
        qh = (q @ Wq + bq).reshape(B, LQ, HEADS, D_K).transpose(0, 2, 1, 3)
        kh = (k @ Wk + bk).reshape(B, LKV, HEADS, D_K).transpose(0, 2, 1, 3)
        vh = (v @ Wv + bv).reshape(B, LKV, HEADS, D_K).transpose(0, 2, 1, 3)
        scale = 1.0 / np.sqrt(D_K)
        scores = jnp.einsum('bhqd,bhkd->bhqk', qh, kh) * scale
        attn = jax.nn.softmax(scores, axis=-1)
        out = jnp.einsum('bhqk,bhkd->bhqd', attn, vh)
        concat = out.transpose(0, 2, 1, 3).reshape(B, LQ, D_MODEL)
        return concat @ Wo + bo

    def _L1_ffn_ref(x, gate_w, gate_b, rms_w, w1, b1, w2, b2):
        import jax, jax.numpy as jnp
        import numpy as np
        TEMPERATURE = 0.5
        CAPACITY_FACTOR = 1.25
        TOP_K = 1
        B, S, D = x.shape
        E = gate_w.shape[0]
        xf = x.reshape(-1, D)
        N = xf.shape[0]
        logits = xf @ gate_w.T + gate_b
        eps = jnp.finfo(logits.dtype).eps
        ms = jnp.mean(logits * logits, axis=-1, keepdims=True)
        logits = logits * jax.lax.rsqrt(ms + eps) * rms_w
        gates = jax.nn.softmax(logits / TEMPERATURE, axis=-1)
        g, idx = jax.lax.top_k(gates, TOP_K)
        g, idx = (g[:, 0], idx[:, 0])
        capacity = min(int(np.ceil(N * TOP_K / E * CAPACITY_FACTOR)), N)
        counts = jnp.zeros((E,), jnp.int32).at[idx].add(1)
        active = (counts > 0) & (capacity >= 1)
        mask = active[idx].astype(gates.dtype)
        masked = g * mask
        norm_g = masked / (masked + 1e-06)
        h = jax.nn.gelu(jnp.einsum('nd,edh->neh', xf, w1) + b1, approximate=False)
        y = jnp.einsum('neh,ehd->ned', h, w2) + b2
        out = (y * norm_g[:, None, None]).sum(axis=1)
        return out.reshape(B, S, D)
    x = _layernorm(x + _L0_attn_ref(x, L0_attn_W_Q, L0_attn_b_Q, L0_attn_W_K, L0_attn_b_K, L0_attn_W_V, L0_attn_b_V, L0_attn_W_O, L0_attn_b_O), axis=-1)
    x = _layernorm(x + _L0_xattn_ref(x, ctx_512, itok_BxS2xS_0_7, L0_xattn_proj_in, L0_xattn_proj_out), axis=-1)
    x = _layernorm(x + _L0_ffn_ref(x, L0_ffn_router_w, L0_ffn_wg_r, L0_ffn_wu_r, L0_ffn_wd_r, L0_ffn_wg_s, L0_ffn_wu_s, L0_ffn_wd_s), axis=-1)
    x = _layernorm(x + _L1_attn_ref(x, L1_attn_Wqkv, L1_attn_Wproj, L1_attn_bproj), axis=-1)
    x = _layernorm(x + _L1_xattn_ref(x, ctx_512, ctx_512, L1_xattn_Wq, L1_xattn_bq, L1_xattn_Wk, L1_xattn_bk, L1_xattn_Wv, L1_xattn_bv, L1_xattn_Wo, L1_xattn_bo), axis=-1)
    x = _layernorm(x + _L1_ffn_ref(x, L1_ffn_gate_w, L1_ffn_gate_b, L1_ffn_rms_w, L1_ffn_w1, L1_ffn_b1, L1_ffn_w2, L1_ffn_b2), axis=-1)
    return x

_drawn_inputs = setup_inputs


def setup_inputs(seed=0):
    import zlib

    import numpy as np

    out = dict(_drawn_inputs(seed))
    spreads = {'L0_attn_b_Q': (0.0, 0.8),
     'L0_attn_b_K': (0.0, 0.8),
     'L0_attn_b_V': (0.0, 0.1),
     'L0_attn_b_O': (0.0, 0.1),
     'L1_attn_bproj': (0.0, 0.1),
     'L1_xattn_bq': (0.0, 0.8),
     'L1_xattn_bk': (0.0, 0.8),
     'L1_xattn_bv': (0.0, 0.1),
     'L1_xattn_bo': (0.0, 0.1),
     'L1_ffn_gate_b': (0.0, 0.8),
     'L1_ffn_rms_w': (1.0, 0.6),
     'L1_ffn_b1': (0.0, 0.1),
     'L1_ffn_b2': (0.0, 0.1)}
    factors = {'L0_attn_W_Q': 8.0,
     'L0_attn_W_K': 8.0,
     'L0_ffn_router_w': 8.0,
     'L0_ffn_wg_r': 8.0,
     'L0_ffn_wu_r': 8.0,
     'L0_ffn_wd_r': 8.0,
     'L0_ffn_wg_s': 4.281,
     'L0_ffn_wu_s': 4.205,
     'L0_ffn_wd_s': 4.193,
     'L1_xattn_Wq': 4.197,
     'L1_xattn_Wk': 4.158,
     'L1_ffn_gate_w': 8.0}
    for name, (base, spread) in spreads.items():
        noise = np.random.default_rng([zlib.crc32(name.encode()), seed]).standard_normal(out[name].shape)
        drawn = base * np.exp(spread * noise) if base else spread * noise
        out[name] = jnp.asarray(drawn.astype(out[name].dtype))
    for name, factor in factors.items():
        out[name] = (out[name] * factor).astype(out[name].dtype)
    return out
```

```python
import concourse.bass as bass
from concourse import mybir

DT = mybir.dt
F32, F32R, BF16, I32 = DT.float32, DT.float32r, DT.bfloat16, DT.int32
ACT = mybir.ActivationFunctionType
ALU = mybir.AluOpType
AX = mybir.AxisListType

P = 128
B, S, D = 16, 128, 256
DC = D // P
GB = 4
NG = B // GB
GT = GB * S
H = 16
QH = 4
NQ = GB * H // QH
E_OUT, E_HID = 8, 512
HC = E_HID // P
R_N, R_MID, SH_HID = 16, 64, 256
FC = (SH_HID + R_N * R_MID) // P
SC = SH_HID // P
LN_EPS = 1e-5
NEG = -float(2 ** 30)
C1 = 1
RAW = 1024


class Region:

    def __init__(self, nc, start, size):
        self.nc, self.start, self.at, self.end = nc, start, start, start + size

    def place(self, name, shape, dt):
        size = 1
        for n in shape[1:]:
            size *= n
        size = (size * (2 if dt == BF16 else 4) + 31) // 32 * 32
        t = self.nc.alloc_sbuf_tensor_at(name, shape, dt, offset=self.at)
        self.at += size
        assert self.at <= self.end, (name, self.at - self.start)
        return t

    def again(self):
        return Region(self.nc, self.start, self.end - self.start)


class Stage:
    pass


class Attn:

    def __init__(self, tag, stage, hd, scale, mask, cross):
        self.tag, self.stage, self.hd, self.scale, self.mask, self.cross = tag, stage, hd, scale, mask, cross
        self.width = H * hd
        self.nch = self.width // P
        self.hpc = P // hd
        self.copies = self.hpc // 2
        self.vh = max(1, self.width // GT)
        self.vn = self.width // self.vh
        self.nz = (self.nch + 3) // 4
        self.zc = self.nch // self.nz
        self.fg = DC + 2 * self.nch + GB * self.vh
        self.qk = DC + 2 * self.nch
        self.fe = GB * (self.nz + 1)
        self.links = 2 * NQ + 2 * GB + (1 if cross else 0)

    def heads(self, q):
        g, half = divmod(q, 2)
        if self.copies == 1:
            return [(8 * g + 2 * i + half, 4 * g + i, half, 0) for i in range(QH)]
        return [(4 * q + i, g, half, i) for i in range(QH)]

    def of_quad(self, t, q):
        g, half = divmod(q, 2)
        if self.copies == 1:
            return t.rearrange("p (g i r e) -> p g r i e", g=2, i=QH, r=2)[:, g, half]
        return t.rearrange("p (g i e) -> p g i e", g=4, i=QH)[:, q]


def split3(nc, out, wh, wl, xh, xl, start, stop, **kw):
    nc.tensor.matmul(out, wh, xh, start=start, stop=False, **kw)
    nc.tensor.matmul(out, wh, xl, start=False, stop=False, **kw)
    return nc.tensor.matmul(out, wl, xh, start=False, stop=stop, **kw)


def program(nc, x_in, ctxT_in, itokT_in, w_a1, w_e1i, w_e1o, w_ffn, w_a4, w_a5, w_e6i, w_e6o,
            cols_in, rows_in, bv_in, b2_in, out):
    sem = nc.alloc_semaphore

    def signals(tag, names):
        return {n: sem(f"{tag}_{n}") for n in names.split()}

    base = (nc.sbuf_base + 31) // 32 * 32
    KB = 1024
    keep = Region(nc, base, 34 * KB)
    r3 = Region(nc, keep.end, 16 * KB)
    r1 = Region(nc, r3.end, 64 * KB)
    r2 = Region(nc, r1.end, nc.sbuf_usable_end - r1.end - 64)

    X = keep.place("X", [P, B, D], F32)
    raw = [keep.place(f"raw{i}", [P, RAW], F32) for i in range(2)]
    ident = keep.place("ident", [P, P], F32)
    identb = keep.place("identb", [P, P], BF16)
    causal = keep.place("causal", [P, QH, S], BF16)
    band = keep.place("band", [P, QH, S], BF16)
    rows = keep.place("rows", [P, 4 * D + 16], F32)
    cols = keep.place("cols", [P, 100], F32)
    gates = keep.place("gates", [P, B, E_OUT], F32)
    head8 = keep.place("head8", [P, 2, 4], F32)
    head = keep.place("head", [P, 4], F32)
    rw_h = keep.place("rw_h", [P, 48], F32R)
    rw_l = keep.place("rw_l", [P, 48], F32R)
    mx = keep.place("mx", [P, 2, QH], F32)
    negm = keep.place("negm", [P, 2, QH], F32)
    rec = keep.place("rec", [P, QH], F32)
    stats = keep.place("stats", [P, B, 6], F32)
    mv = keep.place("mv", [P, B, 2], F32)
    veps = keep.place("veps", [P, B], F32)
    rstd = keep.place("rstd", [P, B], F32)
    mhalf = keep.place("mhalf", [P, B], F32)
    ng = keep.place("ng", [P, B], F32)

    row_bo1, row_bo4 = rows[:, 0:D], rows[:, D:2 * D]
    row_bv5, row_bo5 = rows[:, 2 * D:3 * D], rows[:, 3 * D:4 * D]
    row_gb, row_rms = rows[:, 4 * D:4 * D + 8], rows[:, 4 * D + 8:4 * D + 16]
    col_bq1, col_bk1, col_bq5, col_bk5 = cols[:, 0:8], cols[:, 8:16], cols[:, 16:18], cols[:, 18:20]
    col_b1, col_rw = cols[:, 20:52], cols[:, 52:100]

    ps = nc.alloc_psum_tensor("ps", [P, 8, GT], F32)

    def pair(region, name, shape):
        return region.place(name + "_h", shape, F32R), region.place(name + "_l", shape, F32R)

    wA1 = pair(r1, "wA1", [P, 8 * RAW])
    r1b = r1.again()
    FU = (2 * DC + 2) * FC * P // 8
    wF = pair(r1b, "wF", [P, 8 * FU])
    r1c = r1.again()
    wA5 = pair(r1c, "wA5", [P, 1536])
    slots6 = [pair(r1c, f"w6_{i}", [P, 2 * RAW]) for i in range(2)]
    wA4 = pair(r3, "wA4", [P, 2048])
    r3a = r3.again()
    bv1 = r3a.place("bv1", [P, H * 64], F32)
    ctxg1 = r3a.place("ctxg1", [P, GB, S], F32)
    itokg = r3a.place("itokg", [P, GB, S], I32)
    junk = r3a.place("junk", [P, S], F32)
    r3b = r3.again()
    b2rows = r3b.place("b2rows", [P, E_OUT, D], F32)
    b2sum = r3b.place("b2sum", [P, D], F32)

    consts_pool = sem("consts_pool")
    consts_dve = sem("consts_dve")
    small_loaded = sem("small_loaded")
    x_loaded = sem("x_loaded")
    b2_loaded = sem("b2_loaded")
    split_hi = sem("split_hi")
    raw_loaded = [sem("raw_loaded0"), sem("raw_loaded1")]
    prep_done = sem("prep_done")
    chain = sem("chain")
    waited_sp = sem("waited_sp")
    waited = sem("waited")
    stage_done = sem("stage_done")
    out_stored = sem("out_stored")

    U_A1, U_E0 = 0, 8
    U_PAIR = 10
    U_A4 = U_PAIR + 6 * 4
    U_A5 = U_A4 + 4
    U_E6 = U_A5 + 2
    U_PAIR6 = U_E6 + 2

    def attn_setup(c):
        t = c.tag
        m = r2.again()
        c.Xs = m.place(t + "Xs", [P, GB, D], F32)
        c.XB = m.place(t + "XB", [P, GB, D], F32)
        c.XT = pair(m, t + "XT", [P, DC, GT])
        c.QT = m.place(t + "QT", [P, c.nch, GT], F32)
        c.KT = m.place(t + "KT", [P, c.nch, c.copies, GT], F32)
        c.V = m.place(t + "V", [P, GB, H, c.hd + 1], F32)
        c.Pr = m.place(t + "Pr", [P, 2, QH, S], F32)
        c.PT = m.place(t + "PT", [P, 2, QH, S], F32)
        c.z = m.place(t + "z", [P, 2, c.width], F32)
        c.zT = pair(m, t + "zT", [P, c.nch, S])
        c.r = m.place(t + "r", [P, 2, D], F32)
        if c.cross:
            c.ctxg = m.place(t + "ctxg", [P, GT], F32)
            c.CT = pair(m, t + "CT", [P, GT])
        c.s = signals(t, "xs_loaded ctx_loaded xb_ready xt_hi ct_ready g_full g_evac s_full s_max p_ready pt_full "
                      "pt_ready z_full z_ready e_full e_hi e_evac ln_var rstd_ready x_done gates_done")

    A1 = Attn("a1", 1, 64, 1 / 8.0, causal, False)
    A4 = Attn("a4", 4, 16, 1 / 4.0, band, False)
    A5 = Attn("a5", 5, 16, 1 / 4.0, None, True)
    for c in (A1, A4, A5):
        attn_setup(c)
    def view(w, at, k, n):
        return [t[:, at:at + k * n].rearrange("p (k n) -> p k n", k=k) for t in w]
    A1.wq, A1.wk, A1.wv = (view(wA1, i * 2048, DC, 1024) for i in range(3))
    A1.wo = view(wA1, 3 * 2048, 8, D)
    qkv4 = view(wA4, 0, DC, 768)
    A4.wq, A4.wk, A4.wv = ([t[:, :, i * D:(i + 1) * D] for t in qkv4] for i in range(3))
    A4.wo = view(wA4, 1536, DC, D)
    A5.wq, A5.wk, A5.wv, A5.wo = view(wA5, 0, DC, D), view(wA5, 512, 1, D), view(wA5, 768, 1, D), view(wA5, 1024, DC, D)
    A1.bq, A1.bk, A1.bv, A1.bo = col_bq1, col_bk1, bv1[:, :], row_bo1
    A4.bq, A4.bk, A4.bv, A4.bo = None, None, None, row_bo4
    A5.bq, A5.bk, A5.bv, A5.bo = col_bq5, col_bk5, row_bv5, row_bo5
    A1.weights, A4.weights, A5.weights = U_E0, U_A5, U_E6

    def attn_sync(sp, c):
        with sp.Fori(0, NG) as g:
            sp.wait_ge(c.s["xt_hi"], g * DC + C1)
            sp.sem_inc(waited_sp, 1)
            sp.wait_ge(c.s["xb_ready"], g + C1)
            sp.sem_inc(waited_sp, 1)
            sp.dma_start(c.Xs[:, :, :], X[:, bass.ds(g * GB, GB), :]).then_inc(c.s["xs_loaded"], 16)
            if c.cross:
                sp.wait_ge(c.s["ct_ready"], g + C1)
                sp.sem_inc(waited_sp, 1)
                sp.dma_start(c.ctxg[:, :], ctxT_in[:, bass.ds(g * GT, GT)]).then_inc(c.s["ctx_loaded"], 16)
            if c is A1:
                sp.wait_ge(c.s["gates_done"], g * GB * E_OUT + C1)
                sp.sem_inc(waited_sp, 1)
                sp.dma_start(ctxg1[:, :, :].rearrange("p b s -> p (b s)"),
                             ctxT_in[:, bass.ds(g * GT, GT)]).then_inc(c.s["ctx_loaded"], 16)
                sp.dma_start(itokg[:, :, :].rearrange("p b s -> p (b s)"),
                             itokT_in[:, bass.ds(g * GT, GT)]).then_inc(c.s["ctx_loaded"], 16)

    def attn_pool(pool, c):
        pool.sem_inc(c.s["xb_ready"], C1)
        with pool.Fori(0, NG) as g:
            pool.wait_ge(c.s["xs_loaded"], (g + 1) * 16)
            pool.wait_ge(c.s["x_done"], g * GB + C1)
            nc.gpsimd.tensor_tensor(c.XB[:, :, :], c.Xs[:, :, :],
                                    c.bo.unsqueeze(1).broadcast_to([P, GB, D]), ALU.add).then_inc(c.s["xb_ready"], 1)
            for b in range(GB):
                pool.wait_ge(c.s["ln_var"], g * GB + b + 1)
                nc.gpsimd.tensor_tensor(rstd[:, b:b + 1], veps[:, b:b + 1], mhalf[:, b:b + 1],
                                        ALU.pow).then_inc(c.s["rstd_ready"], 1)

    def attn_tensor(pe, c):
        G0, E0, PTB, ZB = 4, 6, 2, 3

        def g_fill(g, k):
            pe.wait_ge(c.s["g_evac"], g * c.fg + k + 1)
            return ps[:, G0 + k % 2, :]

        def e_fill(g, k):
            pe.wait_ge(c.s["e_evac"], g * c.fe + k + 1)
            return ps[:, E0 + k % 2, :]

        def project(g, k, w, ch, xh, xl, kc):
            bank = g_fill(g, k)
            for i in range(kc):
                last = split3(nc, bank, w[0][:, i, ch * P:(ch + 1) * P], w[1][:, i, ch * P:(ch + 1) * P],
                              xh[i], xl[i], i == 0, i == kc - 1)
            last.then_inc(c.s["g_full"], 1)

        def scores(g, n):
            b, q = divmod(n, H // QH)
            pe.wait_ge(c.s["p_ready"], g * NQ + n + 1)
            if n == 0:
                pe.wait_ge(c.s["g_evac"], g * c.fg + c.qk + 2)
            bank = ps[:, n % 2, :]
            if c.mask is not None:
                nc.tensor.matmul(bank, identb[:, :], c.mask[:, :, :].rearrange("p a b -> p (a b)"),
                                 start=True, stop=False)
            for i, (h, ch, half, j) in enumerate(c.heads(q)):
                rows64 = slice(64 * half, 64 * half + 64)
                last = nc.tensor.matmul(bank[:, i * S:(i + 1) * S], c.QT[rows64, ch, b * S:(b + 1) * S],
                                        c.KT[rows64, ch, j, b * S:(b + 1) * S],
                                        start=c.mask is None, stop=c.mask is None or i == QH - 1)
            last.then_inc(c.s["s_full"], 1)

        def transpose_p(g, n):
            pe.wait_ge(c.s["p_ready"], g * NQ + n + 3)
            pe.wait_ge(c.s["pt_ready"], g * NQ + n + C1)
            for i in range(QH):
                last = nc.tensor.transpose(ps[:, PTB, i * S:(i + 1) * S], c.Pr[:, n % 2, i, :], ident[:, :])
            last.then_inc(c.s["pt_full"], 1)

        def values(g, n):
            b, q = divmod(n, H // QH)
            pe.wait_ge(c.s["pt_ready"], g * NQ + n + 1 + C1)
            pe.wait_ge(c.s["z_ready"], g * NQ + n + C1)
            if n == 0:
                pe.wait_ge(c.s["g_evac"], (g + 1) * c.fg + 2)
            w = c.hd + 1
            for i, (h, _, _, _) in enumerate(c.heads(q)):
                last = nc.tensor.matmul(ps[:, ZB, i * w:(i + 1) * w], c.PT[:, n % 2, i, :],
                                        c.V[:, b, h, :], start=True, stop=True)
            last.then_inc(c.s["z_full"], 1)

        def transpose_z(g, b):
            pe.wait_ge(c.s["z_ready"], g * NQ + (b + 1) * (H // QH) + C1)
            for f in range(c.nz):
                bank = e_fill(g, b * (c.nz + 1) + f)
                for i in range(c.zc):
                    ch = f * c.zc + i
                    last = nc.tensor.transpose(bank[:, i * S:(i + 1) * S], c.z[:, b % 2, ch * P:(ch + 1) * P],
                                               ident[:, :])
                last.then_inc(c.s["e_full"], 1)

        def out_project(g, b):
            k = b * (c.nz + 1) + c.nz
            bank = e_fill(g, k)
            pe.wait_ge(c.s["e_evac"], g * c.fe + k + 2)
            for ch in range(c.nch):
                last = split3(nc, bank[:, 0:D], c.zT[0][:, ch, :], c.zT[1][:, ch, :],
                              c.wo[0][:, ch, :], c.wo[1][:, ch, :], ch == 0, ch == c.nch - 1)
            last.then_inc(c.s["e_full"], 1)

        pe.wait_ge(prep_done, c.weights)
        with pe.Fori(0, NG) as g:
            pe.wait_ge(c.s["xs_loaded"], (g + 1) * 16)
            for ch in range(DC):
                bank = g_fill(g, ch)
                for j in range(GB):
                    last = nc.tensor.transpose(bank[:, j * S:(j + 1) * S], c.Xs[:, j, ch * P:(ch + 1) * P], ident[:, :])
                last.then_inc(c.s["g_full"], 1)
            pe.wait_ge(c.s["g_evac"], g * c.fg + DC + 2)
            xh, xl = [c.XT[0][:, i, :] for i in range(DC)], [c.XT[1][:, i, :] for i in range(DC)]
            if c.cross:
                pe.wait_ge(c.s["ct_ready"], g + 1 + C1)
                kh, kl = [c.CT[0][:, :]], [c.CT[1][:, :]]
            else:
                kh, kl = xh, xl
            for ch in range(c.nch):
                project(g, DC + ch, c.wq, ch, xh, xl, DC)
            for ch in range(c.nch):
                project(g, DC + c.nch + ch, c.wk, ch, kh, kl, len(kh))
            for b in range(GB):
                for v in range(c.vh):
                    bank = g_fill(g, c.qk + b * c.vh + v)
                    for i in range(len(kh)):
                        cut = slice(v * c.vn, (v + 1) * c.vn)
                        last = split3(nc, bank[:, 0:c.vn], kh[i][:, b * S:(b + 1) * S], kl[i][:, b * S:(b + 1) * S],
                                      c.wv[0][:, i, cut], c.wv[1][:, i, cut], i == 0, i == len(kh) - 1)
                    last.then_inc(c.s["g_full"], 1)
            for n in range(NQ + 4):
                if n < NQ:
                    scores(g, n)
                if 1 <= n <= NQ:
                    transpose_p(g, n - 1)
                if 2 <= n <= NQ + 1:
                    values(g, n - 2)
                if n % 4 == 2 and n >= 6:
                    transpose_z(g, (n - 6) // 4)
                if n % 4 == 3 and n >= 7:
                    out_project(g, (n - 7) // 4)

    def attn_scalar(act, c):
        act.sem_inc(c.s["p_ready"], 2)
        act.sem_inc(c.s["xt_hi"], C1)
        with act.Fori(0, NG) as g:
            for ch in range(DC):
                act.wait_ge(c.s["g_full"], g * c.fg + ch + 1)
                nc.scalar.activation(c.XT[0][:, ch, :], ps[:, 4 + ch % 2, :], ACT.Identity).then_inc(c.s["xt_hi"], 1)
            for n in range(NQ + 4):
                if n < NQ:
                    act.wait_ge(c.s["s_max"], g * NQ + n + 1)
                    for i in range(QH):
                        last = nc.scalar.activation(c.Pr[:, n % 2, i, :], ps[:, n % 2, i * S:(i + 1) * S], ACT.Exp,
                                                    bias=negm[:, n % 2, i:i + 1], scale=c.scale)
                    last.then_inc(c.s["p_ready"], 1)
                if n % 4 == 2 and n >= 6:
                    b = (n - 6) // 4
                    for f in range(c.nz):
                        k = b * (c.nz + 1) + f
                        act.wait_ge(c.s["e_full"], g * c.fe + k + 1)
                        nc.scalar.activation(c.zT[0][:, f * c.zc:(f + 1) * c.zc, :].rearrange("p a b -> p (a b)"),
                                             ps[:, 6 + k % 2, 0:c.zc * S], ACT.Identity).then_inc(c.s["e_hi"], 1)

    def attn_vector(v, c, link):
        v.sem_inc(c.s["g_evac"], 2)
        v.sem_inc(c.s["e_evac"], 2)
        for first in (c.s["ct_ready"], c.s["gates_done"], c.s["x_done"], c.s["pt_ready"], c.s["z_ready"]):
            v.sem_inc(first, C1)
        nc.vector.memset(c.V[:, :, :, c.hd:c.hd + 1], 1.0)

        def lo(hi, low, psum, done):
            nc.vector.tensor_tensor(low, psum, hi.bitcast(F32), ALU.subtract).then_inc(done, 1)

        def norm_a(g, b):
            k = b * (c.nz + 1) + c.nz
            v.wait_ge(c.s["e_full"], g * c.fe + k + 1)
            if b == 0:
                v.wait_ge(c.s["xb_ready"], g + 1 + C1)
            nc.vector.tensor_tensor(c.r[:, b % 2, :], ps[:, 6 + k % 2, 0:D], c.XB[:, b, :], ALU.add).then_inc(c.s["e_evac"], 1)
            v.wait_ge(c.s["e_evac"], g * c.fe + k + 3)
            link(nc.vector.bn_stats(stats[:, b, :], c.r[:, b % 2, :]), alone=True)
            link(nc.vector.bn_aggr(mv[:, b, :], stats[:, b, :]))
            nc.vector.tensor_scalar(veps[:, b:b + 1], mv[:, b, 1:2], LN_EPS, None, ALU.add).then_inc(c.s["ln_var"], 1)

        def norm_b(g, b):
            v.wait_ge(c.s["rstd_ready"], g * GB + b + 1)
            nc.vector.tensor_scalar(X[:, g * GB + b, :], c.r[:, b % 2, :], mv[:, b, 0:1], rstd[:, b:b + 1],
                                    ALU.subtract, ALU.mult).then_inc(c.s["x_done"], 1)
            v.wait_ge(c.s["x_done"], g * GB + b + 1 + C1)

        with v.Fori(0, NG) as g:
            link.begin(g, c.links)
            for ch in range(DC):
                v.wait_ge(c.s["xt_hi"], g * DC + ch + 1 + C1)
                lo(c.XT[0][:, ch, :], c.XT[1][:, ch, :], ps[:, 4 + ch % 2, :], c.s["g_evac"])
            if c.cross:
                v.wait_ge(c.s["ctx_loaded"], (g + 1) * 16)
                link(nc.vector.tensor_copy(c.CT[0][:, :], c.ctxg[:, :]))
                nc.vector.tensor_tensor(c.CT[1][:, :], c.ctxg[:, :], c.CT[0][:, :].bitcast(F32),
                                        ALU.subtract).then_inc(c.s["ct_ready"], 1)
            for ch in range(c.nch):
                k = DC + ch
                v.wait_ge(c.s["g_full"], g * c.fg + k + 1)
                if c.bq is None:
                    last = nc.vector.tensor_copy(c.QT[:, ch, :], ps[:, 4 + k % 2, :])
                else:
                    last = nc.vector.tensor_scalar(c.QT[:, ch, :], ps[:, 4 + k % 2, :], c.bq[:, ch:ch + 1], None, ALU.add)
                last.then_inc(c.s["g_evac"], 1)
            for ch in range(c.nch):
                k = DC + c.nch + ch
                v.wait_ge(c.s["g_full"], g * c.fg + k + 1)
                for j in range(c.copies):
                    if c.copies == 1:
                        last = nc.vector.tensor_scalar(c.KT[:, ch, j, :], ps[:, 4 + k % 2, :], c.bk[:, ch:ch + 1], None, ALU.add)
                    elif c.bk is None:
                        last = nc.vector.tensor_scalar(c.KT[:, ch, j, :], ps[:, 4 + k % 2, :], head[:, j:j + 1], None, ALU.mult)
                    else:
                        last = nc.vector.tensor_scalar(c.KT[:, ch, j, :], ps[:, 4 + k % 2, :], c.bk[:, ch:ch + 1],
                                                       head[:, j:j + 1], ALU.add, ALU.mult)
                last.then_inc(c.s["g_evac"], 1)
            hv = c.vn // c.hd
            for b in range(GB):
                for w in range(c.vh):
                    k = c.qk + b * c.vh + w
                    v.wait_ge(c.s["g_full"], g * c.fg + k + 1)
                    dst = c.V[:, b, w * hv:(w + 1) * hv, 0:c.hd]
                    src = ps[:, 4 + k % 2, 0:c.vn].rearrange("p (h e) -> p h e", h=hv)
                    if c.bv is None:
                        last = nc.vector.tensor_copy(dst, src)
                    else:
                        bias = c.bv[:, w * c.vn:(w + 1) * c.vn].rearrange("p (h e) -> p h e", h=hv)
                        last = nc.vector.tensor_tensor(dst, src, bias, ALU.add)
                    last.then_inc(c.s["g_evac"], 1)
            if c is A1:
                v.wait_ge(c.s["ctx_loaded"], (g + 1) * 32)
            for n in range(NQ + 6):
                if n < NQ:
                    v.wait_ge(c.s["s_full"], g * NQ + n + 1)
                    link(nc.vector.reduce_max(mx[:, n % 2, :], ps[:, n % 2, :].rearrange("p (h k) -> p h k", h=QH), AX.X))
                    nc.vector.tensor_scalar(negm[:, n % 2, :], mx[:, n % 2, :], -c.scale, None, ALU.mult).then_inc(c.s["s_max"], 1)
                if n % 4 == 0 and n >= 8:
                    norm_a(g, (n - 8) // 4)
                if n % 4 == 1 and n >= 9:
                    norm_b(g, (n - 9) // 4)
                if 1 <= n <= NQ:
                    m = n - 1
                    v.wait_ge(c.s["pt_full"], g * NQ + m + 1)
                    nc.vector.tensor_copy(c.PT[:, m % 2, :, :].rearrange("p a b -> p (a b)"), ps[:, 2, :]).then_inc(c.s["pt_ready"], 1)
                if 2 <= n <= NQ + 1:
                    m = n - 2
                    b, q = divmod(m, H // QH)
                    w = c.hd + 1
                    zz = ps[:, 3, 0:QH * w].rearrange("p (h e) -> p h e", h=QH)
                    v.wait_ge(c.s["z_full"], g * NQ + m + 1)
                    link(nc.vector.reciprocal(rec[:, :].unsqueeze(2), zz[:, :, c.hd:w]))
                    dst = c.of_quad(c.z[:, b % 2, :], q)
                    nc.vector.tensor_tensor(dst, zz[:, :, 0:c.hd], rec[:, :].unsqueeze(2).broadcast_to([P, QH, c.hd]),
                                            ALU.mult).then_inc(c.s["z_ready"], 1)
                if n % 4 == 2 and n >= 6:
                    b = (n - 6) // 4
                    for f in range(c.nz):
                        k = b * (c.nz + 1) + f
                        v.wait_ge(c.s["e_hi"], g * GB * c.nz + b * c.nz + f + 1)
                        lo(c.zT[0][:, f * c.zc:(f + 1) * c.zc, :].rearrange("p a b -> p (a b)"),
                           c.zT[1][:, f * c.zc:(f + 1) * c.zc, :].rearrange("p a b -> p (a b)"),
                           ps[:, 6 + k % 2, 0:c.zc * S], c.s["e_evac"])
                if c is A1 and n < NQ:
                    b = n // 4
                    for e in range(2 * (n % 4), 2 * (n % 4) + 2):
                        nc.vector.scalar_tensor_tensor(junk[:, :], itokg[:, b, :], float(e), ctxg1[:, b, :], ALU.is_equal,
                                                       ALU.mult, accum_out=gates[:, g * GB + b, e:e + 1]).then_inc(c.s["gates_done"], 1)
                        v.wait_ge(c.s["gates_done"], g * GB * E_OUT + b * E_OUT + e + 1 + C1)
        link.end(NG)

    NU = 2 * NG * HC
    NG_STEPS = 8

    def mix_setup(tag, gelu, win, wout, first, pair0, per):
        c = Stage()
        c.gelu, c.win, c.wout = gelu, win, wout
        c.first, c.pair0, c.per = first, pair0, per
        m = r2.again()
        c.XT = pair(m, tag + "XT", [P, DC, B * S])
        c.hT = pair(m, tag + "hT", [P, HC, GT])
        if gelu:
            c.slots = slots6
            c.h32 = m.place(tag + "h32", [P, 2, GT], F32)
            c.lg = m.place(tag + "lg", [P, B, E_OUT], F32)
            c.ex = m.place(tag + "ex", [P, B, E_OUT], F32)
            c.t1 = m.place(tag + "t1", [P, B], F32)
            c.t2 = m.place(tag + "t2", [P, B], F32)
            c.b1 = m.place(tag + "b1", [P, 2, HC], F32)
        else:
            c.slots = [pair(m, f"{tag}w{i}", [P, 2 * RAW]) for i in range(2)]
        c.steps = 14 + B if gelu else 0
        c.s = signals(tag, "g_full xt_hi g_evac u_full hi_ready lo_ready d_full comb_done ln_var rstd_ready x_done "
                           "logits ex_ready step b1_ready")
        return c

    M2 = mix_setup("m2", False, w_e1i, w_e1o, U_E0, U_PAIR, 6)
    M6 = mix_setup("m6", True, w_e6i, w_e6o, U_E6, U_PAIR6, 4)

    def load_unit(sp, base, k, src, ncols):
        sp.wait_ge(prep_done, base + (k - 1))
        sp.dma_start(raw[k % 2][:, 0:ncols], src).then_inc(raw_loaded[k % 2], 16)

    def split_unit(v, base, k, w, ncols):
        v.wait_ge(raw_loaded[k % 2], (base + (k - k % 2)) * 8 + 16)
        nc.vector.tensor_scalar(w[0], raw[k % 2][:, 0:ncols], 1.0, None, ALU.mult).then_inc(split_hi, 1)
        v.wait_ge(split_hi, base + (k + 1))
        nc.vector.tensor_tensor(w[1], raw[k % 2][:, 0:ncols], w[0].bitcast(F32), ALU.subtract).then_inc(prep_done, 1)

    def cut(w, at, n):
        return [t[:, at:at + n] for t in w]

    def mix_sync(sp, c):
        with sp.Fori(0, E_OUT // 2) as i:
            base = i * c.per + c.pair0
            odd, even = i * 2 + 1, (i * 2 + 2) % E_OUT
            load_unit(sp, base, 0, c.win[bass.ds(odd, 1)].rearrange("a p n -> (a p) n"), RAW)
            load_unit(sp, base, 1, c.wout[bass.ds(odd, 1)].rearrange("a p n -> (a p) n"), RAW)
            if not c.gelu:
                for k in range(2):
                    load_unit(sp, base, 2 + k, w_ffn[:, bass.ds(i * (2 * FU) + k * FU, FU)], FU)
            load_unit(sp, base, c.per - 2, c.win[bass.ds(even, 1)].rearrange("a p n -> (a p) n"), RAW)
            load_unit(sp, base, c.per - 1, c.wout[bass.ds(even, 1)].rearrange("a p n -> (a p) n"), RAW)

    def mix_tensor(pe, c):
        for k in range(NG * DC):
            g, ch = divmod(k, DC)
            pe.wait_ge(c.s["g_evac"], k + 1)
            for j in range(GB):
                last = nc.tensor.transpose(ps[:, 4 + k % 2, j * S:(j + 1) * S], X[:, g * GB + j, ch * P:(ch + 1) * P], ident[:, :])
            last.then_inc(c.s["g_full"], 1)
        pe.wait_ge(c.s["g_evac"], NG * DC + 2)
        if c.gelu:
            rh, rl = (t[:, 32:48].rearrange("p (k n) -> p k n", k=DC) for t in (rw_h, rw_l))
            for t in range(B):
                for i in range(DC):
                    last = split3(nc, ps[:, 4, t * 8:(t + 1) * 8], c.XT[0][:, i, t * S:(t + 1) * S],
                                  c.XT[1][:, i, t * S:(t + 1) * S], rh[:, i, :], rl[:, i, :], i == 0, i == DC - 1)
            last.then_inc(c.s["logits"], 1)

        def up(i, u):
            e2, r = divmod(u, NG * HC)
            g, ch = divmod(r, HC)
            if r == 0:
                pe.wait_ge(prep_done, i * c.per + (c.pair0 + 2 * e2))
            wh, wl = (t[:, 0:RAW].rearrange("p (k n) -> p k n", k=DC) for t in c.slots[e2])
            pe.wait_ge(c.s["lo_ready"], i * NU + u + 1)
            for k in range(DC):
                last = split3(nc, ps[:, u % 2, :], wh[:, k, ch * P:(ch + 1) * P], wl[:, k, ch * P:(ch + 1) * P],
                              c.XT[0][:, k, g * GT:(g + 1) * GT], c.XT[1][:, k, g * GT:(g + 1) * GT], k == 0, k == DC - 1)
            last.then_inc(c.s["u_full"], 1)

        def down(i, u):
            e2 = u // (NG * HC)
            q, ch = divmod(u, HC)
            pe.wait_ge(c.s["lo_ready"], i * NU + u + 3)
            if ch == 0:
                pe.wait_ge(c.s["comb_done"], i * (2 * B) + GB * (q + 1))
            wh, wl = (t[:, RAW:2 * RAW].rearrange("p (k n) -> p k n", k=HC) for t in c.slots[e2])
            for j in range(GB):
                acc = ps[:, (2, 6)[q % 2] + j // 2, (j % 2) * D:(j % 2 + 1) * D]
                last = split3(nc, acc, c.hT[0][:, ch, j * S:(j + 1) * S], c.hT[1][:, ch, j * S:(j + 1) * S],
                              wh[:, ch, :], wl[:, ch, :], ch == 0 and j % 2 == 0, ch == HC - 1 and j % 2 == 1,
                              skip_group_check=True)
            if ch == HC - 1:
                last.then_inc(c.s["d_full"], 1)

        with pe.Fori(0, E_OUT // 2) as i:
            for u in range(NU + 2):
                if u < NU:
                    up(i, u)
                if u >= 2:
                    down(i, u - 2)

    def mix_scalar(act, c):
        for k in range(NG * DC):
            g, ch = divmod(k, DC)
            act.wait_ge(c.s["g_full"], k + 1)
            nc.scalar.activation(c.XT[0][:, ch, g * GT:(g + 1) * GT], ps[:, 4 + k % 2, :], ACT.Identity).then_inc(c.s["xt_hi"], 1)
        if c.gelu:
            act.wait_ge(c.s["step"], NG_STEPS)
            nc.scalar.activation(c.ex[:, :, :], c.lg[:, :, :], ACT.Exp, scale=2.0).then_inc(c.s["ex_ready"], 1)
        with act.Fori(0, E_OUT // 2) as i:
            if c.gelu:
                act.wait_ge(c.s["b1_ready"], i + 1)
            for u in range(NU):
                e2, ch = u // (NG * HC), u % HC
                act.wait_ge(c.s["u_full"], i * NU + u + 1)
                if c.gelu:
                    bias = c.b1[:, e2, ch:ch + 1]
                    nc.scalar.activation(c.h32[:, u % 2, :], ps[:, u % 2, :], ACT.Gelu, bias=bias)
                    nc.scalar.activation(c.hT[0][:, ch, :], ps[:, u % 2, :], ACT.Gelu, bias=bias).then_inc(c.s["hi_ready"], 1)
                else:
                    nc.scalar.activation(c.hT[0][:, ch, :], ps[:, u % 2, :], ACT.Relu).then_inc(c.s["hi_ready"], 1)

    def mix_pool(pool, c):
        if c.gelu:
            pool.wait_ge(c.s["step"], 4)
            nc.gpsimd.tensor_tensor(c.t2[:, :], c.t1[:, :], mhalf[:, :], ALU.pow).then_inc(c.s["rstd_ready"], 1)
        pool.wait_ge(c.s["ln_var"], 1)
        nc.gpsimd.tensor_tensor(rstd[:, :], veps[:, :], mhalf[:, :], ALU.pow).then_inc(c.s["rstd_ready"], 1)

    def gate_scale(v, c):
        n = [0]

        def step(ins):
            n[0] += 1
            ins.then_inc(c.s["step"], 1)
            v.wait_ge(c.s["step"], n[0])

        def over(t):
            return t[:, :].unsqueeze(2).broadcast_to([P, B, E_OUT])

        def across(row):
            return row.unsqueeze(1).broadcast_to([P, B, row.shape[1]])
        v.wait_ge(c.s["logits"], 1)
        step(nc.vector.tensor_tensor(c.lg[:, :, :], ps[:, 4, 0:B * E_OUT].rearrange("p (b e) -> p b e", b=B), across(row_gb), ALU.add))
        step(nc.vector.tensor_tensor(c.ex[:, :, :], c.lg[:, :, :], c.lg[:, :, :], ALU.mult))
        step(nc.vector.reduce_sum(c.t1[:, :], c.ex[:, :, :], AX.X))
        step(nc.vector.tensor_scalar(c.t1[:, :], c.t1[:, :], 1.0 / E_OUT, 2.0 ** -23, ALU.mult, ALU.add))
        v.wait_ge(c.s["rstd_ready"], 1)
        step(nc.vector.tensor_tensor(c.lg[:, :, :], c.lg[:, :, :], over(c.t2), ALU.mult))
        step(nc.vector.tensor_tensor(c.lg[:, :, :], c.lg[:, :, :], across(row_rms), ALU.mult))
        step(nc.vector.reduce_max(c.t1[:, :], c.lg[:, :, :], AX.X))
        step(nc.vector.tensor_tensor(c.lg[:, :, :], c.lg[:, :, :], over(c.t1), ALU.subtract))
        assert n[0] == NG_STEPS
        v.wait_ge(c.s["ex_ready"], 1)
        step(nc.vector.reduce_sum(c.t1[:, :], c.ex[:, :, :], AX.X))
        step(nc.vector.reciprocal(c.t2[:, :], c.t1[:, :]))
        step(nc.vector.tensor_scalar(c.t1[:, :], c.t2[:, :], 1e-6, None, ALU.add))
        step(nc.vector.reciprocal(c.t1[:, :], c.t1[:, :]))
        step(nc.vector.tensor_tensor(ng[:, :], c.t1[:, :], c.t2[:, :], ALU.mult))
        v.wait_ge(b2_loaded, 16)
        step(nc.vector.reduce_sum(b2sum[:, :], b2rows[:, :, :].rearrange("p e d -> p d e"), AX.X))
        for t in range(B):
            n[0] += 1
            nc.vector.scalar_tensor_tensor(X[:, t, :], b2sum[:, :], ng[:, t:t + 1], X[:, t, :], ALU.mult, ALU.add).then_inc(c.s["step"], 1)
        assert n[0] == c.steps
        v.wait_ge(c.s["step"], n[0])

    def mix_vector(v, c):
        v.sem_inc(c.s["g_evac"], 2)
        v.sem_inc(c.s["lo_ready"], 2)
        v.sem_inc(c.s["comb_done"], 2 * GB)
        for k in range(NG * DC):
            g, ch = divmod(k, DC)
            tok = slice(g * GT, (g + 1) * GT)
            v.wait_ge(c.s["xt_hi"], k + 1)
            nc.vector.tensor_tensor(c.XT[1][:, ch, tok], ps[:, 4 + k % 2, :], c.XT[0][:, ch, tok].bitcast(F32),
                                    ALU.subtract).then_inc(c.s["g_evac"], 1)
        if c.gelu:
            gate_scale(v, c)
        else:
            for k in range(2):
                split_unit(v, c.first, k, cut(c.slots[0], k * RAW, RAW), RAW)

        def combine(i, q):
            e2, g = divmod(q, NG)
            v.wait_ge(c.s["d_full"], i * (2 * NG) + q + 1)
            for j in range(GB):
                t = g * GB + j
                gate = ng[:, t:t + 1] if c.gelu else gates[:, t, bass.ds(i * 2 + e2, 1)]
                acc = ps[:, (2, 6)[q % 2] + j // 2, (j % 2) * D:(j % 2 + 1) * D]
                nc.vector.scalar_tensor_tensor(X[:, t, :], acc, gate, X[:, t, :], ALU.mult, ALU.add).then_inc(c.s["comb_done"], 1)

        with v.Fori(0, E_OUT // 2) as i:
            base = i * c.per + c.pair0
            if c.gelu:
                nc.vector.tensor_scalar(c.b1[:, :, :].rearrange("p a b -> p (a b)"), col_b1[:, bass.ds(i * (2 * HC), 2 * HC)],
                                        1.0, None, ALU.mult).then_inc(c.s["b1_ready"], 1)
            for u in range(NU):
                ch = u % HC
                v.wait_ge(c.s["hi_ready"], i * NU + u + 1)
                if c.gelu:
                    last = nc.vector.tensor_tensor(c.hT[1][:, ch, :], c.h32[:, u % 2, :], c.hT[0][:, ch, :].bitcast(F32), ALU.subtract)
                else:
                    last = nc.vector.scalar_tensor_tensor(c.hT[1][:, ch, :], ps[:, u % 2, :], 0.0,
                                                          c.hT[0][:, ch, :].bitcast(F32), ALU.max, ALU.subtract)
                last.then_inc(c.s["lo_ready"], 1)
                if u >= HC + 2 and u % HC == 2:
                    combine(i, u // HC - 1)
                if u in (3, 5):
                    k = (u - 3) // 2
                    split_unit(v, base, k, cut(c.slots[1], k * RAW, RAW), RAW)
                if u in (8, 12) and not c.gelu:
                    k = (u - 8) // 4
                    split_unit(v, base, 2 + k, [t[:, bass.ds(i * (2 * FU) + k * FU, FU)] for t in wF], FU)
                if u in (20, 24):
                    k = (u - 20) // 4
                    split_unit(v, base, c.per - 2 + k, cut(c.slots[0], k * RAW, RAW), RAW)
            combine(i, 2 * NG - 1)
        v.wait_ge(c.s["comb_done"], E_OUT * B + 2 * GB)
        for t in range(B):
            nc.vector.bn_stats(stats[:, t, :], X[:, t, :]).then_inc(c.s["step"], 1)
        v.wait_ge(c.s["step"], c.steps + B)
        for t in range(B):
            nc.vector.bn_aggr(mv[:, t, :], stats[:, t, :]).then_inc(c.s["step"], 1)
        v.wait_ge(c.s["step"], c.steps + 2 * B)
        nc.vector.tensor_scalar(veps[:, :].unsqueeze(2), mv[:, :, 1:2], LN_EPS, None, ALU.add).then_inc(c.s["ln_var"], 1)
        v.wait_ge(c.s["rstd_ready"], 2 if c.gelu else 1)
        for t in range(B):
            nc.vector.tensor_scalar(X[:, t, :], X[:, t, :], mv[:, t, 0:1], rstd[:, t:t + 1],
                                    ALU.subtract, ALU.mult).then_inc(c.s["x_done"], 1)
        v.wait_ge(c.s["x_done"], B)

    F3 = Stage()
    m = r2.again()
    F3.Xs = m.place("f3Xs", [P, GB, D], F32)
    F3.XT = pair(m, "f3XT", [P, DC, GT])
    F3.gs = m.place("f3gs", [P, 2, GT], F32)
    F3.tt = m.place("f3tt", [P, 2, GT], F32)
    F3.h32 = m.place("f3h32", [P, 2, GT], F32)
    F3.hT = pair(m, "f3hT", [P, 3, GT])
    F3.r = m.place("f3r", [P, GB, D], F32)
    F3.sel32 = m.place("f3sel32", [R_N, FC - SC, P], F32)
    F3.sel = m.place("f3sel", [R_N, FC - SC, P], F32R)
    F3.combT = pair(m, "f3combT", [R_N, GT])
    F3.lg = m.place("f3lg", [P, GB, R_N], F32)
    F3.pr = m.place("f3pr", [P, GB, R_N + 6], F32)
    F3.mr = m.place("f3mr", [P, GB, R_N + 6], F32)
    F3.comb = m.place("f3comb", [P, GB, R_N], F32)
    F3.top = m.place("f3top", [P, GB, 8], F32)
    F3.t1 = m.place("f3t1", [P, GB], F32)
    F3.t2 = m.place("f3t2", [P, GB], F32)
    F3.s = signals("f3", "xs_loaded xt_hi g_full g_evac soft_exp comb_ready gu_full sg_ready t_done hi_ready h_ready "
                         "d_full r_done ln_var rstd_ready x_done sel_pool sel_ready")
    FG = DC + 2 + FC - SC
    F_LINKS = 18 + 2 * GB

    def ffn_sync(sp):
        s = F3.s
        with sp.Fori(0, NG) as g:
            sp.wait_ge(s["xt_hi"], g * DC + C1)
            sp.dma_start(F3.Xs[:, :, :], X[:, bass.ds(g * GB, GB), :]).then_inc(s["xs_loaded"], 16)

    def ffn_pool(pool):
        s = F3.s
        nc.gpsimd.memset(F3.sel32[:, :, :], 0.0).then_inc(s["sel_pool"], 1)
        pool.wait_ge(s["sel_pool"], 1)
        sel = F3.sel32[:, :, :].rearrange("e c (a m) -> e c a m", a=2)
        nc.gpsimd.affine_select(out=sel, in_=sel, compare_op=ALU.not_equal, fill=1.0, base=0,
                                pattern=[[-2, FC - SC], [-1, 2], [0, R_MID]], channel_multiplier=1).then_inc(s["sel_pool"], 1)
        with pool.Fori(0, NG) as g:
            pool.wait_ge(s["ln_var"], g + 1)
            nc.gpsimd.tensor_tensor(rstd[:, 0:GB], veps[:, 0:GB], mhalf[:, 0:GB], ALU.pow).then_inc(s["rstd_ready"], 1)

    def ffn_tensor(pe):
        s = F3.s
        wgu = [t[:, 0:2 * DC * FC * P].rearrange("p (k n) -> p k n", k=DC) for t in wF]
        wd = [t[:, 2 * DC * FC * P:].rearrange("p (k n) -> p k n", k=FC) for t in wF]
        rh, rl = (t[:, 0:32].rearrange("p (k n) -> p k n", k=DC) for t in (rw_h, rw_l))

        def g_fill(g, k):
            pe.wait_ge(s["g_evac"], g * FG + k + 1)
            return ps[:, 4 + k % 2, :]

        def up(g, c):
            pe.wait_ge(s["sg_ready"], g * FC + c + 1)
            pe.wait_ge(s["t_done"], g * FC + c + 1)
            for part in range(2):
                at = (part * FC + c) * P
                for k in range(DC):
                    last = split3(nc, ps[:, 2 * part + c % 2, :], wgu[0][:, k, at:at + P], wgu[1][:, k, at:at + P],
                                  F3.XT[0][:, k, :], F3.XT[1][:, k, :], k == 0, k == DC - 1)
            last.then_inc(s["gu_full"], 1)

        def spread(g, c):
            bank = g_fill(g, DC + 2 + c - SC)
            if c == SC:
                pe.wait_ge(s["g_evac"], g * FG + DC + 4)
            nc.tensor.matmul(bank, F3.sel[:, c - SC, :], F3.combT[0][:, :], start=True, stop=False)
            nc.tensor.matmul(bank, F3.sel[:, c - SC, :], F3.combT[1][:, :], start=False, stop=True).then_inc(s["g_full"], 1)

        def down(g, c):
            pe.wait_ge(s["h_ready"], g * FC + c + 1 + C1)
            if c == 0:
                pe.wait_ge(s["r_done"], g * GB + C1)
            for j in range(GB):
                acc = ps[:, 6 + j // 2, (j % 2) * D:(j % 2 + 1) * D]
                last = split3(nc, acc, F3.hT[0][:, c % 3, j * S:(j + 1) * S], F3.hT[1][:, c % 3, j * S:(j + 1) * S],
                              wd[0][:, c, :], wd[1][:, c, :], c == 0 and j % 2 == 0, c == FC - 1 and j % 2 == 1,
                              skip_group_check=True)
            if c == FC - 1:
                last.then_inc(s["d_full"], 1)

        pe.wait_ge(s["sel_ready"], 1)
        with pe.Fori(0, NG) as g:
            pe.wait_ge(s["xs_loaded"], (g + 1) * 16)
            for ch in range(DC):
                bank = g_fill(g, ch)
                for j in range(GB):
                    last = nc.tensor.transpose(bank[:, j * S:(j + 1) * S], F3.Xs[:, j, ch * P:(ch + 1) * P], ident[:, :])
                last.then_inc(s["g_full"], 1)
            bank = g_fill(g, DC)
            pe.wait_ge(s["g_evac"], g * FG + DC + 2)
            for j in range(GB):
                for i in range(DC):
                    last = split3(nc, bank[:, j * R_N:(j + 1) * R_N], F3.XT[0][:, i, j * S:(j + 1) * S],
                                  F3.XT[1][:, i, j * S:(j + 1) * S], rh[:, i, :], rl[:, i, :], i == 0, i == DC - 1)
            last.then_inc(s["g_full"], 1)
            for c in range(FC + 2):
                if c < FC:
                    up(g, c)
                if c == SC - 1:
                    bank = g_fill(g, DC + 1)
                    pe.wait_ge(s["comb_ready"], g + 1)
                    for j in range(GB):
                        last = nc.tensor.transpose(bank[0:R_N, j * S:(j + 1) * S], F3.comb[:, j, :], ident[:, :])
                    last.then_inc(s["g_full"], 1)
                if SC <= c < FC:
                    spread(g, c)
                if c >= 2:
                    down(g, c - 2)

    def ffn_scalar(act):
        s = F3.s
        act.sem_inc(s["sg_ready"], 2)
        act.sem_inc(s["xt_hi"], C1)
        with act.Fori(0, NG) as g:
            for ch in range(DC):
                act.wait_ge(s["g_full"], g * FG + ch + 1)
                nc.scalar.activation(F3.XT[0][:, ch, :], ps[:, 4 + ch % 2, :], ACT.Identity).then_inc(s["xt_hi"], 1)
            act.wait_ge(s["g_evac"], g * FG + DC + 3)
            nc.scalar.activation(F3.pr[:, :, 0:R_N], F3.lg[:, :, :], ACT.Exp).then_inc(s["soft_exp"], 1)
            for c in range(FC + 1):
                if c < FC:
                    act.wait_ge(s["gu_full"], g * FC + c + 1)
                    nc.scalar.activation(F3.gs[:, c % 2, :], ps[:, c % 2, :], ACT.Silu).then_inc(s["sg_ready"], 1)
                if c >= 1:
                    w = c - 1
                    if w < SC:
                        act.wait_ge(s["t_done"], g * FC + w + 3)
                    else:
                        act.wait_ge(s["g_evac"], g * FG + DC + 2 + w - SC + 3)
                    nc.scalar.activation(F3.hT[0][:, w % 3, :], F3.h32[:, w % 2, :], ACT.Identity).then_inc(s["hi_ready"], 1)

    def ffn_vector(v, link):
        s = F3.s
        v.sem_inc(s["g_evac"], 2)
        v.sem_inc(s["t_done"], 2)
        v.sem_inc(s["r_done"], C1)
        v.sem_inc(s["h_ready"], C1)
        v.wait_ge(s["sel_pool"], 2)
        nc.vector.tensor_copy(F3.sel[:, :, :], F3.sel32[:, :, :]).then_inc(s["sel_ready"], 1)
        nc.vector.memset(F3.pr[:, :, R_N:], -1.0).then_inc(s["sel_ready"], 1)
        v.wait_ge(s["sel_ready"], 2)
        for k in range(4):
            n, at = (768, k * 768) if k < 2 else (256, 1536 + (k - 2) * 256)
            split_unit(v, U_A4, k, cut(wA4, at, n), n)

        def over(t, n):
            return t.unsqueeze(2).broadcast_to([P, GB, n])

        with v.Fori(0, NG) as g:
            link.begin(g, F_LINKS)
            for ch in range(DC):
                v.wait_ge(s["xt_hi"], g * DC + ch + 1 + C1)
                nc.vector.tensor_tensor(F3.XT[1][:, ch, :], ps[:, 4 + ch % 2, :], F3.XT[0][:, ch, :].bitcast(F32),
                                        ALU.subtract).then_inc(s["g_evac"], 1)
            v.wait_ge(s["g_full"], g * FG + DC + 1)
            lgp = ps[:, 4, 0:GB * R_N].rearrange("p (b e) -> p b e", b=GB)
            link(nc.vector.reduce_max(F3.t1[:, :], lgp, AX.X))
            nc.vector.tensor_tensor(F3.lg[:, :, :], lgp, over(F3.t1[:, :], R_N), ALU.subtract).then_inc(s["g_evac"], 1)
            v.wait_ge(s["soft_exp"], g + 1)
            probs = F3.pr[:, :, 0:R_N]
            link(nc.vector.reduce_sum(F3.t1[:, :], probs, AX.X))
            link(nc.vector.reciprocal(F3.t2[:, :], F3.t1[:, :]))
            link(nc.vector.tensor_tensor(probs, probs, over(F3.t2[:, :], R_N), ALU.mult), alone=True)
            for j in range(GB):
                (link if j == GB - 1 else link.note)(nc.vector.max(F3.top[:, j, :], F3.pr[:, j, 0:R_N]))
            link(nc.vector.tensor_tensor(F3.t1[:, :].unsqueeze(2), F3.top[:, :, 0:1], F3.top[:, :, 1:2], ALU.add))
            link(nc.vector.tensor_scalar(F3.t1[:, :], F3.t1[:, :], 1e-9, None, ALU.add))
            link(nc.vector.reciprocal(F3.t2[:, :], F3.t1[:, :]))
            link(nc.vector.memset(F3.top[:, :, 2:8], -1.0), alone=True)
            for j in range(GB):
                (link if j == GB - 1 else link.note)(
                    nc.vector.match_replace(F3.mr[:, j, :], F3.top[:, j, :], F3.pr[:, j, :], -2.0))
            link(nc.vector.scalar_tensor_tensor(F3.comb[:, :, :], F3.mr[:, :, 0:R_N], -2.0, probs, ALU.is_equal, ALU.mult))
            nc.vector.tensor_tensor(F3.comb[:, :, :], F3.comb[:, :, :], over(F3.t2[:, :], R_N), ALU.mult).then_inc(s["comb_ready"], 1)
            for c in range(FC + 1):
                if c < FC:
                    v.wait_ge(s["sg_ready"], g * FC + c + 3)
                    v.wait_ge(s["h_ready"], g * FC + max(c - 1, 0) + C1)
                    dst = F3.h32 if c < SC else F3.tt
                    nc.vector.tensor_tensor(dst[:, c % 2, :], F3.gs[:, c % 2, :], ps[:, 2 + c % 2, :], ALU.mult).then_inc(s["t_done"], 1)
                    if c >= SC:
                        k = DC + 2 + c - SC
                        v.wait_ge(s["g_full"], g * FG + k + 1)
                        v.wait_ge(s["t_done"], g * FC + c + 3)
                        nc.vector.tensor_tensor(F3.h32[:, c % 2, :], F3.tt[:, c % 2, :], ps[:, 4 + k % 2, :], ALU.mult).then_inc(s["g_evac"], 1)
                        v.wait_ge(s["g_evac"], g * FG + k + 3)
                if c == SC - 1:
                    v.wait_ge(s["g_full"], g * FG + DC + 2)
                    src = ps[0:R_N, 4 + (DC + 1) % 2, :]
                    link(nc.vector.tensor_copy(F3.combT[0][:, :], src))
                    nc.vector.tensor_tensor(F3.combT[1][:, :], src, F3.combT[0][:, :].bitcast(F32), ALU.subtract).then_inc(s["g_evac"], 1)
                if c >= 1:
                    w = c - 1
                    v.wait_ge(s["hi_ready"], g * FC + w + 1)
                    nc.vector.tensor_tensor(F3.hT[1][:, w % 3, :], F3.h32[:, w % 2, :], F3.hT[0][:, w % 3, :].bitcast(F32),
                                            ALU.subtract).then_inc(s["h_ready"], 1)
            v.wait_ge(s["d_full"], g + 1)
            for j in range(GB):
                acc = ps[:, 6 + j // 2, (j % 2) * D:(j % 2 + 1) * D]
                nc.vector.tensor_tensor(F3.r[:, j, :], acc, X[:, g * GB + j, :], ALU.add).then_inc(s["r_done"], 1)
            v.wait_ge(s["r_done"], (g + 1) * GB + C1)
            for j in range(GB):
                bn = nc.vector.bn_stats(stats[:, j, :], F3.r[:, j, :])
                if j == GB - 1:
                    link(bn, alone=True)
                else:
                    link.note(bn)
            for j in range(GB):
                (link if j == GB - 1 else link.note)(nc.vector.bn_aggr(mv[:, j, :], stats[:, j, :]))
            nc.vector.tensor_scalar(veps[:, 0:GB].unsqueeze(2), mv[:, 0:GB, 1:2], LN_EPS, None, ALU.add).then_inc(s["ln_var"], 1)
            v.wait_ge(s["rstd_ready"], g + 1)
            for j in range(GB):
                nc.vector.tensor_scalar(X[:, g * GB + j, :], F3.r[:, j, :], mv[:, j, 0:1], rstd[:, j:j + 1],
                                        ALU.subtract, ALU.mult).then_inc(s["x_done"], 1)
            v.wait_ge(s["x_done"], (g + 1) * GB)
        link.end(NG)

    class Link:

        def __init__(self, v):
            self.v, self.total = v, 0

        def begin(self, g, per):
            self.g, self.per, self.k = g, per, 0

        def note(self, ins):
            self.k += 1
            ins.then_inc(chain, 1)

        def __call__(self, ins, alone=False):
            self.note(ins)
            self.v.wait_ge(chain, self.g * self.per + (self.total + self.k))
            if alone:
                self.v.sem_inc(waited, 1)

        def end(self, times):
            assert self.k == self.per, (self.k, self.per)
            self.total += self.per * times

    block = nc.Block()
    with block as block:
        @block.sync
        def _(sp):
            sp.dma_start(X[:, :, :], x_in.rearrange("b s d -> s b d")).then_inc(x_loaded, 16)
            sp.dma_start(rows[:, :], rows_in.partition_broadcast(P)).then_inc(small_loaded, 16)
            sp.dma_start(cols[:, :], cols_in).then_inc(small_loaded, 16)
            sp.dma_start(bv1[:, :], bv_in.partition_broadcast(P)).then_inc(small_loaded, 16)
            for k in range(8):
                if k >= 2:
                    sp.wait_ge(prep_done, k - 1)
                sp.dma_start(raw[k % 2][:, :], w_a1[:, k * RAW:(k + 1) * RAW]).then_inc(raw_loaded[k % 2], 16)
            sp.wait_ge(x_loaded, 16)
            attn_sync(sp, A1)
            load_unit(sp, U_E0, 0, w_e1i[0], RAW)
            load_unit(sp, U_E0, 1, w_e1o[0], RAW)
            mix_sync(sp, M2)
            for k in range(4):
                n, at = (768, k * 768) if k < 2 else (256, 1536 + (k - 2) * 256)
                load_unit(sp, U_A4, k, w_a4[:, at:at + n], n)
            sp.wait_ge(stage_done, 2)
            ffn_sync(sp)
            for k in range(2):
                load_unit(sp, U_A5, k, w_a5[:, k * 768:(k + 1) * 768], 768)
            sp.wait_ge(stage_done, 3)
            attn_sync(sp, A4)
            load_unit(sp, U_E6, 0, w_e6i[0], RAW)
            load_unit(sp, U_E6, 1, w_e6o[0], RAW)
            sp.wait_ge(stage_done, 4)
            sp.dma_start(b2rows[:, :, :].rearrange("p e d -> p (e d)"), b2_in.partition_broadcast(P)).then_inc(b2_loaded, 16)
            attn_sync(sp, A5)
            mix_sync(sp, M6)
            sp.wait_ge(stage_done, 6)
            sp.dma_start(out.rearrange("b s d -> s b d"), X[:, :, :]).then_inc(out_stored, 16)
            sp.wait_ge(out_stored, 16)

        @block.gpsimd
        def _(pool):
            nc.gpsimd.memset(ident[:, :], 0.0).then_inc(consts_pool, 1)
            nc.gpsimd.memset(causal[:, :, :], 0.0).then_inc(consts_pool, 1)
            nc.gpsimd.memset(band[:, :, :], 0.0).then_inc(consts_pool, 1)
            nc.gpsimd.memset(head8[:, :, :], 1.0).then_inc(consts_pool, 1)
            pool.wait_ge(consts_pool, 4)
            nc.gpsimd.affine_select(out=ident[:, :], in_=ident[:, :], compare_op=ALU.not_equal, fill=1.0, base=0,
                                    pattern=[[-1, P]], channel_multiplier=1).then_inc(consts_pool, 1)
            nc.gpsimd.affine_select(out=causal[:, :, :], in_=causal[:, :, :], compare_op=ALU.is_ge, fill=NEG, base=0,
                                    pattern=[[0, QH], [-1, S]], channel_multiplier=1).then_inc(consts_pool, 1)
            nc.gpsimd.affine_select(out=band[:, :, :], in_=band[:, :, :], compare_op=ALU.is_ge, fill=NEG, base=8,
                                    pattern=[[0, QH], [-1, S]], channel_multiplier=1).then_inc(consts_pool, 1)
            nc.gpsimd.affine_select(out=head8[:, :, :], in_=head8[:, :, :], compare_op=ALU.is_ge, fill=0.0, base=0,
                                    pattern=[[-64, 2], [-16, 4]], channel_multiplier=1).then_inc(consts_pool, 1)
            pool.wait_ge(consts_pool, 8)
            nc.gpsimd.affine_select(out=band[:, :, :], in_=band[:, :, :], compare_op=ALU.is_ge, fill=NEG, base=8,
                                    pattern=[[0, QH], [1, S]], channel_multiplier=-1).then_inc(consts_pool, 1)
            nc.gpsimd.affine_select(out=head8[:, :, :], in_=head8[:, :, :], compare_op=ALU.is_ge, fill=0.0, base=15,
                                    pattern=[[64, 2], [16, 4]], channel_multiplier=-1).then_inc(consts_pool, 1)
            pool.wait_ge(consts_dve, 5)
            pool.wait_ge(small_loaded, 48)
            attn_pool(pool, A1)
            mix_pool(pool, M2)
            pool.wait_ge(stage_done, 2)
            ffn_pool(pool)
            pool.wait_ge(stage_done, 3)
            attn_pool(pool, A4)
            pool.wait_ge(stage_done, 4)
            attn_pool(pool, A5)
            mix_pool(pool, M6)

        @block.tensor
        def _(pe):
            pe.wait_ge(consts_pool, 10)
            pe.wait_ge(consts_dve, 5)
            attn_tensor(pe, A1)
            pe.wait_ge(stage_done, 1)
            mix_tensor(pe, M2)
            pe.wait_ge(stage_done, 2)
            ffn_tensor(pe)
            pe.wait_ge(stage_done, 3)
            attn_tensor(pe, A4)
            pe.wait_ge(stage_done, 4)
            attn_tensor(pe, A5)
            pe.wait_ge(stage_done, 5)
            mix_tensor(pe, M6)

        @block.scalar
        def _(act):
            attn_scalar(act, A1)
            mix_scalar(act, M2)
            ffn_scalar(act)
            attn_scalar(act, A4)
            attn_scalar(act, A5)
            mix_scalar(act, M6)

        @block.vector
        def _(v):
            link = Link(v)
            nc.vector.memset(mhalf[:, :], -0.5).then_inc(consts_dve, 1)
            v.wait_ge(consts_pool, 10)
            nc.vector.tensor_copy(identb[:, :], ident[:, :]).then_inc(consts_dve, 1)
            nc.vector.tensor_tensor(head[:, :], head8[:, 0, :], head8[:, 1, :], ALU.add).then_inc(consts_dve, 1)
            v.wait_ge(small_loaded, 48)
            nc.vector.tensor_copy(rw_h[:, :], col_rw).then_inc(consts_dve, 1)
            v.wait_ge(consts_dve, 4)
            nc.vector.tensor_tensor(rw_l[:, :], col_rw, rw_h[:, :].bitcast(F32), ALU.subtract).then_inc(consts_dve, 1)
            for k in range(8):
                split_unit(v, U_A1, k, cut(wA1, k * RAW, RAW), RAW)
            attn_vector(v, A1, link)
            v.sem_inc(stage_done, 1)
            mix_vector(v, M2)
            v.sem_inc(stage_done, 1)
            ffn_vector(v, link)
            v.sem_inc(stage_done, 1)
            for k in range(2):
                split_unit(v, U_A5, k, cut(wA5, k * 768, 768), 768)
            attn_vector(v, A4, link)
            v.sem_inc(stage_done, 1)
            for k in range(2):
                split_unit(v, U_E6, k, cut(slots6[0], k * RAW, RAW), RAW)
            attn_vector(v, A5, link)
            v.sem_inc(stage_done, 1)
            mix_vector(v, M6)
            v.sem_inc(stage_done, 1)


def kernel(**inputs):
    import numpy as np
    import concourse.bacc as bacc
    from concourse import mybir as mb
    from concourse.bass_utils import run_bass_kernel_spmd as run

    a = {k: np.asarray(v) for k, v in inputs.items()}

    def chunked(w):
        k, n = w.shape
        return w.reshape(k // 128, 128, n).transpose(1, 0, 2).reshape(128, -1)

    def heads(w):
        return w.transpose(1, 0, 2).reshape(256, -1)

    def experts(w):
        return np.stack([chunked(e) for e in w])

    x = {}
    x["x"] = a["x"]
    x["ctxT"] = a["ctx_512"].transpose(2, 0, 1).reshape(128, -1)
    x["itokT"] = a["itok_BxS2xS_0_7"].transpose(2, 0, 1).reshape(128, -1)
    x["w_a1"] = np.concatenate([chunked(heads(a[f"L0_attn_W_{n}"])) for n in "QKV"]
                               + [chunked(a["L0_attn_W_O"].reshape(-1, 256))], 1)
    x["w_e1i"] = experts(a["L0_xattn_proj_in"].transpose(0, 2, 1))
    x["w_e1o"] = experts(a["L0_xattn_proj_out"].transpose(0, 2, 1))
    gu = [heads(a[f"L0_ffn_w{n}"]) for n in ("g_s", "g_r", "u_s", "u_r")]
    down = [a[f"L0_ffn_wd_{n}"].reshape(-1, 256) for n in "sr"]
    x["w_ffn"] = np.concatenate([chunked(np.concatenate(gu, 1)), chunked(np.concatenate(down, 0))], 1)
    x["w_a4"] = np.concatenate([chunked(a["L1_attn_Wqkv"]), chunked(a["L1_attn_Wproj"])], 1)
    x["w_a5"] = np.concatenate([chunked(a[f"L1_xattn_W{n}"]) for n in "qkvo"], 1)
    x["w_e6i"] = experts(a["L1_ffn_w1"])
    x["w_e6o"] = experts(a["L1_ffn_w2"])
    x["cols"] = np.concatenate([a["L0_attn_b_Q"].reshape(-1, 128).T, a["L0_attn_b_K"].reshape(-1, 128).T,
                                a["L1_xattn_bq"].reshape(-1, 128).T, a["L1_xattn_bk"].reshape(-1, 128).T,
                                a["L1_ffn_b1"].reshape(-1, 128).T, chunked(a["L0_ffn_router_w"]),
                                chunked(a["L1_ffn_gate_w"].T)], 1)
    x["rows"] = np.concatenate([a["L0_attn_b_O"], a["L1_attn_bproj"], a["L1_xattn_bv"], a["L1_xattn_bo"],
                                a["L1_ffn_gate_b"], a["L1_ffn_rms_w"]])
    x["bv"] = a["L0_attn_b_V"].reshape(-1)
    x["b2"] = a["L1_ffn_b2"].reshape(-1)
    nc = bacc.Bacc("TRN2", target_bir_lowering=False, num_devices=1)
    arrays, args = {}, []
    for name, v in x.items():
        v = np.ascontiguousarray(v)
        arrays[f"in_{name}"] = v
        args.append(nc.dram_tensor(f"in_{name}", v.shape, mb.dt.from_np(v.dtype), kind="ExternalInput").ap())
    args.append(nc.dram_tensor("out_0", (16, 128, 256), mb.dt.float32, kind="ExternalOutput").ap())
    program(nc, *args)
    r = run(nc, [arrays], core_ids=[0])
    return r.results[0]["out_0"]
```

```python
import concourse.bass as bass
from concourse import mybir

DT = mybir.dt
F32, F32R, BF16, I32 = DT.float32, DT.float32r, DT.bfloat16, DT.int32
ACT = mybir.ActivationFunctionType
ALU = mybir.AluOpType
AX = mybir.AxisListType

P = 128
B, S, D = 16, 128, 256
DC = D // P
GB = 4
NG = B // GB
GT = GB * S
H = 16
QH = 4
NQ = GB * H // QH
E_OUT, E_HID = 8, 512
HC = E_HID // P
R_N, R_MID, SH_HID = 16, 64, 256
FC = (SH_HID + R_N * R_MID) // P
SC = SH_HID // P
LN_EPS = 1e-5
NEG = -float(2 ** 30)
C1 = 1
RAW = 1024


class Region:

    def __init__(self, nc, start, size):
        self.nc, self.start, self.at, self.end = nc, start, start, start + size

    def place(self, name, shape, dt):
        size = 1
        for n in shape[1:]:
            size *= n
        size = (size * (2 if dt == BF16 else 4) + 31) // 32 * 32
        t = self.nc.alloc_sbuf_tensor_at(name, shape, dt, offset=self.at)
        self.at += size
        assert self.at <= self.end, (name, self.at - self.start)
        return t

    def again(self):
        return Region(self.nc, self.start, self.end - self.start)


class Stage:
    pass


class Attn:

    def __init__(self, tag, stage, hd, scale, mask, cross):
        self.tag, self.stage, self.hd, self.scale, self.mask, self.cross = tag, stage, hd, scale, mask, cross
        self.width = H * hd
        self.nch = self.width // P
        self.hpc = P // hd
        self.copies = self.hpc // 2
        self.vh = max(1, self.width // GT)
        self.vn = self.width // self.vh
        self.narrow = self.copies > 1
        self.nz = 0 if self.narrow else 2
        self.slots = 4 if self.narrow else 2
        self.zc = self.nch // max(1, self.nz)
        self.fg = DC + 2 * self.nch + GB * self.vh
        self.qk = DC + 2 * self.nch
        self.fe = GB * (self.nz + 1)
        self.links = (0 if self.narrow else NQ) + 2 * GB

    def q_at(self, ch):
        return 2 * ch + 1 if self.narrow else ch

    def k_at(self, ch):
        return 2 * ch if self.narrow else self.nch + ch

    def bank(self, n):
        if not self.narrow:
            return n % 2
        return (0, 1, 6)[n % 3 if n < NQ - 1 else 1]

    def before(self, n):
        if not self.narrow:
            return n - 2
        return {0: -4, 1: -1, 2: -2, NQ - 1: NQ - 3}.get(n, n - 3)

    def heads(self, q):
        g, half = divmod(q, 2)
        if self.copies == 1:
            return [(8 * g + 2 * i + half, 4 * g + i, half, 0) for i in range(QH)]
        return [(4 * q + i, g, half, i) for i in range(QH)]

    def of_quad(self, t, q):
        g, half = divmod(q, 2)
        if self.copies == 1:
            return t.rearrange("p (g i r e) -> p g r i e", g=2, i=QH, r=2)[:, g, half]
        return t.rearrange("p (g i e) -> p g i e", g=4, i=QH)[:, q]


def split3(nc, out, wh, wl, xh, xl, start, stop, **kw):
    nc.tensor.matmul(out, wh, xh, start=start, stop=False, **kw)
    nc.tensor.matmul(out, wh, xl, start=False, stop=False, **kw)
    return nc.tensor.matmul(out, wl, xh, start=False, stop=stop, **kw)


def program(nc, x_in, ctxT_in, itokT_in, w_a1, w_e1i, w_e1o, w_ffn, w_a4, w_a5, w_e6i, w_e6o,
            cols_in, rows_in, bv_in, b2_in, out):
    sem = nc.alloc_semaphore

    def signals(tag, names):
        return {n: sem(f"{tag}_{n}") for n in names.split()}

    base = (nc.sbuf_base + 31) // 32 * 32
    KB = 1024
    keep = Region(nc, base, 34 * KB)
    r3 = Region(nc, keep.end, 16 * KB)
    r1 = Region(nc, r3.end, 64 * KB)
    r2 = Region(nc, r1.end, nc.sbuf_usable_end - r1.end - 64)

    X = keep.place("X", [P, B, D], F32)
    raw = [keep.place(f"raw{i}", [P, RAW], F32) for i in range(2)]
    ident = keep.place("ident", [P, P], F32)
    identb = keep.place("identb", [P, P], BF16)
    causal = keep.place("causal", [P, QH, S], BF16)
    band = keep.place("band", [P, QH, S], BF16)
    rows = keep.place("rows", [P, 4 * D + 16], F32)
    cols = keep.place("cols", [P, 100], F32)
    gates = keep.place("gates", [P, B, E_OUT], F32)
    head8 = keep.place("head8", [P, 2, 4], F32)
    head = keep.place("head", [P, 4], F32)
    rw_h = keep.place("rw_h", [P, 48], F32R)
    rw_l = keep.place("rw_l", [P, 48], F32R)
    negm = keep.place("negm", [P, 4, QH], F32)
    rec = keep.place("rec", [P, QH], F32)
    stats = keep.place("stats", [P, B, 6], F32)
    mv = keep.place("mv", [P, B, 2], F32)
    veps = keep.place("veps", [P, B], F32)
    rstd = keep.place("rstd", [P, B], F32)
    mhalf = keep.place("mhalf", [P, B], F32)
    ng = keep.place("ng", [P, B], F32)

    row_bo1, row_bo4 = rows[:, 0:D], rows[:, D:2 * D]
    row_bv5, row_bo5 = rows[:, 2 * D:3 * D], rows[:, 3 * D:4 * D]
    row_gb, row_rms = rows[:, 4 * D:4 * D + 8], rows[:, 4 * D + 8:4 * D + 16]
    col_bq1, col_bk1, col_bq5, col_bk5 = cols[:, 0:8], cols[:, 8:16], cols[:, 16:18], cols[:, 18:20]
    col_b1, col_rw = cols[:, 20:52], cols[:, 52:100]

    ps = nc.alloc_psum_tensor("ps", [P, 8, GT], F32)

    def pair(region, name, shape):
        return region.place(name + "_h", shape, F32R), region.place(name + "_l", shape, F32R)

    wA1 = pair(r1, "wA1", [P, 8 * RAW])
    r1b = r1.again()
    FU = (2 * DC + 2) * FC * P // 8
    wF = pair(r1b, "wF", [P, 8 * FU])
    r1c = r1.again()
    wA5 = pair(r1c, "wA5", [P, 1536])
    slots6 = [pair(r1c, f"w6_{i}", [P, 2 * RAW]) for i in range(2)]
    KT45 = r1c.place("KT45", [P, 2, 4, GT], F32)
    V_ROW = 144 * QH
    V45_at = (r2.end - GB * (H // QH) * V_ROW * 4) // 32 * 32
    V45 = Region(nc, V45_at, r2.end - V45_at).place("V45", [P, GB, H // QH, V_ROW], F32)
    wA4 = pair(r3, "wA4", [P, 2048])
    r3a = r3.again()
    bv1 = r3a.place("bv1", [P, H * 64], F32)
    ctxg1 = r3a.place("ctxg1", [P, GB, S], F32)
    itokg = r3a.place("itokg", [P, GB, S], I32)
    junk = r3a.place("junk", [P, S], F32)
    r3b = r3.again()
    b2rows = r3b.place("b2rows", [P, E_OUT, D], F32)
    b2sum = r3b.place("b2sum", [P, D], F32)

    consts_pool = sem("consts_pool")
    consts_dve = sem("consts_dve")
    small_loaded = sem("small_loaded")
    x_loaded = sem("x_loaded")
    b2_loaded = sem("b2_loaded")
    v45_made = sem("v45_made")
    split_hi = sem("split_hi")
    raw_loaded = [sem("raw_loaded0"), sem("raw_loaded1")]
    prep_done = sem("prep_done")
    chain = sem("chain")
    waited_sp = sem("waited_sp")
    waited_pool = sem("waited_pool")
    waited = sem("waited")
    stage_done = sem("stage_done")
    out_stored = sem("out_stored")

    U_A1, U_E0 = 0, 8
    U_PAIR = 10
    U_A4 = U_PAIR + 6 * 4
    U_A5 = U_A4 + 4
    U_E6 = U_A5 + 2
    U_PAIR6 = U_E6 + 2

    def attn_setup(c):
        t = c.tag
        m = r2.again()
        if c.narrow:
            m.end = V45_at
        c.Xs = m.place(t + "Xs", [P, GB, D], F32)
        c.XB = m.place(t + "XB", [P, GB, D], F32)
        c.XT = pair(m, t + "XT", [P, DC, GT])
        c.QT = m.place(t + "QT", [P, c.nch, GT], F32)
        if c.narrow:
            c.KT, c.V = KT45, V45
            c.z = m.place(t + "z", [P, 2, c.nch, S], F32)
            c.rz = m.place(t + "rz", [P, 2, S], F32)
            c.sums = m.place(t + "sums", [P, 2, 2 * QH], F32)
            c.rec = m.place(t + "rec", [P, 2, 2 * QH], F32)
            c.recx = m.place(t + "recx", [P, 2, 2 * QH, c.hd], F32)
        else:
            c.KT = m.place(t + "KT", [P, c.nch, c.copies, GT], F32)
            c.V = m.place(t + "V", [P, GB, H, c.hd + 1], F32)
            c.z = m.place(t + "z", [P, 2, c.width], F32)
        c.Pr = m.place(t + "Pr", [P, c.slots, QH, S], F32)
        c.PT = m.place(t + "PT", [P, 2, QH, S], F32)
        c.zT = pair(m, t + "zT", [P, c.nch, S])
        c.r = m.place(t + "r", [P, 2, D], F32)
        if c.cross:
            c.ctxg = m.place(t + "ctxg", [P, GT], F32)
            c.CT = pair(m, t + "CT", [P, GT])
            c.bkm = m.place(t + "bkm", [P, c.nch, 4], F32)
        c.s = signals(t, "xs_loaded ctx_loaded xb_ready xt_hi ct_ready g_full g_evac s_full s_max p_ready pt_full "
                      "pt_ready z_full z_ready e_full e_hi e_evac ln_var rstd_ready x_done gates_done k_most bk_ready zt_ready rz_ready rec_ready recx_ready r_full ct_hi")

    A1 = Attn("a1", 1, 64, 1 / 8.0, causal, False)
    A4 = Attn("a4", 4, 16, 1 / 4.0, band, False)
    A5 = Attn("a5", 5, 16, 1 / 4.0, None, True)
    for c in (A1, A4, A5):
        attn_setup(c)
    def view(w, at, k, n):
        return [t[:, at:at + k * n].rearrange("p (k n) -> p k n", k=k) for t in w]
    A1.wq, A1.wk, A1.wv = (view(wA1, i * 2048, DC, 1024) for i in range(3))
    A1.wo = view(wA1, 3 * 2048, 8, D)
    qkv4 = view(wA4, 0, DC, 768)
    A4.wq, A4.wk, A4.wv = ([t[:, :, i * D:(i + 1) * D] for t in qkv4] for i in range(3))
    A4.wo = view(wA4, 1536, DC, D)
    A5.wq, A5.wk, A5.wv, A5.wo = view(wA5, 0, DC, D), view(wA5, 512, 1, D), view(wA5, 768, 1, D), view(wA5, 1024, DC, D)
    A1.bq, A1.bk, A1.bv, A1.bo = col_bq1, col_bk1, bv1[:, :], row_bo1
    A4.bq, A4.bk, A4.bv, A4.bo = None, None, None, row_bo4
    A5.bq, A5.bk, A5.bv, A5.bo = col_bq5, col_bk5, row_bv5, row_bo5
    A1.needs = {("q", 0): U_A1 + 2, ("k", 0): U_A1 + 4, ("v", 0): U_A1 + 6, ("o", 0): U_A1 + 8}
    A4.needs, A5.needs = {("k", 0): U_A5}, {("k", 0): U_E6}

    def attn_order(c, first, last):
        fills = [(kind, ch, 0) for kind in "qk" for ch in range(c.nch)]
        if c.narrow:
            fills = [(kind, ch, 0) for ch in range(c.nch) for kind in "kq"]
        fills += [("v", f, 0) for f in range(GB * c.vh)]

        def wide(n):
            steps = [("s", n), ("e", n)]
            if n >= 8 and n % 4 < 2:
                steps += [[("na", n // 4 - 2), ("ns", n // 4 - 2)], [("nb", n // 4 - 2)]][n % 4]
            steps += [("t", n - 1), ("pv", n - 2)]
            if n >= 6 and n % 4 >= 2:
                steps.append((("zt", "o")[n % 4 - 2], (n - 6) // 4))
            return steps

        def narrow(n):
            phase, b = n % 4, n // 4 - 2
            steps = [("z", (n - 5) // 2)] if n % 2 else []
            steps += [("zl", b)] if phase == 0 else []
            steps += [("s", n), ("t", n - 2)]
            steps += [("r", (n - 4) // 2)] if n % 2 == 0 else []
            steps += [("e", n), ("pv", n - 3)]
            steps += [[("o", b)], [("na", b), ("ns", b)], [("nb", b)], [("zh", b + 1)]][phase]
            of = {"s": NQ, "e": NQ, "t": NQ, "pv": NQ, "z": NQ // 2, "r": NQ // 2}
            return [(kind, i) for kind, i in steps if 0 <= i < of.get(kind, GB)]

        if c.narrow:
            tail = [narrow(n) for n in range(NQ, NQ + 7)]
        else:
            tail = [[("t", NQ - 1)], [("na", 2), ("ns", 2), ("pv", NQ - 2)], [("nb", 2), ("pv", NQ - 1)], [("zt", 3)], [],
                    [("o", 3)], [("na", 3), ("ns", 3)], [("nb", 3)]]
        order = []
        s0 = len(fills) - 1 - 2 * c.vh
        for f in range(max(len(fills), len(tail))):
            if not last:
                order.append(fills[f])
            if not first and f < len(tail):
                order += [(kind, i, -1) for kind, i in tail[f]]
            if not last and f in (s0, s0 + c.vh):
                n = (f - s0) // c.vh
                order += [("s", n, 0), ("e", n, 0)]
        if last:
            return order
        if not c.narrow:
            order.append(("t", 0, 0))
        for n in range(2, NQ):
            order += [(kind, i, 0) for kind, i in (narrow if c.narrow else wide)(n)]
            if n in (8, 9):
                order.append(("x", n - 8, 0))
        return order

    def attn_groups(eng, c, steps):
        steps(0, attn_order(c, True, False))
        with eng.Fori(1, NG) as g:
            steps(g, attn_order(c, False, False))
        steps(NG, attn_order(c, False, True))

    def attn_load_ctx(sp, g, to, done):
        sp.dma_start(to, ctxT_in[:, bass.ds(g * GT, GT)]).then_inc(done, 16)

    def attn_first_loads(sp, c):
        sp.dma_start(c.Xs[:, :, :], X[:, 0:GB, :]).then_inc(c.s["xs_loaded"], 16)
        if c.cross:
            attn_load_ctx(sp, 0, c.ctxg[:, :], c.s["ctx_loaded"])

    def attn_sync(sp, c):
        def settle():
            sp.sem_inc(waited_sp, 1)

        with sp.Fori(0, NG) as g:
            if c is A1:
                sp.wait_ge(c.s["gates_done"], g * GB * E_OUT + C1)
                settle()
                attn_load_ctx(sp, g, ctxg1[:, :, :].rearrange("p b s -> p (b s)"), c.s["ctx_loaded"])
                sp.dma_start(itokg[:, :, :].rearrange("p b s -> p (b s)"),
                             itokT_in[:, bass.ds(g * GT, GT)]).then_inc(c.s["ctx_loaded"], 16)
            nxt = (g + 1) % NG
            if c.cross:
                sp.wait_ge(c.s["ct_ready"], g + 1 + C1)
                settle()
                attn_load_ctx(sp, nxt, c.ctxg[:, :], c.s["ctx_loaded"])
            sp.wait_ge(c.s["xt_hi"], g * DC + DC + C1)
            settle()
            sp.wait_ge(c.s["xb_ready"], g + 1 + C1)
            settle()
            sp.dma_start(c.Xs[:, :, :], X[:, bass.ds(nxt * GB, GB), :]).then_inc(c.s["xs_loaded"], 16)

    def attn_pool(pool, c, extra):
        pool.sem_inc(c.s["xb_ready"], C1)

        def context(n):
            pool.wait_ge(c.s["ctx_loaded"], n * 16)
            pool.sem_inc(waited_pool, 1)
            nc.gpsimd.tensor_copy(c.CT[0][:, :], c.ctxg[:, :]).then_inc(c.s["ct_hi"], 1)
            pool.wait_ge(c.s["ct_hi"], n)
            nc.gpsimd.tensor_tensor(c.CT[1][:, :], c.ctxg[:, :], c.CT[0][:, :].bitcast(F32),
                                    ALU.subtract).then_inc(c.s["ct_ready"], 1)

        def steps(g, order):
            for kind, b, back in order:
                if kind == "ns":
                    pool.wait_ge(c.s["ln_var"], (g + back) * GB + b + 1)
                    nc.gpsimd.tensor_tensor(rstd[:, b:b + 1], veps[:, b:b + 1], mhalf[:, b:b + 1],
                                            ALU.pow).then_inc(c.s["rstd_ready"], 1)
                if kind == "t" and c.narrow and b % 2:
                    pair = b // 2
                    pool.wait_ge(c.s["rec_ready"], (g + back) * (NQ // 2) + (pair + 1))
                    pool.sem_inc(waited_pool, 1)
                    nc.gpsimd.tensor_copy(c.recx[:, pair % 2, :, :], c.rec[:, pair % 2, :].unsqueeze(2).broadcast_to(
                        [P, 2 * QH, c.hd])).then_inc(c.s["recx_ready"], 1)
                if kind == "s" and b == 2:
                    pool.wait_ge(c.s["xs_loaded"], g * 16 + 16)
                    pool.wait_ge(c.s["x_done"], g * GB + C1)
                    nc.gpsimd.tensor_tensor(c.XB[:, :, :], c.Xs[:, :, :],
                                            c.bo.unsqueeze(1).broadcast_to([P, GB, D]), ALU.add).then_inc(c.s["xb_ready"], 1)
                    if c.cross:
                        pool.wait_ge(c.s["g_evac"], emptied(c, g, c.fg - DC))
                        context(g + 2)
                if type(g) is int and g == 0 and (kind, b) in extra:
                    extra[kind, b]()
        if c.cross:
            context(1)
        attn_groups(pool, c, steps)

    PTB, ZB, G0, E0, E1 = 2, 3, 4, 6, 7

    def filled(c, g, k):
        return g * c.fg + (DC + k + 1)

    def emptied(c, g, k):
        return g * c.fg + (DC + k + 2)

    def attn_tensor(pe, c):
        def g_fill(g, k):
            pe.wait_ge(c.s["g_evac"], emptied(c, g, k - 1))
            return ps[:, G0 + k % 2, :]

        def e_fill(g, k):
            pe.wait_ge(c.s["e_evac"], g * c.fe + (k + 1))
            return ps[:, E0 + k % 2, :]

        def transposed_x(g, n, k, chunks=range(DC)):
            pe.wait_ge(c.s["xs_loaded"], n)
            for ch in chunks:
                bank = g_fill(g, k + ch)
                for j in range(GB):
                    last = nc.tensor.transpose(bank[:, j * S:(j + 1) * S], c.Xs[:, j, ch * P:(ch + 1) * P], ident[:, :])
                last.then_inc(c.s["g_full"], 1)

        xh, xl = [c.XT[0][:, i, :] for i in range(DC)], [c.XT[1][:, i, :] for i in range(DC)]
        kh, kl = ([c.CT[0][:, :]], [c.CT[1][:, :]]) if c.cross else (xh, xl)

        def project(g, k, w, ch, xh, xl):
            bank = g_fill(g, k)
            for i in range(len(xh)):
                last = split3(nc, bank, w[0][:, i, ch * P:(ch + 1) * P], w[1][:, i, ch * P:(ch + 1) * P],
                              xh[i], xl[i], i == 0, i == len(xh) - 1)
            last.then_inc(c.s["g_full"], 1)

        def project_v(g, f):
            b, w = divmod(f, c.vh)
            bank = g_fill(g, 2 * c.nch + f)
            cols_v = slice(w * c.vn, (w + 1) * c.vn)
            for i in range(len(kh)):
                last = split3(nc, bank[:, 0:c.vn], kh[i][:, b * S:(b + 1) * S], kl[i][:, b * S:(b + 1) * S],
                              c.wv[0][:, i, cols_v], c.wv[1][:, i, cols_v], i == 0, i == len(kh) - 1)
            last.then_inc(c.s["g_full"], 1)

        def scores(g, n):
            b, q = divmod(n, H // QH)
            if type(g) is not int or n >= c.slots or c.before(n) >= 0:
                pe.wait_ge(c.s["p_ready"], g * NQ + (c.before(n) + 3))
            if n == 0:
                pe.wait_ge(c.s["g_evac"], emptied(c, g, 2 * c.nch))
            bank = ps[:, c.bank(n), :]
            if c.mask is not None:
                nc.tensor.matmul(bank, identb[:, :], c.mask[:, :, :].rearrange("p a b -> p (a b)"),
                                 start=True, stop=False)
            for i, (h, ch, half, j) in enumerate(c.heads(q)):
                rows64 = slice(64 * half, 64 * half + 64)
                last = nc.tensor.matmul(bank[:, i * S:(i + 1) * S], c.QT[rows64, ch, b * S:(b + 1) * S],
                                        c.KT[rows64, ch, j, b * S:(b + 1) * S],
                                        start=c.mask is None, stop=c.mask is None or i == QH - 1)
            last.then_inc(c.s["s_full"], 1)

        def transpose_p(g, n):
            pe.wait_ge(c.s["p_ready"], g * NQ + (n + 3))
            pe.wait_ge(c.s["pt_ready"], g * NQ + (n + C1))
            for i in range(QH):
                last = nc.tensor.transpose(ps[:, PTB, i * S:(i + 1) * S], c.Pr[:, n % c.slots, i, :], ident[:, :])
            last.then_inc(c.s["pt_full"], 1)

        def values(g, n):
            b, q = divmod(n, H // QH)
            pe.wait_ge(c.s["pt_ready"], g * NQ + (n + 1 + C1))
            if not c.narrow:
                pe.wait_ge(c.s["z_ready"], g * NQ + (n + C1))
            elif n % 2 == 0:
                pe.wait_ge(c.s["z_ready"], g * (NQ // 2) + (n // 2 + C1))
            if q == 0:
                pe.wait_ge(c.s["g_evac"], emptied(c, g, 2 * c.nch + (b + 1) * c.vh))
            if c.narrow:
                for i in range(QH):
                    last = nc.tensor.matmul(ps[:, ZB, 0:S], c.V[:, b, q, i * P:(i + 1) * P], c.PT[:, n % 2, i, :],
                                            start=n % 2 == 0 and i == 0, stop=n % 2 == 1 and i == QH - 1)
                if n % 2:
                    last.then_inc(c.s["z_full"], 1)
                return
            w = c.hd + 1
            for i, (h, _, _, _) in enumerate(c.heads(q)):
                last = nc.tensor.matmul(ps[:, ZB, i * w:(i + 1) * w], c.PT[:, n % 2, i, :],
                                        c.V[:, b, h, :], start=True, stop=True)
            last.then_inc(c.s["z_full"], 1)

        def transpose_r(g, p):
            pe.wait_ge(c.s["recx_ready"], g * (NQ // 2) + (p + 1))
            pe.wait_ge(c.s["rz_ready"], g * (NQ // 2) + (p + C1))
            pe.wait_ge(c.s["e_evac"], g * GB + (max(0, (p - 1) // 2) + 2))
            nc.tensor.transpose(ps[:, E1, 0:S], c.recx[:, p % 2, :, :].rearrange("p h e -> p (h e)"),
                                ident[:, :]).then_inc(c.s["r_full"], 1)

        def transpose_z(g, b):
            pe.wait_ge(c.s["z_ready"], g * NQ + ((b + 1) * (H // QH) + C1))
            for f in range(c.nz):
                bank = e_fill(g, b * (c.nz + 1) + f)
                for i in range(c.zc):
                    ch = f * c.zc + i
                    last = nc.tensor.transpose(bank[:, i * S:(i + 1) * S], c.z[:, b % 2, ch * P:(ch + 1) * P],
                                               ident[:, :])
                last.then_inc(c.s["e_full"], 1)

        def out_project(g, b):
            k = b * (c.nz + 1) + c.nz
            if c.narrow:
                bank = ps[:, E1, :]
                pe.wait_ge(c.s["rz_ready"], g * (NQ // 2) + (min(NQ // 2, 2 * b + 3) + C1))
                pe.wait_ge(c.s["e_evac"], g * GB + (b + 2))
                pe.wait_ge(c.s["zt_ready"], g * GB + (b + 1 + C1))
            else:
                bank = e_fill(g, k)
                pe.wait_ge(c.s["e_evac"], g * c.fe + (k + 2))
            for ch in range(c.nch):
                last = split3(nc, bank[:, 0:D], c.zT[0][:, ch, :], c.zT[1][:, ch, :],
                              c.wo[0][:, ch, :], c.wo[1][:, ch, :], ch == 0, ch == c.nch - 1)
            last.then_inc(c.s["e_full"], 1)

        def steps(g, order):
            for kind, i, back in order:
                if type(g) is int and g == 0 and (kind, i) in c.needs:
                    pe.wait_ge(prep_done, c.needs[kind, i])
                if kind == "q":
                    if i == 0:
                        pe.wait_ge(c.s["g_evac"], emptied(c, g, 0))
                    project(g, c.q_at(i), c.wq, i, xh, xl)
                elif kind == "k":
                    if i == 0 and c.cross:
                        pe.wait_ge(c.s["ct_ready"], g + 1 + C1)
                    elif i == 0 and c.narrow:
                        pe.wait_ge(c.s["g_evac"], emptied(c, g, 0))
                    project(g, c.k_at(i), c.wk, i, kh, kl)
                elif kind == "v":
                    project_v(g, i)
                elif kind == "s":
                    scores(g, i)
                elif kind == "t":
                    transpose_p(g + back, i)
                elif kind == "pv":
                    values(g + back, i)
                elif kind == "r":
                    transpose_r(g + back, i)
                elif kind == "zt":
                    transpose_z(g + back, i)
                elif kind == "o":
                    out_project(g + back, i)
                elif kind == "x":
                    transposed_x(g, g * 16 + 32, c.fg - DC, [i])

        transposed_x(0, 16, -DC)
        attn_groups(pe, c, steps)

    def attn_scalar(act, c):
        act.sem_inc(c.s["p_ready"], 2)
        act.sem_inc(c.s["xt_hi"], C1)

        def transposed_x(g, k, chunks=range(DC)):
            for ch in chunks:
                act.wait_ge(c.s["g_full"], filled(c, g, k + ch))
                nc.scalar.activation(c.XT[0][:, ch, :], ps[:, G0 + ch % 2, :], ACT.Identity).then_inc(c.s["xt_hi"], 1)

        def steps(g, order):
            for kind, i, back in order:
                if kind == "e":
                    act.wait_ge(c.s["s_max"], g * NQ + (i + 1))
                    for j in range(QH):
                        kw = {"accum_out": c.sums[:, i // 2 % 2, i % 2 * QH + j:i % 2 * QH + j + 1]} if c.narrow else {}
                        last = nc.scalar.activation(c.Pr[:, i % c.slots, j, :], ps[:, c.bank(i), j * S:(j + 1) * S], ACT.Exp,
                                                    bias=negm[:, i % c.slots, j:j + 1], **kw)
                    last.then_inc(c.s["p_ready"], 1)
                elif kind == "k" and c.copies > 1:
                    k = c.k_at(i)
                    act.wait_ge(c.s["g_full"], filled(c, g, k))
                    for j in range(c.copies - 1):
                        bias = 0.0 if c.bk is None else c.bkm[:, i, j:j + 1]
                        last = nc.scalar.activation(c.KT[:, i, j, :], ps[:, G0 + k % 2, :], ACT.Identity,
                                                    bias=bias, scale=head[:, j:j + 1])
                    last.then_inc(c.s["k_most"], 1)
                elif kind == "zh":
                    act.wait_ge(c.s["z_ready"], (g + back) * (NQ // 2) + ((i + 1) * 2 + C1))
                    if type(g) is not int or g + back > 0 or i > 0:
                        act.wait_ge(c.s["e_full"], (g + back) * GB + i)
                    nc.scalar.activation(c.zT[0][:, :, :], c.z[:, i % 2, :, :], ACT.Identity).then_inc(c.s["e_hi"], 1)
                elif kind == "zt":
                    for f in range(c.nz):
                        k = i * (c.nz + 1) + f
                        act.wait_ge(c.s["e_full"], (g + back) * c.fe + (k + 1))
                        nc.scalar.activation(c.zT[0][:, f * c.zc:(f + 1) * c.zc, :].rearrange("p a b -> p (a b)"),
                                             ps[:, E0 + k % 2, 0:c.zc * S], ACT.Identity).then_inc(c.s["e_hi"], 1)
                elif kind == "r":
                    act.wait_ge(c.s["r_full"], (g + back) * (NQ // 2) + (i + 1))
                    nc.scalar.activation(c.rz[:, i % 2, :], ps[:, E1, 0:S], ACT.Identity).then_inc(c.s["rz_ready"], 1)
                elif kind == "x":
                    transposed_x(g, c.fg - DC, [i])

        if c.cross:
            act.wait_ge(c.s["bk_ready"], 1)
        transposed_x(0, -DC)
        attn_groups(act, c, steps)

    def attn_vector(v, c, link, extra):
        v.sem_inc(c.s["g_evac"], 2)
        v.sem_inc(c.s["e_evac"], 2)
        for first in ("ct_ready", "gates_done", "x_done", "pt_ready", "z_ready", "zt_ready", "rz_ready"):
            v.sem_inc(c.s[first], C1)
        if c.narrow:
            v.wait_ge(v45_made, 1)
        else:
            nc.vector.memset(c.V[:, :, :, c.hd:c.hd + 1], 1.0)
        if c.cross:
            nc.vector.tensor_tensor(c.bkm[:, :, :], c.bk.unsqueeze(2).broadcast_to([P, c.nch, 4]),
                                    head[:, :].unsqueeze(1).broadcast_to([P, c.nch, 4]), ALU.mult).then_inc(c.s["bk_ready"], 1)

        def lo(hi, low, psum, done):
            nc.vector.tensor_tensor(low, psum, hi.bitcast(F32), ALU.subtract).then_inc(done, 1)

        def transposed_x(g, n, chunks=range(DC)):
            for ch in chunks:
                v.wait_ge(c.s["xt_hi"], n * DC + (ch + 1 + C1 - DC))
                lo(c.XT[0][:, ch, :], c.XT[1][:, ch, :], ps[:, G0 + ch % 2, :], c.s["g_evac"])

        def query(g, ch):
            k = c.q_at(ch)
            v.wait_ge(c.s["g_full"], filled(c, g, k))
            if c.bq is None:
                last = nc.vector.tensor_scalar(c.QT[:, ch, :], ps[:, G0 + k % 2, :], c.scale, None, ALU.mult)
            else:
                last = nc.vector.tensor_scalar(c.QT[:, ch, :], ps[:, G0 + k % 2, :], c.bq[:, ch:ch + 1], c.scale,
                                               ALU.add, ALU.mult)
            last.then_inc(c.s["g_evac"], 1)

        def key(g, ch):
            k = c.k_at(ch)
            src = ps[:, G0 + k % 2, :]
            v.wait_ge(c.s["g_full"], filled(c, g, k))
            if c.copies == 1:
                last = nc.vector.tensor_scalar(c.KT[:, ch, 0, :], src, c.bk[:, ch:ch + 1], None, ALU.add)
            else:
                j = c.copies - 1
                v.wait_ge(c.s["k_most"], g * c.nch + (ch + 1))
                if c.bk is None:
                    last = nc.vector.tensor_scalar(c.KT[:, ch, j, :], src, head[:, j:j + 1], None, ALU.mult)
                else:
                    last = nc.vector.tensor_scalar(c.KT[:, ch, j, :], src, c.bk[:, ch:ch + 1],
                                                   head[:, j:j + 1], ALU.add, ALU.mult)
            last.then_inc(c.s["g_evac"], 1)

        def value(g, f):
            b, w = divmod(f, c.vh)
            k = 2 * c.nch + f
            hv = c.vn // c.hd
            v.wait_ge(c.s["g_full"], filled(c, g, k))
            if c.narrow:
                for half in range(2):
                    def of_half(t, n):
                        return t.rearrange("p (g r i e) -> p g r i e", g=2, r=2, i=QH)[:, :, half, :, n]
                    dst = of_half(c.V[:, b, :, :].rearrange("p q w -> p (q w)"), slice(64 * half, 64 * half + c.hd))
                    src = of_half(ps[:, G0 + k % 2, 0:c.vn], slice(0, c.hd))
                    if c.bv is None:
                        last = nc.vector.tensor_copy(dst, src)
                    else:
                        last = nc.vector.tensor_tensor(dst, src, of_half(c.bv, slice(0, c.hd)), ALU.add)
                last.then_inc(c.s["g_evac"], 1)
                return
            dst = c.V[:, b, w * hv:(w + 1) * hv, 0:c.hd]
            src = ps[:, G0 + k % 2, 0:c.vn].rearrange("p (h e) -> p h e", h=hv)
            if c.bv is None:
                last = nc.vector.tensor_copy(dst, src)
            else:
                bias = c.bv[:, w * c.vn:(w + 1) * c.vn].rearrange("p (h e) -> p h e", h=hv)
                last = nc.vector.tensor_tensor(dst, src, bias, ALU.add)
            last.then_inc(c.s["g_evac"], 1)

        def maxima(g, n):
            v.wait_ge(c.s["s_full"], g * NQ + (n + 1))
            nc.vector.reduce_max(negm[:, n % c.slots, :], ps[:, c.bank(n), :].rearrange("p (h k) -> p h k", h=QH), AX.X,
                                 negate=True).then_inc(c.s["s_max"], 1)

        def gates_of(g, n):
            b = n // 4
            if n == 0:
                v.wait_ge(c.s["ctx_loaded"], g * 32 + 32)
            for e in range(2 * (n % 4), 2 * (n % 4) + 2):
                nc.vector.scalar_tensor_tensor(junk[:, :], itokg[:, b, :], float(e), ctxg1[:, b, :], ALU.is_equal,
                                               ALU.mult, accum_out=gates[:, g * GB + b, e:e + 1]).then_inc(c.s["gates_done"], 1)
                v.wait_ge(c.s["gates_done"], g * (GB * E_OUT) + (b * E_OUT + e + 1 + C1))

        def normalised_pair(g, p):
            v.wait_ge(c.s["rz_ready"], g * (NQ // 2) + (p + 1 + C1))
            v.wait_ge(c.s["z_full"], g * (NQ // 2) + (p + 1))
            nc.vector.tensor_tensor(c.z[:, p // 2 % 2, p % 2, :], ps[:, ZB, 0:S], c.rz[:, p % 2, :],
                                    ALU.mult).then_inc(c.s["z_ready"], 1)

        def head_outputs(g, n):
            q = n % (H // QH)
            w = c.hd + 1
            zz = ps[:, ZB, 0:QH * w].rearrange("p (h e) -> p h e", h=QH)
            v.wait_ge(c.s["z_full"], g * NQ + (n + 1))
            link(nc.vector.reciprocal(rec[:, :].unsqueeze(2), zz[:, :, c.hd:w]))
            nc.vector.tensor_tensor(c.of_quad(c.z[:, n // 4 % 2, :], q), zz[:, :, 0:c.hd],
                                    rec[:, :].unsqueeze(2).broadcast_to([P, QH, c.hd]), ALU.mult).then_inc(c.s["z_ready"], 1)

        def norm_a(g, b):
            k = b * (c.nz + 1) + c.nz
            v.wait_ge(c.s["e_full"], g * c.fe + (k + 1))
            if b == 0:
                v.wait_ge(c.s["xb_ready"], g + 1 + C1)
            nc.vector.tensor_tensor(c.r[:, b % 2, :], ps[:, E1 if c.narrow else E0 + k % 2, 0:D], c.XB[:, b, :], ALU.add).then_inc(c.s["e_evac"], 1)

        def norm_stats(g, b):
            v.wait_ge(c.s["e_evac"], g * c.fe + (b * (c.nz + 1) + c.nz + 3))
            link(nc.vector.bn_stats(stats[:, b, :], c.r[:, b % 2, :]), alone=True)
            link(nc.vector.bn_aggr(mv[:, b, :], stats[:, b, :]))
            nc.vector.tensor_scalar(veps[:, b:b + 1], mv[:, b, 1:2], LN_EPS, None, ALU.add).then_inc(c.s["ln_var"], 1)

        def norm_b(g, b):
            v.wait_ge(c.s["rstd_ready"], g * GB + (b + 1))
            nc.vector.tensor_scalar(X[:, g * GB + b, :], c.r[:, b % 2, :], mv[:, b, 0:1], rstd[:, b:b + 1],
                                    ALU.subtract, ALU.mult).then_inc(c.s["x_done"], 1)
            v.wait_ge(c.s["x_done"], g * GB + (b + 1 + C1))

        def steps(g, order):
            if type(g) is not int:
                link.begin(g, 1, c.links)
            for kind, i, back in order:
                if kind == "q":
                    query(g, i)
                elif kind == "k":
                    key(g, i)
                elif kind == "v":
                    value(g, i)
                elif kind == "s":
                    maxima(g, i)
                    if c is A1:
                        gates_of(g, i)
                elif kind == "t":
                    v.wait_ge(c.s["pt_full"], (g + back) * NQ + (i + 1))
                    if c.narrow and i % 2:
                        pair = i // 2 % 2
                        nc.vector.reciprocal(c.rec[:, pair, :], c.sums[:, pair, :]).then_inc(c.s["rec_ready"], 1)
                    nc.vector.tensor_copy(c.PT[:, i % 2, :, :].rearrange("p a b -> p (a b)"), ps[:, PTB, :]).then_inc(c.s["pt_ready"], 1)
                elif kind == "pv" and not c.narrow:
                    head_outputs(g + back, i)
                elif kind == "z":
                    normalised_pair(g + back, i)
                elif kind == "zl":
                    v.wait_ge(c.s["e_hi"], (g + back) * GB + (i + 1))
                    nc.vector.tensor_tensor(c.zT[1][:, :, :], c.z[:, i % 2, :, :], c.zT[0][:, :, :].bitcast(F32),
                                            ALU.subtract).then_inc(c.s["zt_ready"], 1)
                    v.wait_ge(c.s["zt_ready"], (g + back) * GB + (i + 1 + C1))
                elif kind == "zt":
                    for f in range(c.nz):
                        k = i * (c.nz + 1) + f
                        v.wait_ge(c.s["e_hi"], (g + back) * (GB * c.nz) + (i * c.nz + f + 1))
                        part = slice(f * c.zc, (f + 1) * c.zc)
                        lo(c.zT[0][:, part, :].rearrange("p a b -> p (a b)"), c.zT[1][:, part, :].rearrange("p a b -> p (a b)"),
                           ps[:, E0 + k % 2, 0:c.zc * S], c.s["e_evac"])
                elif kind == "na":
                    norm_a(g + back, i)
                elif kind == "ns":
                    norm_stats(g + back, i)
                elif kind == "nb":
                    norm_b(g + back, i)
                elif kind == "x":
                    transposed_x(g, g + 2, [i])
                if type(g) is int and g == 0 and (kind, i) in extra:
                    extra[kind, i]()
            if type(g) is not int:
                link.end(NG)

        transposed_x(0, 1)
        attn_groups(v, c, steps)

    NU = 2 * NG * HC
    NG_STEPS = 8

    def mix_setup(tag, gelu, win, wout, first, pair0, per):
        c = Stage()
        c.gelu, c.win, c.wout = gelu, win, wout
        c.first, c.pair0, c.per = first, pair0, per
        m = r2.again()
        c.XT = pair(m, tag + "XT", [P, DC, B * S])
        c.hT = pair(m, tag + "hT", [P, HC, GT])
        if gelu:
            c.slots = slots6
            c.h32 = m.place(tag + "h32", [P, 2, GT], F32)
            c.lg = m.place(tag + "lg", [P, B, E_OUT], F32)
            c.ex = m.place(tag + "ex", [P, B, E_OUT], F32)
            c.t1 = m.place(tag + "t1", [P, B], F32)
            c.t2 = m.place(tag + "t2", [P, B], F32)
            c.b1 = m.place(tag + "b1", [P, 2, HC], F32)
        else:
            c.slots = [pair(m, f"{tag}w{i}", [P, 2 * RAW]) for i in range(2)]
        c.s = signals(tag, "g_full xt_hi g_evac u_full hi_ready lo_ready d_full comb_done ln_var rstd_ready x_done "
                           "logits ex_ready step b1_ready")
        return c

    M2 = mix_setup("m2", False, w_e1i, w_e1o, U_E0, U_PAIR, 6)
    M6 = mix_setup("m6", True, w_e6i, w_e6o, U_E6, U_PAIR6, 4)

    def load_unit(sp, base, k, src, ncols):
        sp.wait_ge(prep_done, base + (k - 1))
        sp.dma_start(raw[k % 2][:, 0:ncols], src).then_inc(raw_loaded[k % 2], 16)

    def split_unit(v, base, k, w, ncols, on=nc.vector):
        v.wait_ge(raw_loaded[k % 2], (base + (k - k % 2)) * 8 + 16)
        on.tensor_scalar(w[0], raw[k % 2][:, 0:ncols], 1.0, None, ALU.mult).then_inc(split_hi, 1)
        v.wait_ge(split_hi, base + (k + 1))
        on.tensor_tensor(w[1], raw[k % 2][:, 0:ncols], w[0].bitcast(F32), ALU.subtract).then_inc(prep_done, 1)

    def cut(w, at, n):
        return [t[:, at:at + n] for t in w]

    def mix_sync(sp, c):
        with sp.Fori(0, E_OUT // 2) as i:
            base = i * c.per + c.pair0
            odd, even = i * 2 + 1, (i * 2 + 2) % E_OUT
            load_unit(sp, base, 0, c.win[bass.ds(odd, 1)].rearrange("a p n -> (a p) n"), RAW)
            load_unit(sp, base, 1, c.wout[bass.ds(odd, 1)].rearrange("a p n -> (a p) n"), RAW)
            if not c.gelu:
                for k in range(2):
                    load_unit(sp, base, 2 + k, w_ffn[:, bass.ds(i * (2 * FU) + k * FU, FU)], FU)
            load_unit(sp, base, c.per - 2, c.win[bass.ds(even, 1)].rearrange("a p n -> (a p) n"), RAW)
            load_unit(sp, base, c.per - 1, c.wout[bass.ds(even, 1)].rearrange("a p n -> (a p) n"), RAW)

    def mix_order(c):
        if c.gelu:
            start = [("x", k) for k in range(4)]
        else:
            start = [("w", 0)] + [("x", k) for k in range(4)] + [("w", 1)]
        start += [("u", 0), ("x", 4), ("x", 5), ("u", 1), ("x", 6), ("x", 7)]
        for u in range(2, NU + 2):
            start += [("u", u)] if u < NU else []
            start.append(("d", u - 2))
            if c.gelu:
                start += {2: [("l", 0)], 3: [("g", 0)], 5: [("g", 1)], 6: [("e", 0)], 7: [("g", 2)]}.get(u, [])
            if u < NU and u % HC == 2 and u >= HC + 2 and u != HC + 2:
                start.append(("c", u // HC - 1))
            elif u == 2 * HC:
                start.append(("c", 0))
        return start + [("c", 2 * NG - 1)]

    def mix_tensor(pe, c):
        def transposed_x(k):
            g, ch = divmod(k, DC)
            pe.wait_ge(c.s["g_evac"], k + 1)
            for j in range(GB):
                last = nc.tensor.transpose(ps[:, 4 + k % 2, j * S:(j + 1) * S], X[:, g * GB + j, ch * P:(ch + 1) * P], ident[:, :])
            last.then_inc(c.s["g_full"], 1)

        def logits():
            rh, rl = (t[:, 32:48].rearrange("p (k n) -> p k n", k=DC) for t in (rw_h, rw_l))
            pe.wait_ge(c.s["g_evac"], NG * DC + 2)
            for t in range(B):
                for i in range(DC):
                    last = split3(nc, ps[:, 4, t * 8:(t + 1) * 8], c.XT[0][:, i, t * S:(t + 1) * S],
                                  c.XT[1][:, i, t * S:(t + 1) * S], rh[:, i, :], rl[:, i, :], i == 0, i == DC - 1)
            last.then_inc(c.s["logits"], 1)

        def up(i, u):
            e2, r = divmod(u, NG * HC)
            g, ch = divmod(r, HC)
            first = type(i) is int
            if first and ch == 0 and e2 == 0:
                pe.wait_ge(c.s["g_evac"], (g + 1) * DC + 2)
            if first and u == 0:
                pe.wait_ge(prep_done, c.first + 1)
            elif r == 0:
                pe.wait_ge(prep_done, i * c.per + (c.pair0 + 2 * e2))
            wh, wl = (t[:, 0:RAW].rearrange("p (k n) -> p k n", k=DC) for t in c.slots[e2])
            pe.wait_ge(c.s["lo_ready"], i * NU + u + 1)
            for k in range(DC):
                last = split3(nc, ps[:, u % 2, :], wh[:, k, ch * P:(ch + 1) * P], wl[:, k, ch * P:(ch + 1) * P],
                              c.XT[0][:, k, g * GT:(g + 1) * GT], c.XT[1][:, k, g * GT:(g + 1) * GT], k == 0, k == DC - 1)
            last.then_inc(c.s["u_full"], 1)

        def down(i, u):
            e2 = u // (NG * HC)
            q, ch = divmod(u, HC)
            if type(i) is int and u == 0:
                pe.wait_ge(prep_done, c.pair0)
            pe.wait_ge(c.s["lo_ready"], i * NU + u + 3)
            if ch == 0:
                pe.wait_ge(c.s["comb_done"], i * (2 * B) + GB * (q + 1))
            wh, wl = (t[:, RAW:2 * RAW].rearrange("p (k n) -> p k n", k=HC) for t in c.slots[e2])
            for j in range(GB):
                acc = ps[:, (2, 6)[q % 2] + j // 2, (j % 2) * D:(j % 2 + 1) * D]
                last = split3(nc, acc, c.hT[0][:, ch, j * S:(j + 1) * S], c.hT[1][:, ch, j * S:(j + 1) * S],
                              wh[:, ch, :], wl[:, ch, :], ch == 0 and j % 2 == 0, ch == HC - 1 and j % 2 == 1,
                              skip_group_check=True)
            if ch == HC - 1:
                last.then_inc(c.s["d_full"], 1)

        for kind, k in mix_order(c):
            if kind == "x":
                transposed_x(k)
            elif kind == "u":
                up(0, k)
            elif kind == "d":
                down(0, k)
            elif kind == "l":
                logits()
        with pe.Fori(1, E_OUT // 2) as i:
            for u in range(NU + 2):
                if u < NU:
                    up(i, u)
                if u >= 2:
                    down(i, u - 2)

    def mix_scalar(act, c):
        def hidden(i, u):
            e2, ch = u // (NG * HC), u % HC
            if c.gelu and u == 0:
                act.wait_ge(c.s["b1_ready"], i + 1)
            act.wait_ge(c.s["u_full"], i * NU + u + 1)
            if c.gelu:
                bias = c.b1[:, e2, ch:ch + 1]
                nc.scalar.activation(c.h32[:, u % 2, :], ps[:, u % 2, :], ACT.Gelu, bias=bias)
                nc.scalar.activation(c.hT[0][:, ch, :], ps[:, u % 2, :], ACT.Gelu, bias=bias).then_inc(c.s["hi_ready"], 1)
            else:
                nc.scalar.activation(c.hT[0][:, ch, :], ps[:, u % 2, :], ACT.Relu).then_inc(c.s["hi_ready"], 1)

        for kind, k in mix_order(c):
            if kind == "x":
                g, ch = divmod(k, DC)
                act.wait_ge(c.s["g_full"], k + 1)
                nc.scalar.activation(c.XT[0][:, ch, g * GT:(g + 1) * GT], ps[:, 4 + k % 2, :], ACT.Identity).then_inc(c.s["xt_hi"], 1)
            elif kind == "u":
                hidden(0, k)
            elif kind == "e":
                act.wait_ge(c.s["step"], NG_STEPS)
                nc.scalar.activation(c.ex[:, :, :], c.lg[:, :, :], ACT.Exp, scale=2.0).then_inc(c.s["ex_ready"], 1)
        with act.Fori(1, E_OUT // 2) as i:
            for u in range(NU):
                hidden(i, u)

    def mix_pool(pool, c):
        if c.gelu:
            pool.wait_ge(c.s["step"], 4)
            nc.gpsimd.tensor_tensor(c.t2[:, :], c.t1[:, :], mhalf[:, :], ALU.pow).then_inc(c.s["rstd_ready"], 1)
        for g in range(NG):
            own = slice(g * GB, (g + 1) * GB)
            pool.wait_ge(c.s["ln_var"], g + 1)
            nc.gpsimd.tensor_tensor(rstd[:, own], veps[:, own], mhalf[:, own], ALU.pow).then_inc(c.s["rstd_ready"], 1)

    def gate_scale(v, c, n, part):
        def step(ins):
            n[0] += 1
            ins.then_inc(c.s["step"], 1)
            v.wait_ge(c.s["step"], n[0])

        def over(t):
            return t[:, :].unsqueeze(2).broadcast_to([P, B, E_OUT])

        def across(row):
            return row.unsqueeze(1).broadcast_to([P, B, row.shape[1]])
        if part == 0:
            v.wait_ge(c.s["logits"], 1)
            step(nc.vector.tensor_tensor(c.lg[:, :, :], ps[:, 4, 0:B * E_OUT].rearrange("p (b e) -> p b e", b=B), across(row_gb), ALU.add))
            step(nc.vector.tensor_tensor(c.ex[:, :, :], c.lg[:, :, :], c.lg[:, :, :], ALU.mult))
            step(nc.vector.reduce_sum(c.t1[:, :], c.ex[:, :, :], AX.X))
            step(nc.vector.tensor_scalar(c.t1[:, :], c.t1[:, :], 1.0 / E_OUT, 2.0 ** -23, ALU.mult, ALU.add))
        elif part == 1:
            v.wait_ge(c.s["rstd_ready"], 1)
            step(nc.vector.tensor_tensor(c.lg[:, :, :], c.lg[:, :, :], over(c.t2), ALU.mult))
            step(nc.vector.tensor_tensor(c.lg[:, :, :], c.lg[:, :, :], across(row_rms), ALU.mult))
            step(nc.vector.reduce_max(c.t1[:, :], c.lg[:, :, :], AX.X))
            step(nc.vector.tensor_tensor(c.lg[:, :, :], c.lg[:, :, :], over(c.t1), ALU.subtract))
            assert n[0] == NG_STEPS
        else:
            v.wait_ge(c.s["ex_ready"], 1)
            step(nc.vector.reduce_sum(c.t1[:, :], c.ex[:, :, :], AX.X))
            step(nc.vector.reciprocal(c.t2[:, :], c.t1[:, :]))
            step(nc.vector.tensor_scalar(c.t1[:, :], c.t2[:, :], 1e-6, None, ALU.add))
            step(nc.vector.reciprocal(c.t1[:, :], c.t1[:, :]))
            step(nc.vector.tensor_tensor(ng[:, :], c.t1[:, :], c.t2[:, :], ALU.mult))
            v.wait_ge(b2_loaded, 16)
            step(nc.vector.reduce_sum(b2sum[:, :], b2rows[:, :, :].rearrange("p e d -> p d e"), AX.X))

    def mix_vector(v, c):
        n = [0]
        v.sem_inc(c.s["g_evac"], 2)
        v.sem_inc(c.s["lo_ready"], 2)
        v.sem_inc(c.s["comb_done"], 2 * GB)

        def transposed_x(k):
            g, ch = divmod(k, DC)
            tok = slice(g * GT, (g + 1) * GT)
            v.wait_ge(c.s["xt_hi"], k + 1)
            nc.vector.tensor_tensor(c.XT[1][:, ch, tok], ps[:, 4 + k % 2, :], c.XT[0][:, ch, tok].bitcast(F32),
                                    ALU.subtract).then_inc(c.s["g_evac"], 1)

        def biases(i):
            if c.gelu:
                nc.vector.tensor_scalar(c.b1[:, :, :].rearrange("p a b -> p (a b)"), col_b1[:, bass.ds(i * (2 * HC), 2 * HC)],
                                        1.0, None, ALU.mult).then_inc(c.s["b1_ready"], 1)

        def hidden(i, u):
            ch = u % HC
            v.wait_ge(c.s["hi_ready"], i * NU + u + 1)
            if c.gelu:
                last = nc.vector.tensor_tensor(c.hT[1][:, ch, :], c.h32[:, u % 2, :], c.hT[0][:, ch, :].bitcast(F32), ALU.subtract)
            else:
                last = nc.vector.scalar_tensor_tensor(c.hT[1][:, ch, :], ps[:, u % 2, :], 0.0,
                                                      c.hT[0][:, ch, :].bitcast(F32), ALU.max, ALU.subtract)
            last.then_inc(c.s["lo_ready"], 1)

        def combine(i, q):
            e2, g = divmod(q, NG)
            if c.gelu and type(i) is int and i + e2 == 0:
                for t in range(g * GB, (g + 1) * GB):
                    n[0] += 1
                    nc.vector.scalar_tensor_tensor(X[:, t, :], b2sum[:, :], ng[:, t:t + 1], X[:, t, :], ALU.mult, ALU.add).then_inc(c.s["step"], 1)
                v.wait_ge(c.s["step"], n[0])
            v.wait_ge(c.s["d_full"], i * (2 * NG) + q + 1)
            for j in range(GB):
                t = g * GB + j
                gate = ng[:, t:t + 1] if c.gelu else gates[:, t, bass.ds(i * 2 + e2, 1)]
                acc = ps[:, (2, 6)[q % 2] + j // 2, (j % 2) * D:(j % 2 + 1) * D]
                nc.vector.scalar_tensor_tensor(X[:, t, :], acc, gate, X[:, t, :], ALU.mult, ALU.add).then_inc(c.s["comb_done"], 1)

        def weights(i, u):
            base = i * c.per + c.pair0
            if u in (3, 5):
                k = (u - 3) // 2
                split_unit(v, base, k, cut(c.slots[1], k * RAW, RAW), RAW)
            if u in (8, 12) and not c.gelu:
                k = (u - 8) // 4
                split_unit(v, base, 2 + k, [t[:, bass.ds(i * (2 * FU) + k * FU, FU)] for t in wF], FU)
            if u in (20, 24):
                k = (u - 20) // 4
                split_unit(v, base, c.per - 2 + k, cut(c.slots[0], k * RAW, RAW), RAW)

        def stats_of(g):
            seqs = range(g * GB, (g + 1) * GB)
            v.wait_ge(c.s["comb_done"], (E_OUT - 1) * B + (g + 1) * GB + 2 * GB)
            for t in seqs:
                n[0] += 1
                nc.vector.bn_stats(stats[:, t, :], X[:, t, :]).then_inc(c.s["step"], 1)
            v.wait_ge(c.s["step"], n[0])
            for t in seqs:
                n[0] += 1
                nc.vector.bn_aggr(mv[:, t, :], stats[:, t, :]).then_inc(c.s["step"], 1)
            v.wait_ge(c.s["step"], n[0])
            own = slice(g * GB, (g + 1) * GB)
            nc.vector.tensor_scalar(veps[:, own].unsqueeze(2), mv[:, own, 1:2], LN_EPS, None, ALU.add).then_inc(c.s["ln_var"], 1)

        def normalise(g):
            v.wait_ge(c.s["rstd_ready"], g + (2 if c.gelu else 1))
            for t in range(g * GB, (g + 1) * GB):
                nc.vector.tensor_scalar(X[:, t, :], X[:, t, :], mv[:, t, 0:1], rstd[:, t:t + 1],
                                        ALU.subtract, ALU.mult).then_inc(c.s["x_done"], 1)

        biases(0)
        for kind, k in mix_order(c):
            if kind == "w":
                split_unit(v, c.first, k, cut(c.slots[0], k * RAW, RAW), RAW)
            elif kind == "x":
                transposed_x(k)
            elif kind == "u":
                hidden(0, k)
                weights(0, k)
            elif kind == "g":
                gate_scale(v, c, n, k)
            elif kind == "c":
                combine(0, k)
        with v.Fori(1, E_OUT // 2 - 1) as i:
            biases(i)
            for u in range(NU):
                hidden(i, u)
                if u >= HC + 2 and u % HC == 2:
                    combine(i, u // HC - 1)
                weights(i, u)
            combine(i, 2 * NG - 1)
        i = E_OUT // 2 - 1
        biases(i)
        for u in range(NU):
            hidden(i, u)
            q = u // HC - 1
            if u >= HC + 2 and u % HC == 2:
                combine(i, q)
                if q >= NG:
                    stats_of(q - NG)
            if u % HC == 3 and q >= NG:
                normalise(q - NG)
            weights(i, u)
        combine(i, 2 * NG - 1)
        stats_of(NG - 1)
        normalise(NG - 1)
        v.wait_ge(c.s["x_done"], B)

    F3 = Stage()
    m = r2.again()
    F3.Xs = m.place("f3Xs", [P, GB, D], F32)
    F3.XT = pair(m, "f3XT", [P, DC, GT])
    F3.gs = m.place("f3gs", [P, 2, GT], F32)
    F3.tt = m.place("f3tt", [P, 2, GT], F32)
    F3.h32 = m.place("f3h32", [P, 2, GT], F32)
    F3.hT = pair(m, "f3hT", [P, 3, GT])
    F3.r = m.place("f3r", [P, GB, D], F32)
    F3.sel32 = m.place("f3sel32", [R_N, FC - SC, P], F32)
    F3.sel = m.place("f3sel", [R_N, FC - SC, P], F32R)
    F3.combT = pair(m, "f3combT", [R_N, GT])
    F3.lg = m.place("f3lg", [P, GB, R_N], F32)
    F3.pr = m.place("f3pr", [P, GB, R_N + 6], F32)
    F3.mr = m.place("f3mr", [P, GB, R_N + 6], F32)
    F3.comb = m.place("f3comb", [P, GB, R_N], F32)
    F3.top = m.place("f3top", [P, GB, 8], F32)
    F3.t1 = m.place("f3t1", [P, GB], F32)
    F3.t2 = m.place("f3t2", [P, GB], F32)
    F3.s = signals("f3", "xs_loaded xt_hi g_full g_evac soft_exp comb_ready gu_full sg_ready t_done hi_ready h_ready "
                         "d_full r_done ln_var rstd_ready x_done sel_pool sel_ready")
    assert m.at <= V45_at
    FG = DC + 2 + FC - SC
    F_LINKS = 18 + 2 * GB

    def ffn_sync(sp):
        s = F3.s
        with sp.Fori(0, NG) as g:
            sp.wait_ge(s["xt_hi"], g * DC + C1)
            sp.dma_start(F3.Xs[:, :, :], X[:, bass.ds(g * GB, GB), :]).then_inc(s["xs_loaded"], 16)

    def ffn_pool(pool):
        s = F3.s
        nc.gpsimd.memset(F3.sel32[:, :, :], 0.0).then_inc(s["sel_pool"], 1)
        pool.wait_ge(s["sel_pool"], 1)
        sel = F3.sel32[:, :, :].rearrange("e c (a m) -> e c a m", a=2)
        nc.gpsimd.affine_select(out=sel, in_=sel, compare_op=ALU.not_equal, fill=1.0, base=0,
                                pattern=[[-2, FC - SC], [-1, 2], [0, R_MID]], channel_multiplier=1).then_inc(s["sel_pool"], 1)
        nc.gpsimd.memset(V45[:, :, :, :], 0.0).then_inc(v45_made, 1)
        with pool.Fori(0, NG) as g:
            pool.wait_ge(s["ln_var"], g + 1)
            nc.gpsimd.tensor_tensor(rstd[:, 0:GB], veps[:, 0:GB], mhalf[:, 0:GB], ALU.pow).then_inc(s["rstd_ready"], 1)

    def ffn_tensor(pe):
        s = F3.s
        wgu = [t[:, 0:2 * DC * FC * P].rearrange("p (k n) -> p k n", k=DC) for t in wF]
        wd = [t[:, 2 * DC * FC * P:].rearrange("p (k n) -> p k n", k=FC) for t in wF]
        rh, rl = (t[:, 0:32].rearrange("p (k n) -> p k n", k=DC) for t in (rw_h, rw_l))

        def g_fill(g, k):
            pe.wait_ge(s["g_evac"], g * FG + k + 1)
            return ps[:, 4 + k % 2, :]

        def up(g, c):
            pe.wait_ge(s["sg_ready"], g * FC + c + 1)
            pe.wait_ge(s["t_done"], g * FC + c + 1)
            for part in range(2):
                at = (part * FC + c) * P
                for k in range(DC):
                    last = split3(nc, ps[:, 2 * part + c % 2, :], wgu[0][:, k, at:at + P], wgu[1][:, k, at:at + P],
                                  F3.XT[0][:, k, :], F3.XT[1][:, k, :], k == 0, k == DC - 1)
            last.then_inc(s["gu_full"], 1)

        def spread(g, c):
            bank = g_fill(g, DC + 2 + c - SC)
            if c == SC:
                pe.wait_ge(s["g_evac"], g * FG + DC + 4)
            nc.tensor.matmul(bank, F3.sel[:, c - SC, :], F3.combT[0][:, :], start=True, stop=False)
            nc.tensor.matmul(bank, F3.sel[:, c - SC, :], F3.combT[1][:, :], start=False, stop=True).then_inc(s["g_full"], 1)

        def down(g, c):
            pe.wait_ge(s["h_ready"], g * FC + c + 1 + C1)
            if c == 0:
                pe.wait_ge(s["r_done"], g * GB + C1)
            for j in range(GB):
                acc = ps[:, 6 + j // 2, (j % 2) * D:(j % 2 + 1) * D]
                last = split3(nc, acc, F3.hT[0][:, c % 3, j * S:(j + 1) * S], F3.hT[1][:, c % 3, j * S:(j + 1) * S],
                              wd[0][:, c, :], wd[1][:, c, :], c == 0 and j % 2 == 0, c == FC - 1 and j % 2 == 1,
                              skip_group_check=True)
            if c == FC - 1:
                last.then_inc(s["d_full"], 1)

        pe.wait_ge(s["sel_ready"], 1)
        with pe.Fori(0, NG) as g:
            pe.wait_ge(s["xs_loaded"], (g + 1) * 16)
            for ch in range(DC):
                bank = g_fill(g, ch)
                for j in range(GB):
                    last = nc.tensor.transpose(bank[:, j * S:(j + 1) * S], F3.Xs[:, j, ch * P:(ch + 1) * P], ident[:, :])
                last.then_inc(s["g_full"], 1)
            bank = g_fill(g, DC)
            pe.wait_ge(s["g_evac"], g * FG + DC + 2)
            for j in range(GB):
                for i in range(DC):
                    last = split3(nc, bank[:, j * R_N:(j + 1) * R_N], F3.XT[0][:, i, j * S:(j + 1) * S],
                                  F3.XT[1][:, i, j * S:(j + 1) * S], rh[:, i, :], rl[:, i, :], i == 0, i == DC - 1)
            last.then_inc(s["g_full"], 1)
            for c in range(FC + 2):
                if c < FC:
                    up(g, c)
                if c == SC - 1:
                    bank = g_fill(g, DC + 1)
                    pe.wait_ge(s["comb_ready"], g + 1)
                    for j in range(GB):
                        last = nc.tensor.transpose(bank[0:R_N, j * S:(j + 1) * S], F3.comb[:, j, :], ident[:, :])
                    last.then_inc(s["g_full"], 1)
                if SC <= c < FC:
                    spread(g, c)
                if c >= 2:
                    down(g, c - 2)

    def ffn_scalar(act):
        s = F3.s
        act.sem_inc(s["sg_ready"], 2)
        act.sem_inc(s["xt_hi"], C1)
        with act.Fori(0, NG) as g:
            for ch in range(DC):
                act.wait_ge(s["g_full"], g * FG + ch + 1)
                nc.scalar.activation(F3.XT[0][:, ch, :], ps[:, 4 + ch % 2, :], ACT.Identity).then_inc(s["xt_hi"], 1)
            act.wait_ge(s["g_evac"], g * FG + DC + 3)
            nc.scalar.activation(F3.pr[:, :, 0:R_N], F3.lg[:, :, :], ACT.Exp).then_inc(s["soft_exp"], 1)
            for c in range(FC + 1):
                if c < FC:
                    act.wait_ge(s["gu_full"], g * FC + c + 1)
                    nc.scalar.activation(F3.gs[:, c % 2, :], ps[:, c % 2, :], ACT.Silu).then_inc(s["sg_ready"], 1)
                if c >= 1:
                    w = c - 1
                    if w < SC:
                        act.wait_ge(s["t_done"], g * FC + w + 3)
                    else:
                        act.wait_ge(s["g_evac"], g * FG + DC + 2 + w - SC + 3)
                    nc.scalar.activation(F3.hT[0][:, w % 3, :], F3.h32[:, w % 2, :], ACT.Identity).then_inc(s["hi_ready"], 1)

    def ffn_vector(v, link):
        s = F3.s
        v.sem_inc(s["g_evac"], 2)
        v.sem_inc(s["t_done"], 2)
        v.sem_inc(s["r_done"], C1)
        v.sem_inc(s["h_ready"], C1)
        v.wait_ge(s["sel_pool"], 2)
        nc.vector.tensor_copy(F3.sel[:, :, :], F3.sel32[:, :, :]).then_inc(s["sel_ready"], 1)
        nc.vector.memset(F3.pr[:, :, R_N:], -1.0).then_inc(s["sel_ready"], 1)
        v.wait_ge(s["sel_ready"], 2)
        for k in range(4):
            n, at = (768, k * 768) if k < 2 else (256, 1536 + (k - 2) * 256)
            split_unit(v, U_A4, k, cut(wA4, at, n), n)

        def over(t, n):
            return t.unsqueeze(2).broadcast_to([P, GB, n])

        with v.Fori(0, NG) as g:
            link.begin(g, 0, F_LINKS)
            for ch in range(DC):
                v.wait_ge(s["xt_hi"], g * DC + ch + 1 + C1)
                nc.vector.tensor_tensor(F3.XT[1][:, ch, :], ps[:, 4 + ch % 2, :], F3.XT[0][:, ch, :].bitcast(F32),
                                        ALU.subtract).then_inc(s["g_evac"], 1)
            v.wait_ge(s["g_full"], g * FG + DC + 1)
            lgp = ps[:, 4, 0:GB * R_N].rearrange("p (b e) -> p b e", b=GB)
            link(nc.vector.reduce_max(F3.t1[:, :], lgp, AX.X))
            nc.vector.tensor_tensor(F3.lg[:, :, :], lgp, over(F3.t1[:, :], R_N), ALU.subtract).then_inc(s["g_evac"], 1)
            v.wait_ge(s["soft_exp"], g + 1)
            probs = F3.pr[:, :, 0:R_N]
            link(nc.vector.reduce_sum(F3.t1[:, :], probs, AX.X))
            link(nc.vector.reciprocal(F3.t2[:, :], F3.t1[:, :]))
            link(nc.vector.tensor_tensor(probs, probs, over(F3.t2[:, :], R_N), ALU.mult), alone=True)
            for j in range(GB):
                (link if j == GB - 1 else link.note)(nc.vector.max(F3.top[:, j, :], F3.pr[:, j, 0:R_N]))
            link(nc.vector.tensor_tensor(F3.t1[:, :].unsqueeze(2), F3.top[:, :, 0:1], F3.top[:, :, 1:2], ALU.add))
            link(nc.vector.tensor_scalar(F3.t1[:, :], F3.t1[:, :], 1e-9, None, ALU.add))
            link(nc.vector.reciprocal(F3.t2[:, :], F3.t1[:, :]))
            link(nc.vector.memset(F3.top[:, :, 2:8], -1.0), alone=True)
            for j in range(GB):
                (link if j == GB - 1 else link.note)(
                    nc.vector.match_replace(F3.mr[:, j, :], F3.top[:, j, :], F3.pr[:, j, :], -2.0))
            link(nc.vector.scalar_tensor_tensor(F3.comb[:, :, :], F3.mr[:, :, 0:R_N], -2.0, probs, ALU.is_equal, ALU.mult))
            nc.vector.tensor_tensor(F3.comb[:, :, :], F3.comb[:, :, :], over(F3.t2[:, :], R_N), ALU.mult).then_inc(s["comb_ready"], 1)
            for c in range(FC + 1):
                if c < FC:
                    v.wait_ge(s["sg_ready"], g * FC + c + 3)
                    v.wait_ge(s["h_ready"], g * FC + max(c - 1, 0) + C1)
                    dst = F3.h32 if c < SC else F3.tt
                    nc.vector.tensor_tensor(dst[:, c % 2, :], F3.gs[:, c % 2, :], ps[:, 2 + c % 2, :], ALU.mult).then_inc(s["t_done"], 1)
                    if c >= SC:
                        k = DC + 2 + c - SC
                        v.wait_ge(s["g_full"], g * FG + k + 1)
                        v.wait_ge(s["t_done"], g * FC + c + 3)
                        nc.vector.tensor_tensor(F3.h32[:, c % 2, :], F3.tt[:, c % 2, :], ps[:, 4 + k % 2, :], ALU.mult).then_inc(s["g_evac"], 1)
                        v.wait_ge(s["g_evac"], g * FG + k + 3)
                if c == SC - 1:
                    v.wait_ge(s["g_full"], g * FG + DC + 2)
                    src = ps[0:R_N, 4 + (DC + 1) % 2, :]
                    link(nc.vector.tensor_copy(F3.combT[0][:, :], src))
                    nc.vector.tensor_tensor(F3.combT[1][:, :], src, F3.combT[0][:, :].bitcast(F32), ALU.subtract).then_inc(s["g_evac"], 1)
                if c >= 1:
                    w = c - 1
                    v.wait_ge(s["hi_ready"], g * FC + w + 1)
                    nc.vector.tensor_tensor(F3.hT[1][:, w % 3, :], F3.h32[:, w % 2, :], F3.hT[0][:, w % 3, :].bitcast(F32),
                                            ALU.subtract).then_inc(s["h_ready"], 1)
            v.wait_ge(s["d_full"], g + 1)
            for j in range(GB):
                acc = ps[:, 6 + j // 2, (j % 2) * D:(j % 2 + 1) * D]
                nc.vector.tensor_tensor(F3.r[:, j, :], acc, X[:, g * GB + j, :], ALU.add).then_inc(s["r_done"], 1)
            v.wait_ge(s["r_done"], (g + 1) * GB + C1)
            for j in range(GB):
                bn = nc.vector.bn_stats(stats[:, j, :], F3.r[:, j, :])
                if j == GB - 1:
                    link(bn, alone=True)
                else:
                    link.note(bn)
            for j in range(GB):
                (link if j == GB - 1 else link.note)(nc.vector.bn_aggr(mv[:, j, :], stats[:, j, :]))
            nc.vector.tensor_scalar(veps[:, 0:GB].unsqueeze(2), mv[:, 0:GB, 1:2], LN_EPS, None, ALU.add).then_inc(s["ln_var"], 1)
            v.wait_ge(s["rstd_ready"], g + 1)
            for j in range(GB):
                nc.vector.tensor_scalar(X[:, g * GB + j, :], F3.r[:, j, :], mv[:, j, 0:1], rstd[:, j:j + 1],
                                        ALU.subtract, ALU.mult).then_inc(s["x_done"], 1)
            v.wait_ge(s["x_done"], (g + 1) * GB)
        link.end(NG)

    class Link:

        def __init__(self, v):
            self.v, self.total, self.g, self.per, self.k = v, 0, 0, 0, 0

        def begin(self, g, first, per):
            self.total += self.k - first * per
            self.g, self.per, self.k = g, per, 0

        def note(self, ins):
            self.k += 1
            ins.then_inc(chain, 1)

        def __call__(self, ins, alone=False):
            self.note(ins)
            self.v.wait_ge(chain, self.g * self.per + (self.total + self.k))
            if alone:
                self.v.sem_inc(waited, 1)

        def end(self, beyond):
            assert self.k == self.per, (self.k, self.per)
            self.total += self.per * beyond
            self.g, self.per, self.k = 0, 0, 0

    block = nc.Block()
    with block as block:
        @block.sync
        def _(sp):
            sp.dma_start(X[:, :, :], x_in.rearrange("b s d -> s b d")).then_inc(x_loaded, 16)
            sp.dma_start(rows[:, :], rows_in.partition_broadcast(P)).then_inc(small_loaded, 16)
            sp.dma_start(cols[:, :], cols_in).then_inc(small_loaded, 16)
            sp.dma_start(bv1[:, :], bv_in.partition_broadcast(P)).then_inc(small_loaded, 16)
            for k in range(8):
                if k == 2:
                    sp.wait_ge(x_loaded, 16)
                    attn_first_loads(sp, A1)
                if k >= 2:
                    sp.wait_ge(prep_done, k - 1)
                sp.dma_start(raw[k % 2][:, :], w_a1[:, k * RAW:(k + 1) * RAW]).then_inc(raw_loaded[k % 2], 16)
            attn_sync(sp, A1)
            load_unit(sp, U_E0, 0, w_e1i[0], RAW)
            load_unit(sp, U_E0, 1, w_e1o[0], RAW)
            mix_sync(sp, M2)
            for k in range(4):
                n, at = (768, k * 768) if k < 2 else (256, 1536 + (k - 2) * 256)
                load_unit(sp, U_A4, k, w_a4[:, at:at + n], n)
            sp.wait_ge(stage_done, 2)
            ffn_sync(sp)
            for k in range(2):
                load_unit(sp, U_A5, k, w_a5[:, k * 768:(k + 1) * 768], 768)
            sp.wait_ge(stage_done, 3)
            attn_first_loads(sp, A4)
            attn_sync(sp, A4)
            load_unit(sp, U_E6, 0, w_e6i[0], RAW)
            load_unit(sp, U_E6, 1, w_e6o[0], RAW)
            sp.wait_ge(stage_done, 4)
            sp.dma_start(b2rows[:, :, :].rearrange("p e d -> p (e d)"), b2_in.partition_broadcast(P)).then_inc(b2_loaded, 16)
            attn_first_loads(sp, A5)
            attn_sync(sp, A5)
            mix_sync(sp, M6)
            for g in range(NG):
                own = slice(g * GB, (g + 1) * GB)
                sp.wait_ge(M6.s["x_done"], (g + 1) * GB)
                sp.dma_start(out[own].rearrange("b s d -> s b d"), X[:, own, :]).then_inc(out_stored, 16)
            sp.wait_ge(out_stored, 16 * NG)

        @block.gpsimd
        def _(pool):
            nc.gpsimd.memset(ident[:, :], 0.0).then_inc(consts_pool, 1)
            nc.gpsimd.memset(causal[:, :, :], 0.0).then_inc(consts_pool, 1)
            nc.gpsimd.memset(band[:, :, :], 0.0).then_inc(consts_pool, 1)
            nc.gpsimd.memset(head8[:, :, :], 1.0).then_inc(consts_pool, 1)
            pool.wait_ge(consts_pool, 4)
            nc.gpsimd.affine_select(out=ident[:, :], in_=ident[:, :], compare_op=ALU.not_equal, fill=1.0, base=0,
                                    pattern=[[-1, P]], channel_multiplier=1).then_inc(consts_pool, 1)
            nc.gpsimd.affine_select(out=causal[:, :, :], in_=causal[:, :, :], compare_op=ALU.is_ge, fill=NEG, base=0,
                                    pattern=[[0, QH], [-1, S]], channel_multiplier=1).then_inc(consts_pool, 1)
            nc.gpsimd.affine_select(out=band[:, :, :], in_=band[:, :, :], compare_op=ALU.is_ge, fill=NEG, base=8,
                                    pattern=[[0, QH], [-1, S]], channel_multiplier=1).then_inc(consts_pool, 1)
            nc.gpsimd.affine_select(out=head8[:, :, :], in_=head8[:, :, :], compare_op=ALU.is_ge, fill=0.0, base=0,
                                    pattern=[[-64, 2], [-16, 4]], channel_multiplier=1).then_inc(consts_pool, 1)
            pool.wait_ge(consts_pool, 8)
            nc.gpsimd.affine_select(out=band[:, :, :], in_=band[:, :, :], compare_op=ALU.is_ge, fill=NEG, base=8,
                                    pattern=[[0, QH], [1, S]], channel_multiplier=-1).then_inc(consts_pool, 1)
            nc.gpsimd.affine_select(out=head8[:, :, :], in_=head8[:, :, :], compare_op=ALU.is_ge, fill=0.0, base=15,
                                    pattern=[[64, 2], [16, 4]], channel_multiplier=-1).then_inc(consts_pool, 1)
            pool.wait_ge(consts_dve, 5)
            pool.wait_ge(small_loaded, 48)
            attn_pool(pool, A1, {})
            mix_pool(pool, M2)
            pool.wait_ge(stage_done, 2)
            ffn_pool(pool)
            pool.wait_ge(stage_done, 3)

            def split_a5():
                for k in range(2):
                    split_unit(pool, U_A5, k, cut(wA5, k * 768, 768), 768, nc.gpsimd)

            def split_e6():
                for k in range(2):
                    split_unit(pool, U_E6, k, cut(slots6[0], k * RAW, RAW), RAW, nc.gpsimd)

            attn_pool(pool, A4, {("q", 0): split_a5})
            pool.wait_ge(stage_done, 4)
            attn_pool(pool, A5, {("q", 0): split_e6})
            mix_pool(pool, M6)

        @block.tensor
        def _(pe):
            pe.wait_ge(consts_pool, 10)
            pe.wait_ge(consts_dve, 5)
            attn_tensor(pe, A1)
            pe.wait_ge(stage_done, 1)
            mix_tensor(pe, M2)
            pe.wait_ge(stage_done, 2)
            ffn_tensor(pe)
            pe.wait_ge(stage_done, 3)
            attn_tensor(pe, A4)
            pe.wait_ge(stage_done, 4)
            attn_tensor(pe, A5)
            pe.wait_ge(stage_done, 5)
            mix_tensor(pe, M6)

        @block.scalar
        def _(act):
            attn_scalar(act, A1)
            mix_scalar(act, M2)
            ffn_scalar(act)
            attn_scalar(act, A4)
            attn_scalar(act, A5)
            mix_scalar(act, M6)

        @block.vector
        def _(v):
            link = Link(v)
            nc.vector.memset(mhalf[:, :], -0.5).then_inc(consts_dve, 1)
            v.wait_ge(consts_pool, 10)
            nc.vector.tensor_copy(identb[:, :], ident[:, :]).then_inc(consts_dve, 1)
            nc.vector.tensor_tensor(head[:, :], head8[:, 0, :], head8[:, 1, :], ALU.add).then_inc(consts_dve, 1)
            v.wait_ge(small_loaded, 48)
            nc.vector.tensor_copy(rw_h[:, :], col_rw).then_inc(consts_dve, 1)
            v.wait_ge(consts_dve, 4)
            nc.vector.tensor_tensor(rw_l[:, :], col_rw, rw_h[:, :].bitcast(F32), ALU.subtract).then_inc(consts_dve, 1)

            def split_a1(k):
                split_unit(v, U_A1, k, cut(wA1, k * RAW, RAW), RAW)

            split_a1(0)
            split_a1(1)
            attn_vector(v, A1, link, {("q", 0): lambda: split_a1(2), ("q", 2): lambda: split_a1(3),
                                      ("q", 4): lambda: split_a1(4), ("q", 6): lambda: split_a1(5),
                                      ("k", 0): lambda: split_a1(6), ("k", 2): lambda: split_a1(7)})
            v.sem_inc(stage_done, 1)
            mix_vector(v, M2)
            v.sem_inc(stage_done, 1)
            ffn_vector(v, link)
            v.sem_inc(stage_done, 1)
            attn_vector(v, A4, link, {})
            v.sem_inc(stage_done, 1)
            attn_vector(v, A5, link, {})
            v.sem_inc(stage_done, 1)
            v.wait_ge(prep_done, U_PAIR6)
            mix_vector(v, M6)
            v.sem_inc(stage_done, 1)


def kernel(**inputs):
    import numpy as np
    import concourse.bacc as bacc
    from concourse import mybir as mb
    from concourse.bass_utils import run_bass_kernel_spmd as run

    a = {k: np.asarray(v) for k, v in inputs.items()}

    def chunked(w):
        k, n = w.shape
        return w.reshape(k // 128, 128, n).transpose(1, 0, 2).reshape(128, -1)

    def heads(w):
        return w.transpose(1, 0, 2).reshape(256, -1)

    def experts(w):
        return np.stack([chunked(e) for e in w])

    x = {}
    x["x"] = a["x"]
    x["ctxT"] = a["ctx_512"].transpose(2, 0, 1).reshape(128, -1)
    x["itokT"] = a["itok_BxS2xS_0_7"].transpose(2, 0, 1).reshape(128, -1)
    x["w_a1"] = np.concatenate([chunked(heads(a[f"L0_attn_W_{n}"])) for n in "QKV"]
                               + [chunked(a["L0_attn_W_O"].reshape(-1, 256))], 1)
    x["w_e1i"] = experts(a["L0_xattn_proj_in"].transpose(0, 2, 1))
    x["w_e1o"] = experts(a["L0_xattn_proj_out"].transpose(0, 2, 1))
    gu = [heads(a[f"L0_ffn_w{n}"]) for n in ("g_s", "g_r", "u_s", "u_r")]
    down = [a[f"L0_ffn_wd_{n}"].reshape(-1, 256) for n in "sr"]
    x["w_ffn"] = np.concatenate([chunked(np.concatenate(gu, 1)), chunked(np.concatenate(down, 0))], 1)
    x["w_a4"] = np.concatenate([chunked(a["L1_attn_Wqkv"]), chunked(a["L1_attn_Wproj"])], 1)
    x["w_a5"] = np.concatenate([chunked(a[f"L1_xattn_W{n}"]) for n in "qkvo"], 1)
    x["w_e6i"] = experts(a["L1_ffn_w1"])
    x["w_e6o"] = experts(a["L1_ffn_w2"])
    x["cols"] = np.concatenate([a["L0_attn_b_Q"].reshape(-1, 128).T, a["L0_attn_b_K"].reshape(-1, 128).T,
                                a["L1_xattn_bq"].reshape(-1, 128).T, a["L1_xattn_bk"].reshape(-1, 128).T,
                                a["L1_ffn_b1"].reshape(-1, 128).T, chunked(a["L0_ffn_router_w"]),
                                chunked(a["L1_ffn_gate_w"].T)], 1)
    x["rows"] = np.concatenate([a["L0_attn_b_O"], a["L1_attn_bproj"], a["L1_xattn_bv"], a["L1_xattn_bo"],
                                a["L1_ffn_gate_b"], a["L1_ffn_rms_w"]])
    x["bv"] = a["L0_attn_b_V"].reshape(-1)
    x["b2"] = a["L1_ffn_b2"].reshape(-1)
    nc = bacc.Bacc("TRN2", target_bir_lowering=False, num_devices=1)
    arrays, args = {}, []
    for name, v in x.items():
        v = np.ascontiguousarray(v)
        arrays[f"in_{name}"] = v
        args.append(nc.dram_tensor(f"in_{name}", v.shape, mb.dt.from_np(v.dtype), kind="ExternalInput").ap())
    args.append(nc.dram_tensor("out_0", (16, 128, 256), mb.dt.float32, kind="ExternalOutput").ap())
    program(nc, *args)
    r = run(nc, [arrays], core_ids=[0])
    return r.results[0]["out_0"]
```

```python
import concourse.bass as bass
from concourse import mybir

DT = mybir.dt
F32, F32R, BF16, I32 = DT.float32, DT.float32r, DT.bfloat16, DT.int32
ACT = mybir.ActivationFunctionType
ALU = mybir.AluOpType
AX = mybir.AxisListType

P = 128
B, S, D = 16, 128, 256
DC = D // P
GB = 4
NG = B // GB
GT = GB * S
H = 16
QH = 4
NQ = GB * H // QH
E_OUT, E_HID = 8, 512
HC = E_HID // P
R_N, R_MID, SH_HID = 16, 64, 256
FC = (SH_HID + R_N * R_MID) // P
SC = SH_HID // P
LN_EPS = 1e-5
NEG = -float(2 ** 30)
C1 = 1
RAW = 1024


class Region:

    def __init__(self, nc, start, size):
        self.nc, self.start, self.at, self.end = nc, start, start, start + size

    def place(self, name, shape, dt):
        size = 1
        for n in shape[1:]:
            size *= n
        size = (size * (2 if dt == BF16 else 4) + 31) // 32 * 32
        t = self.nc.alloc_sbuf_tensor_at(name, shape, dt, offset=self.at)
        self.at += size
        assert self.at <= self.end, (name, self.at - self.start)
        return t

    def again(self):
        return Region(self.nc, self.start, self.end - self.start)


class Stage:
    pass


class Attn:

    def __init__(self, tag, stage, hd, scale, mask, cross):
        self.tag, self.stage, self.hd, self.scale, self.mask, self.cross = tag, stage, hd, scale, mask, cross
        self.width = H * hd
        self.nch = self.width // P
        self.hpc = P // hd
        self.copies = self.hpc // 2
        self.vh = max(1, self.width // GT)
        self.vn = self.width // self.vh
        self.narrow = self.copies > 1
        self.nz = 0 if self.narrow else 2
        self.slots = 4 if self.narrow else 2
        self.zc = self.nch // max(1, self.nz)
        self.fg = DC + 2 * self.nch + GB * self.vh
        self.qk = DC + 2 * self.nch
        self.fe = GB * (self.nz + 1)
        self.links = (0 if self.narrow else NQ) + 2 * GB

    def q_at(self, ch):
        return 2 * ch + 1 if self.narrow else ch

    def k_at(self, ch):
        return 2 * ch if self.narrow else self.nch + ch

    def bank(self, n):
        if not self.narrow:
            return n % 2
        return (0, 1, 6)[n % 3 if n < NQ - 1 else 1]

    def before(self, n):
        if not self.narrow:
            return n - 2
        return {0: -4, 1: -1, 2: -2, NQ - 1: NQ - 3}.get(n, n - 3)

    def heads(self, q):
        g, half = divmod(q, 2)
        if self.copies == 1:
            return [(8 * g + 2 * i + half, 4 * g + i, half, 0) for i in range(QH)]
        return [(4 * q + i, g, half, i) for i in range(QH)]

    def of_quad(self, t, q):
        g, half = divmod(q, 2)
        if self.copies == 1:
            return t.rearrange("p (g i r e) -> p g r i e", g=2, i=QH, r=2)[:, g, half]
        return t.rearrange("p (g i e) -> p g i e", g=4, i=QH)[:, q]


def split3(nc, out, wh, wl, xh, xl, start, stop, **kw):
    nc.tensor.matmul(out, wh, xh, start=start, stop=False, **kw)
    nc.tensor.matmul(out, wh, xl, start=False, stop=False, **kw)
    return nc.tensor.matmul(out, wl, xh, start=False, stop=stop, **kw)


def program(nc, x_in, ctxT_in, itokT_in, w_a1, w_e1i, w_e1o, w_ffn, w_a4, w_a5, w_e6i, w_e6o,
            cols_in, rows_in, bv_in, b2_in, out):
    sem = nc.alloc_semaphore

    def signals(tag, names):
        return {n: sem(f"{tag}_{n}") for n in names.split()}

    base = (nc.sbuf_base + 31) // 32 * 32
    KB = 1024
    keep = Region(nc, base, 34 * KB)
    r3 = Region(nc, keep.end, 16 * KB)
    r1 = Region(nc, r3.end, 64 * KB)
    r2 = Region(nc, r1.end, nc.sbuf_usable_end - r1.end - 64)

    X = keep.place("X", [P, B, D], F32)
    raw = [keep.place(f"raw{i}", [P, RAW], F32) for i in range(2)]
    ident = keep.place("ident", [P, P], F32)
    identb = keep.place("identb", [P, P], BF16)
    causal = keep.place("causal", [P, QH, S], BF16)
    band = keep.place("band", [P, QH, S], BF16)
    rows = keep.place("rows", [P, 4 * D + 16], F32)
    cols = keep.place("cols", [P, 100], F32)
    gates = keep.place("gates", [P, B, E_OUT], F32)
    head8 = keep.place("head8", [P, 2, 4], F32)
    head = keep.place("head", [P, 4], F32)
    rw_h = keep.place("rw_h", [P, 48], F32R)
    rw_l = keep.place("rw_l", [P, 48], F32R)
    negm = keep.place("negm", [P, 4, QH], F32)
    rec = keep.place("rec", [P, QH], F32)
    stats = keep.place("stats", [P, B, 6], F32)
    mv = keep.place("mv", [P, B, 2], F32)
    veps = keep.place("veps", [P, B], F32)
    rstd = keep.place("rstd", [P, B], F32)
    mhalf = keep.place("mhalf", [P, B], F32)
    ng = keep.place("ng", [P, B], F32)

    row_bo1, row_bo4 = rows[:, 0:D], rows[:, D:2 * D]
    row_bv5, row_bo5 = rows[:, 2 * D:3 * D], rows[:, 3 * D:4 * D]
    row_gb, row_rms = rows[:, 4 * D:4 * D + 8], rows[:, 4 * D + 8:4 * D + 16]
    col_bq1, col_bk1, col_bq5, col_bk5 = cols[:, 0:8], cols[:, 8:16], cols[:, 16:18], cols[:, 18:20]
    col_b1, col_rw = cols[:, 20:52], cols[:, 52:100]

    ps = nc.alloc_psum_tensor("ps", [P, 8, GT], F32)

    def pair(region, name, shape):
        return region.place(name + "_h", shape, F32R), region.place(name + "_l", shape, F32R)

    wA1 = pair(r1, "wA1", [P, 8 * RAW])
    r1b = r1.again()
    FU = (2 * DC + 2) * FC * P // 8
    wF = pair(r1b, "wF", [P, 8 * FU])
    r1c = r1.again()
    wA5 = pair(r1c, "wA5", [P, 1536])
    slots6 = [pair(r1c, f"w6_{i}", [P, 2 * RAW]) for i in range(2)]
    KT45 = r1c.place("KT45", [P, 2, 4, GT], F32)
    V_ROW = 144 * QH
    V45_at = (r2.end - GB * (H // QH) * V_ROW * 4) // 32 * 32
    V45 = Region(nc, V45_at, r2.end - V45_at).place("V45", [P, GB, H // QH, V_ROW], F32)
    wA4 = pair(r3, "wA4", [P, 2048])
    r3a = r3.again()
    bv1 = r3a.place("bv1", [P, H * 64], F32)
    ctxg1 = r3a.place("ctxg1", [P, GB, S], F32)
    itokg = r3a.place("itokg", [P, GB, S], I32)
    junk = r3a.place("junk", [P, S], F32)
    r3b = r3.again()
    b2rows = r3b.place("b2rows", [P, E_OUT, D], F32)
    b2sum = r3b.place("b2sum", [P, D], F32)

    consts_pool = sem("consts_pool")
    consts_dve = sem("consts_dve")
    small_loaded = sem("small_loaded")
    x_loaded = sem("x_loaded")
    b2_loaded = sem("b2_loaded")
    v45_made = sem("v45_made")
    split_hi = sem("split_hi")
    raw_loaded = [sem("raw_loaded0"), sem("raw_loaded1")]
    prep_done = sem("prep_done")
    chain = sem("chain")
    waited_sp = sem("waited_sp")
    waited_pool = sem("waited_pool")
    waited = sem("waited")
    stage_done = sem("stage_done")
    out_stored = sem("out_stored")

    U_A1, U_E0 = 0, 8
    U_PAIR = 10
    U_A4 = U_PAIR + 6 * 4
    U_A5 = U_A4 + 4
    U_E6 = U_A5 + 2
    U_PAIR6 = U_E6 + 2

    def attn_setup(c):
        t = c.tag
        m = r2.again()
        if c.narrow:
            m.end = V45_at
        c.Xs = m.place(t + "Xs", [P, GB, D], F32)
        c.XB = m.place(t + "XB", [P, GB, D], F32)
        c.XT = pair(m, t + "XT", [P, DC, GT])
        c.QT = m.place(t + "QT", [P, c.nch, GT], F32)
        if c.narrow:
            c.KT, c.V = KT45, V45
            c.z = m.place(t + "z", [P, 2, c.nch, S], F32)
            c.rz = m.place(t + "rz", [P, 2, S], F32)
            c.sums = m.place(t + "sums", [P, 2, 2 * QH], F32)
            c.rec = m.place(t + "rec", [P, 2, 2 * QH], F32)
            c.recx = m.place(t + "recx", [P, 2, 2 * QH, c.hd], F32)
        else:
            c.KT = m.place(t + "KT", [P, c.nch, c.copies, GT], F32)
            c.V = m.place(t + "V", [P, GB, H, c.hd + 1], F32)
            c.z = m.place(t + "z", [P, 2, c.width], F32)
        c.Pr = m.place(t + "Pr", [P, c.slots, QH, S], F32)
        c.PT = m.place(t + "PT", [P, 2, QH, S], F32)
        c.zT = pair(m, t + "zT", [P, c.nch, S])
        c.r = m.place(t + "r", [P, 2, D], F32)
        if c.cross:
            c.ctxg = m.place(t + "ctxg", [P, GT], F32)
            c.CT = pair(m, t + "CT", [P, GT])
            c.bkm = m.place(t + "bkm", [P, c.nch, 4], F32)
        c.s = signals(t, "xs_loaded ctx_loaded xb_ready xt_hi ct_ready g_full g_evac s_full s_max p_ready pt_full "
                      "pt_ready z_full z_ready e_full e_hi e_evac ln_var rstd_ready x_done gates_done k_most bk_ready zt_ready rz_ready rec_ready recx_ready r_full ct_hi")

    A1 = Attn("a1", 1, 64, 1 / 8.0, causal, False)
    A4 = Attn("a4", 4, 16, 1 / 4.0, band, False)
    A5 = Attn("a5", 5, 16, 1 / 4.0, None, True)
    for c in (A1, A4, A5):
        attn_setup(c)
    def view(w, at, k, n):
        return [t[:, at:at + k * n].rearrange("p (k n) -> p k n", k=k) for t in w]
    A1.wq, A1.wk, A1.wv = (view(wA1, i * 2048, DC, 1024) for i in range(3))
    A1.wo = view(wA1, 3 * 2048, 8, D)
    qkv4 = view(wA4, 0, DC, 768)
    A4.wq, A4.wk, A4.wv = ([t[:, :, i * D:(i + 1) * D] for t in qkv4] for i in range(3))
    A4.wo = view(wA4, 1536, DC, D)
    A5.wq, A5.wk, A5.wv, A5.wo = view(wA5, 0, DC, D), view(wA5, 512, 1, D), view(wA5, 768, 1, D), view(wA5, 1024, DC, D)
    A1.bq, A1.bk, A1.bv, A1.bo = col_bq1, col_bk1, bv1[:, :], row_bo1
    A4.bq, A4.bk, A4.bv, A4.bo = None, None, None, row_bo4
    A5.bq, A5.bk, A5.bv, A5.bo = col_bq5, col_bk5, row_bv5, row_bo5
    A1.needs = {("q", 0): U_A1 + 2, ("k", 0): U_A1 + 4, ("v", 0): U_A1 + 6, ("o", 0): U_A1 + 8}
    A4.needs, A5.needs = {("k", 0): U_A5}, {("k", 0): U_E6}

    def attn_order(c, first, last):
        fills = [(kind, ch, 0) for kind in "qk" for ch in range(c.nch)]
        if c.narrow:
            fills = [(kind, ch, 0) for ch in range(c.nch) for kind in "kq"]
        fills += [("v", f, 0) for f in range(GB * c.vh)]

        def wide(n):
            steps = [("s", n), ("e", n)]
            if n >= 8 and n % 4 < 2:
                steps += [[("na", n // 4 - 2), ("ns", n // 4 - 2)], [("nb", n // 4 - 2)]][n % 4]
            steps += [("t", n - 1), ("pv", n - 2)]
            if n >= 6 and n % 4 >= 2:
                steps.append((("zt", "o")[n % 4 - 2], (n - 6) // 4))
            return steps

        def narrow(n):
            phase, b = n % 4, n // 4 - 2
            steps = [("z", (n - 5) // 2)] if n % 2 else []
            steps += [("zl", b)] if phase == 0 else []
            steps += [("s", n), ("t", n - 2)]
            steps += [("r", (n - 4) // 2)] if n % 2 == 0 else []
            steps += [("e", n), ("pv", n - 3)]
            steps += [[("o", b)], [("na", b), ("ns", b)], [("nb", b)], [("zh", b + 1)]][phase]
            of = {"s": NQ, "e": NQ, "t": NQ, "pv": NQ, "z": NQ // 2, "r": NQ // 2}
            return [(kind, i) for kind, i in steps if 0 <= i < of.get(kind, GB)]

        if c.narrow:
            tail = [narrow(n) for n in range(NQ, NQ + 7)]
            for n, b in ((0, 2), (4, 3)):
                tail[n].remove(("o", b))
                tail[n + 1].insert(0, ("o", b))
        else:
            tail = [[("t", NQ - 1)], [("na", 2), ("ns", 2), ("pv", NQ - 2)], [("nb", 2), ("pv", NQ - 1)], [("zt", 3)], [],
                    [("o", 3)], [("na", 3), ("ns", 3)], [("nb", 3)]]
        order = []
        s0 = len(fills) - 1 - 2 * c.vh
        for f in range(max(len(fills), len(tail))):
            if not last:
                order.append(fills[f])
            if not first and f < len(tail):
                order += [(kind, i, -1) for kind, i in tail[f]]
            if not last and f in (s0, s0 + c.vh):
                n = (f - s0) // c.vh
                order += [("s", n, 0), ("e", n, 0)]
        if last:
            return order
        if not c.narrow:
            order.append(("t", 0, 0))
        for n in range(2, NQ):
            order += [(kind, i, 0) for kind, i in (narrow if c.narrow else wide)(n)]
            when = (8, 9)
            if n in when:
                order.append(("x", when.index(n), 0))
        return order

    def attn_groups(eng, c, steps):
        steps(0, attn_order(c, True, False))
        with eng.Fori(1, NG) as g:
            steps(g, attn_order(c, False, False))
        steps(NG, attn_order(c, False, True))

    def attn_load_ctx(sp, g, to, done):
        sp.dma_start(to, ctxT_in[:, bass.ds(g * GT, GT)]).then_inc(done, 16)

    def attn_first_loads(sp, c):
        sp.dma_start(c.Xs[:, :, :], X[:, 0:GB, :]).then_inc(c.s["xs_loaded"], 16)

    def attn_sync(sp, c):
        def settle():
            sp.sem_inc(waited_sp, 1)

        with sp.Fori(0, NG) as g:
            if c is A1:
                sp.wait_ge(c.s["gates_done"], g * GB * E_OUT + C1)
                settle()
                attn_load_ctx(sp, g, ctxg1[:, :, :].rearrange("p b s -> p (b s)"), c.s["ctx_loaded"])
                sp.dma_start(itokg[:, :, :].rearrange("p b s -> p (b s)"),
                             itokT_in[:, bass.ds(g * GT, GT)]).then_inc(c.s["ctx_loaded"], 16)
            nxt = (g + 1) % NG
            if c.cross:
                sp.wait_ge(c.s["ct_ready"], g + 1 + C1)
                settle()
                attn_load_ctx(sp, nxt, c.ctxg[:, :], c.s["ctx_loaded"])
            sp.wait_ge(c.s["xt_hi"], g * DC + DC + C1)
            settle()
            sp.wait_ge(c.s["xb_ready"], g + 1 + C1)
            settle()
            sp.dma_start(c.Xs[:, :, :], X[:, bass.ds(nxt * GB, GB), :]).then_inc(c.s["xs_loaded"], 16)

    def attn_pool(pool, c, extra):
        pool.sem_inc(c.s["xb_ready"], C1)

        def context(n):
            pool.wait_ge(c.s["ctx_loaded"], n * 16)
            pool.sem_inc(waited_pool, 1)
            nc.gpsimd.tensor_copy(c.CT[0][:, :], c.ctxg[:, :]).then_inc(c.s["ct_hi"], 1)
            pool.wait_ge(c.s["ct_hi"], n)
            nc.gpsimd.tensor_tensor(c.CT[1][:, :], c.ctxg[:, :], c.CT[0][:, :].bitcast(F32),
                                    ALU.subtract).then_inc(c.s["ct_ready"], 1)

        def steps(g, order):
            for kind, b, back in order:
                if kind == "ns":
                    pool.wait_ge(c.s["ln_var"], (g + back) * GB + b + 1)
                    nc.gpsimd.tensor_tensor(rstd[:, b:b + 1], veps[:, b:b + 1], mhalf[:, b:b + 1],
                                            ALU.pow).then_inc(c.s["rstd_ready"], 1)
                if kind == "t" and c.narrow and b % 2:
                    pair = b // 2
                    pool.wait_ge(c.s["rec_ready"], (g + back) * (NQ // 2) + (pair + 1))
                    pool.sem_inc(waited_pool, 1)
                    nc.gpsimd.tensor_copy(c.recx[:, pair % 2, :, :], c.rec[:, pair % 2, :].unsqueeze(2).broadcast_to(
                        [P, 2 * QH, c.hd])).then_inc(c.s["recx_ready"], 1)
                if kind == "s" and b == 2:
                    pool.wait_ge(c.s["xs_loaded"], g * 16 + 16)
                    pool.wait_ge(c.s["x_done"], g * GB + C1)
                    nc.gpsimd.tensor_tensor(c.XB[:, :, :], c.Xs[:, :, :],
                                            c.bo.unsqueeze(1).broadcast_to([P, GB, D]), ALU.add).then_inc(c.s["xb_ready"], 1)
                    if c.cross:
                        pool.wait_ge(c.s["g_evac"], emptied(c, g, c.fg - DC))
                        context(g + 2)
                if type(g) is int and g == 0 and (kind, b) in extra:
                    extra[kind, b]()
        if c.cross:
            context(1)
            pool.wait_ge(stage_done, c.stage - 1)
        attn_groups(pool, c, steps)

    PTB, ZB, G0, E0, E1 = 2, 3, 4, 6, 7

    def filled(c, g, k):
        return g * c.fg + (DC + k + 1)

    def emptied(c, g, k):
        return g * c.fg + (DC + k + 2)

    def attn_tensor(pe, c):
        def g_fill(g, k):
            pe.wait_ge(c.s["g_evac"], emptied(c, g, k - 1))
            return ps[:, G0 + k % 2, :]

        def e_fill(g, k):
            pe.wait_ge(c.s["e_evac"], g * c.fe + (k + 1))
            return ps[:, E0 + k % 2, :]

        def transposed_x(g, n, k, chunks=range(DC)):
            src = c.Xs if k >= 0 else X
            if k >= 0:
                pe.wait_ge(c.s["xs_loaded"], n)
            for ch in chunks:
                bank = g_fill(g, k + ch)
                for j in range(GB):
                    last = nc.tensor.transpose(bank[:, j * S:(j + 1) * S], src[:, j, ch * P:(ch + 1) * P], ident[:, :])
                last.then_inc(c.s["g_full"], 1)

        xh, xl = [c.XT[0][:, i, :] for i in range(DC)], [c.XT[1][:, i, :] for i in range(DC)]
        kh, kl = ([c.CT[0][:, :]], [c.CT[1][:, :]]) if c.cross else (xh, xl)

        def project(g, k, w, ch, xh, xl):
            bank = g_fill(g, k)
            for i in range(len(xh)):
                last = split3(nc, bank, w[0][:, i, ch * P:(ch + 1) * P], w[1][:, i, ch * P:(ch + 1) * P],
                              xh[i], xl[i], i == 0, i == len(xh) - 1)
            last.then_inc(c.s["g_full"], 1)

        def project_v(g, f):
            b, w = divmod(f, c.vh)
            bank = g_fill(g, 2 * c.nch + f)
            cols_v = slice(w * c.vn, (w + 1) * c.vn)
            for i in range(len(kh)):
                last = split3(nc, bank[:, 0:c.vn], kh[i][:, b * S:(b + 1) * S], kl[i][:, b * S:(b + 1) * S],
                              c.wv[0][:, i, cols_v], c.wv[1][:, i, cols_v], i == 0, i == len(kh) - 1)
            last.then_inc(c.s["g_full"], 1)

        def scores(g, n):
            b, q = divmod(n, H // QH)
            if type(g) is not int or n >= c.slots or c.before(n) >= 0:
                pe.wait_ge(c.s["p_ready"], g * NQ + (c.before(n) + 3))
            if n == 0:
                pe.wait_ge(c.s["g_evac"], emptied(c, g, 2 * c.nch))
            if c is A1 and type(g) is int and n == 0:
                pe.wait_ge(consts_pool, 10)
                pe.wait_ge(consts_dve, 5)
            bank = ps[:, c.bank(n), :]
            if c.mask is not None:
                nc.tensor.matmul(bank, identb[:, :], c.mask[:, :, :].rearrange("p a b -> p (a b)"),
                                 start=True, stop=False)
            for i, (h, ch, half, j) in enumerate(c.heads(q)):
                rows64 = slice(64 * half, 64 * half + 64)
                last = nc.tensor.matmul(bank[:, i * S:(i + 1) * S], c.QT[rows64, ch, b * S:(b + 1) * S],
                                        c.KT[rows64, ch, j, b * S:(b + 1) * S],
                                        start=c.mask is None, stop=c.mask is None or i == QH - 1)
            last.then_inc(c.s["s_full"], 1)

        def transpose_p(g, n):
            pe.wait_ge(c.s["p_ready"], g * NQ + (n + 3))
            pe.wait_ge(c.s["pt_ready"], g * NQ + (n + C1))
            for i in range(QH):
                last = nc.tensor.transpose(ps[:, PTB, i * S:(i + 1) * S], c.Pr[:, n % c.slots, i, :], ident[:, :])
            last.then_inc(c.s["pt_full"], 1)

        def values(g, n):
            b, q = divmod(n, H // QH)
            pe.wait_ge(c.s["pt_ready"], g * NQ + (n + 1 + C1))
            if not c.narrow:
                pe.wait_ge(c.s["z_ready"], g * NQ + (n + C1))
            elif n % 2 == 0:
                pe.wait_ge(c.s["z_ready"], g * (NQ // 2) + (n // 2 + C1))
            if q == 0:
                pe.wait_ge(c.s["g_evac"], emptied(c, g, 2 * c.nch + (b + 1) * c.vh))
            if c.narrow:
                for i in range(QH):
                    last = nc.tensor.matmul(ps[:, ZB, 0:S], c.V[:, b, q, i * P:(i + 1) * P], c.PT[:, n % 2, i, :],
                                            start=n % 2 == 0 and i == 0, stop=n % 2 == 1 and i == QH - 1)
                if n % 2:
                    last.then_inc(c.s["z_full"], 1)
                return
            w = c.hd + 1
            for i, (h, _, _, _) in enumerate(c.heads(q)):
                last = nc.tensor.matmul(ps[:, ZB, i * w:(i + 1) * w], c.PT[:, n % 2, i, :],
                                        c.V[:, b, h, :], start=True, stop=True)
            last.then_inc(c.s["z_full"], 1)

        def transpose_r(g, p):
            pe.wait_ge(c.s["recx_ready"], g * (NQ // 2) + (p + 1))
            pe.wait_ge(c.s["rz_ready"], g * (NQ // 2) + (p + C1))
            pe.wait_ge(c.s["e_evac"], g * GB + (max(0, (p - 1) // 2) + 2))
            nc.tensor.transpose(ps[:, E1, 0:S], c.recx[:, p % 2, :, :].rearrange("p h e -> p (h e)"),
                                ident[:, :]).then_inc(c.s["r_full"], 1)

        def transpose_z(g, b):
            pe.wait_ge(c.s["z_ready"], g * NQ + ((b + 1) * (H // QH) + C1))
            for f in range(c.nz):
                bank = e_fill(g, b * (c.nz + 1) + f)
                for i in range(c.zc):
                    ch = f * c.zc + i
                    last = nc.tensor.transpose(bank[:, i * S:(i + 1) * S], c.z[:, b % 2, ch * P:(ch + 1) * P],
                                               ident[:, :])
                last.then_inc(c.s["e_full"], 1)

        def out_project(g, b):
            k = b * (c.nz + 1) + c.nz
            if c.narrow:
                bank = ps[:, E1, :]
                pe.wait_ge(c.s["rz_ready"], g * (NQ // 2) + (min(NQ // 2, 2 * b + 3) + C1))
                pe.wait_ge(c.s["e_evac"], g * GB + (b + 2))
                pe.wait_ge(c.s["zt_ready"], g * GB + (b + 1 + C1))
            else:
                bank = e_fill(g, k)
                pe.wait_ge(c.s["e_evac"], g * c.fe + (k + 2))
            for ch in range(c.nch):
                last = split3(nc, bank[:, 0:D], c.zT[0][:, ch, :], c.zT[1][:, ch, :],
                              c.wo[0][:, ch, :], c.wo[1][:, ch, :], ch == 0, ch == c.nch - 1)
            last.then_inc(c.s["e_full"], 1)

        def steps(g, order):
            for kind, i, back in order:
                if type(g) is int and g == 0 and (kind, i) in c.needs:
                    pe.wait_ge(prep_done, c.needs[kind, i])
                if kind == "q":
                    if i == 0:
                        pe.wait_ge(c.s["g_evac"], emptied(c, g, 0))
                    project(g, c.q_at(i), c.wq, i, xh, xl)
                elif kind == "k":
                    if i == 0 and c.cross:
                        pe.wait_ge(c.s["ct_ready"], g + 1 + C1)
                    elif i == 0 and c.narrow:
                        pe.wait_ge(c.s["g_evac"], emptied(c, g, 0))
                    project(g, c.k_at(i), c.wk, i, kh, kl)
                elif kind == "v":
                    project_v(g, i)
                elif kind == "s":
                    scores(g, i)
                elif kind == "t":
                    transpose_p(g + back, i)
                elif kind == "pv":
                    values(g + back, i)
                elif kind == "r":
                    transpose_r(g + back, i)
                elif kind == "zt":
                    transpose_z(g + back, i)
                elif kind == "o":
                    out_project(g + back, i)
                elif kind == "x":
                    transposed_x(g, g * 16 + 32, c.fg - DC, [i])

        transposed_x(0, 16, -DC)
        attn_groups(pe, c, steps)

    def attn_scalar(act, c):
        act.sem_inc(c.s["p_ready"], 2)
        act.sem_inc(c.s["xt_hi"], C1)

        def transposed_x(g, k, chunks=range(DC)):
            for ch in chunks:
                act.wait_ge(c.s["g_full"], filled(c, g, k + ch))
                nc.scalar.activation(c.XT[0][:, ch, :], ps[:, G0 + ch % 2, :], ACT.Identity).then_inc(c.s["xt_hi"], 1)

        def steps(g, order):
            for kind, i, back in order:
                if kind == "e":
                    act.wait_ge(c.s["s_max"], g * NQ + (i + 1))
                    for j in range(QH):
                        kw = {"accum_out": c.sums[:, i // 2 % 2, i % 2 * QH + j:i % 2 * QH + j + 1]} if c.narrow else {}
                        last = nc.scalar.activation(c.Pr[:, i % c.slots, j, :], ps[:, c.bank(i), j * S:(j + 1) * S], ACT.Exp,
                                                    bias=negm[:, i % c.slots, j:j + 1], **kw)
                    last.then_inc(c.s["p_ready"], 1)
                elif kind == "k" and c.copies > 1:
                    k = c.k_at(i)
                    act.wait_ge(c.s["g_full"], filled(c, g, k))
                    for j in range(c.copies - 1):
                        bias = 0.0 if c.bk is None else c.bkm[:, i, j:j + 1]
                        last = nc.scalar.activation(c.KT[:, i, j, :], ps[:, G0 + k % 2, :], ACT.Identity,
                                                    bias=bias, scale=head[:, j:j + 1])
                    last.then_inc(c.s["k_most"], 1)
                elif kind == "zh":
                    act.wait_ge(c.s["z_ready"], (g + back) * (NQ // 2) + ((i + 1) * 2 + C1))
                    if type(g) is not int or g + back > 0 or i > 0:
                        act.wait_ge(c.s["e_full"], (g + back) * GB + i)
                    nc.scalar.activation(c.zT[0][:, :, :], c.z[:, i % 2, :, :], ACT.Identity).then_inc(c.s["e_hi"], 1)
                elif kind == "zt":
                    for f in range(c.nz):
                        k = i * (c.nz + 1) + f
                        act.wait_ge(c.s["e_full"], (g + back) * c.fe + (k + 1))
                        nc.scalar.activation(c.zT[0][:, f * c.zc:(f + 1) * c.zc, :].rearrange("p a b -> p (a b)"),
                                             ps[:, E0 + k % 2, 0:c.zc * S], ACT.Identity).then_inc(c.s["e_hi"], 1)
                elif kind == "r":
                    act.wait_ge(c.s["r_full"], (g + back) * (NQ // 2) + (i + 1))
                    nc.scalar.activation(c.rz[:, i % 2, :], ps[:, E1, 0:S], ACT.Identity).then_inc(c.s["rz_ready"], 1)
                elif kind == "x":
                    transposed_x(g, c.fg - DC, [i])

        if c.cross:
            act.wait_ge(c.s["bk_ready"], 1)
        transposed_x(0, -DC)
        attn_groups(act, c, steps)

    def attn_vector_start(v, c):
        v.sem_inc(c.s["g_evac"], 2)
        v.sem_inc(c.s["e_evac"], 2)
        for first in ("ct_ready", "gates_done", "x_done", "pt_ready", "z_ready", "zt_ready", "rz_ready"):
            v.sem_inc(c.s[first], C1)
        if c.narrow:
            v.wait_ge(v45_made, 1)
        else:
            nc.vector.memset(c.V[:, :, :, c.hd:c.hd + 1], 1.0)
        if c.cross:
            nc.vector.tensor_tensor(c.bkm[:, :, :], c.bk.unsqueeze(2).broadcast_to([P, c.nch, 4]),
                                    head[:, :].unsqueeze(1).broadcast_to([P, c.nch, 4]), ALU.mult).then_inc(c.s["bk_ready"], 1)

        for ch in range(DC):
            attn_transposed_x(v, c, 1, ch)

    def attn_transposed_x(v, c, n, ch):
        v.wait_ge(c.s["xt_hi"], n * DC + (ch + 1 + C1 - DC))
        nc.vector.tensor_tensor(c.XT[1][:, ch, :], ps[:, G0 + ch % 2, :], c.XT[0][:, ch, :].bitcast(F32),
                                ALU.subtract).then_inc(c.s["g_evac"], 1)

    def attn_vector(v, c, link, extra, following=None):
        def lo(hi, low, psum, done):
            nc.vector.tensor_tensor(low, psum, hi.bitcast(F32), ALU.subtract).then_inc(done, 1)

        def query(g, ch):
            k = c.q_at(ch)
            v.wait_ge(c.s["g_full"], filled(c, g, k))
            if c.bq is None:
                last = nc.vector.tensor_scalar(c.QT[:, ch, :], ps[:, G0 + k % 2, :], c.scale, None, ALU.mult)
            else:
                last = nc.vector.tensor_scalar(c.QT[:, ch, :], ps[:, G0 + k % 2, :], c.bq[:, ch:ch + 1], c.scale,
                                               ALU.add, ALU.mult)
            last.then_inc(c.s["g_evac"], 1)

        def key(g, ch):
            k = c.k_at(ch)
            src = ps[:, G0 + k % 2, :]
            v.wait_ge(c.s["g_full"], filled(c, g, k))
            if c.copies == 1:
                last = nc.vector.tensor_scalar(c.KT[:, ch, 0, :], src, c.bk[:, ch:ch + 1], None, ALU.add)
            else:
                j = c.copies - 1
                v.wait_ge(c.s["k_most"], g * c.nch + (ch + 1))
                if c.bk is None:
                    last = nc.vector.tensor_scalar(c.KT[:, ch, j, :], src, head[:, j:j + 1], None, ALU.mult)
                else:
                    last = nc.vector.tensor_scalar(c.KT[:, ch, j, :], src, c.bk[:, ch:ch + 1],
                                                   head[:, j:j + 1], ALU.add, ALU.mult)
            last.then_inc(c.s["g_evac"], 1)

        def value(g, f):
            b, w = divmod(f, c.vh)
            k = 2 * c.nch + f
            hv = c.vn // c.hd
            v.wait_ge(c.s["g_full"], filled(c, g, k))
            if c.narrow:
                for half in range(2):
                    def of_half(t, n):
                        return t.rearrange("p (g r i e) -> p g r i e", g=2, r=2, i=QH)[:, :, half, :, n]
                    dst = of_half(c.V[:, b, :, :].rearrange("p q w -> p (q w)"), slice(64 * half, 64 * half + c.hd))
                    src = of_half(ps[:, G0 + k % 2, 0:c.vn], slice(0, c.hd))
                    if c.bv is None:
                        last = nc.vector.tensor_copy(dst, src)
                    else:
                        last = nc.vector.tensor_tensor(dst, src, of_half(c.bv, slice(0, c.hd)), ALU.add)
                last.then_inc(c.s["g_evac"], 1)
                return
            dst = c.V[:, b, w * hv:(w + 1) * hv, 0:c.hd]
            src = ps[:, G0 + k % 2, 0:c.vn].rearrange("p (h e) -> p h e", h=hv)
            if c.bv is None:
                last = nc.vector.tensor_copy(dst, src)
            else:
                bias = c.bv[:, w * c.vn:(w + 1) * c.vn].rearrange("p (h e) -> p h e", h=hv)
                last = nc.vector.tensor_tensor(dst, src, bias, ALU.add)
            last.then_inc(c.s["g_evac"], 1)

        def maxima(g, n):
            v.wait_ge(c.s["s_full"], g * NQ + (n + 1))
            nc.vector.reduce_max(negm[:, n % c.slots, :], ps[:, c.bank(n), :].rearrange("p (h k) -> p h k", h=QH), AX.X,
                                 negate=True).then_inc(c.s["s_max"], 1)

        def gates_of(g, n):
            b = n // 4
            if n == 0:
                v.wait_ge(c.s["ctx_loaded"], g * 32 + 32)
            for e in range(2 * (n % 4), 2 * (n % 4) + 2):
                nc.vector.scalar_tensor_tensor(junk[:, :], itokg[:, b, :], float(e), ctxg1[:, b, :], ALU.is_equal,
                                               ALU.mult, accum_out=gates[:, g * GB + b, e:e + 1]).then_inc(c.s["gates_done"], 1)
                v.wait_ge(c.s["gates_done"], g * (GB * E_OUT) + (b * E_OUT + e + 1 + C1))

        def normalised_pair(g, p):
            v.wait_ge(c.s["rz_ready"], g * (NQ // 2) + (p + 1 + C1))
            v.wait_ge(c.s["z_full"], g * (NQ // 2) + (p + 1))
            nc.vector.tensor_tensor(c.z[:, p // 2 % 2, p % 2, :], ps[:, ZB, 0:S], c.rz[:, p % 2, :],
                                    ALU.mult).then_inc(c.s["z_ready"], 1)

        def head_outputs(g, n):
            q = n % (H // QH)
            w = c.hd + 1
            zz = ps[:, ZB, 0:QH * w].rearrange("p (h e) -> p h e", h=QH)
            v.wait_ge(c.s["z_full"], g * NQ + (n + 1))
            link(nc.vector.reciprocal(rec[:, :].unsqueeze(2), zz[:, :, c.hd:w]))
            nc.vector.tensor_tensor(c.of_quad(c.z[:, n // 4 % 2, :], q), zz[:, :, 0:c.hd],
                                    rec[:, :].unsqueeze(2).broadcast_to([P, QH, c.hd]), ALU.mult).then_inc(c.s["z_ready"], 1)

        def norm_a(g, b):
            k = b * (c.nz + 1) + c.nz
            v.wait_ge(c.s["e_full"], g * c.fe + (k + 1))
            if b == 0:
                v.wait_ge(c.s["xb_ready"], g + 1 + C1)
            nc.vector.tensor_tensor(c.r[:, b % 2, :], ps[:, E1 if c.narrow else E0 + k % 2, 0:D], c.XB[:, b, :], ALU.add).then_inc(c.s["e_evac"], 1)

        def norm_stats(g, b):
            v.wait_ge(c.s["e_evac"], g * c.fe + (b * (c.nz + 1) + c.nz + 3))
            link(nc.vector.bn_stats(stats[:, b, :], c.r[:, b % 2, :]), alone=True)
            link(nc.vector.bn_aggr(mv[:, b, :], stats[:, b, :]))
            nc.vector.tensor_scalar(veps[:, b:b + 1], mv[:, b, 1:2], LN_EPS, None, ALU.add).then_inc(c.s["ln_var"], 1)

        def norm_b(g, b):
            v.wait_ge(c.s["rstd_ready"], g * GB + (b + 1))
            nc.vector.tensor_scalar(X[:, g * GB + b, :], c.r[:, b % 2, :], mv[:, b, 0:1], rstd[:, b:b + 1],
                                    ALU.subtract, ALU.mult).then_inc(c.s["x_done"], 1)
            v.wait_ge(c.s["x_done"], g * GB + (b + 1 + C1))

        def steps(g, order):
            if type(g) is not int:
                link.begin(g, 1, c.links)
            for kind, i, back in order:
                if kind == "q":
                    query(g, i)
                elif kind == "k":
                    key(g, i)
                elif kind == "v":
                    value(g, i)
                elif kind == "s":
                    maxima(g, i)
                    if c is A1:
                        gates_of(g, i)
                elif kind == "t":
                    v.wait_ge(c.s["pt_full"], (g + back) * NQ + (i + 1))
                    if c.narrow and i % 2:
                        pair = i // 2 % 2
                        nc.vector.reciprocal(c.rec[:, pair, :], c.sums[:, pair, :]).then_inc(c.s["rec_ready"], 1)
                    nc.vector.tensor_copy(c.PT[:, i % 2, :, :].rearrange("p a b -> p (a b)"), ps[:, PTB, :]).then_inc(c.s["pt_ready"], 1)
                elif kind == "pv" and not c.narrow:
                    head_outputs(g + back, i)
                elif kind == "z":
                    normalised_pair(g + back, i)
                elif kind == "zl":
                    v.wait_ge(c.s["e_hi"], (g + back) * GB + (i + 1))
                    nc.vector.tensor_tensor(c.zT[1][:, :, :], c.z[:, i % 2, :, :], c.zT[0][:, :, :].bitcast(F32),
                                            ALU.subtract).then_inc(c.s["zt_ready"], 1)
                    v.wait_ge(c.s["zt_ready"], (g + back) * GB + (i + 1 + C1))
                elif kind == "zt":
                    for f in range(c.nz):
                        k = i * (c.nz + 1) + f
                        v.wait_ge(c.s["e_hi"], (g + back) * (GB * c.nz) + (i * c.nz + f + 1))
                        part = slice(f * c.zc, (f + 1) * c.zc)
                        lo(c.zT[0][:, part, :].rearrange("p a b -> p (a b)"), c.zT[1][:, part, :].rearrange("p a b -> p (a b)"),
                           ps[:, E0 + k % 2, 0:c.zc * S], c.s["e_evac"])
                elif kind == "na":
                    norm_a(g + back, i)
                elif kind == "ns":
                    norm_stats(g + back, i)
                elif kind == "nb":
                    norm_b(g + back, i)
                elif kind == "x":
                    attn_transposed_x(v, c, g + 2, i)
                if type(g) is int and g == 0 and (kind, i) in extra:
                    extra[kind, i]()
                if type(g) is int and g == NG and (kind, i) == ("ns", GB - 1) and following:
                    following()
            if type(g) is not int:
                link.end(NG)

        attn_groups(v, c, steps)

    NU = 2 * NG * HC
    NG_STEPS = 8

    def mix_setup(tag, gelu, win, wout, first, pair0, per):
        c = Stage()
        c.gelu, c.win, c.wout = gelu, win, wout
        c.first, c.pair0, c.per = first, pair0, per
        m = r2.again()
        c.XT = pair(m, tag + "XT", [P, DC, B * S])
        if gelu:
            m.at += 16 * KB
        c.hT = pair(m, tag + "hT", [P, HC, GT])
        if gelu:
            c.slots = slots6
            c.h32 = m.place(tag + "h32", [P, 2, GT], F32)
            c.lg = m.place(tag + "lg", [P, B, E_OUT], F32)
            c.ex = m.place(tag + "ex", [P, B, E_OUT], F32)
            c.t1 = m.place(tag + "t1", [P, B], F32)
            c.t2 = m.place(tag + "t2", [P, B], F32)
            c.b1 = m.place(tag + "b1", [P, 2, HC], F32)
        else:
            c.slots = [pair(m, f"{tag}w{i}", [P, 2 * RAW]) for i in range(2)]
        c.end = m.at
        c.s = signals(tag, "g_full xt_hi g_evac u_full hi_ready lo_ready d_full comb_done ln_var rstd_ready x_done "
                           "logits ex_ready step b1_ready")
        return c

    M2 = mix_setup("m2", False, w_e1i, w_e1o, U_E0, U_PAIR, 6)
    M6 = mix_setup("m6", True, w_e6i, w_e6o, U_E6, U_PAIR6, 4)

    def load_unit(sp, base, k, src, ncols):
        sp.wait_ge(prep_done, base + (k - 1))
        sp.dma_start(raw[k % 2][:, 0:ncols], src).then_inc(raw_loaded[k % 2], 16)

    def split_unit(v, base, k, w, ncols, on=nc.vector):
        v.wait_ge(raw_loaded[k % 2], (base + (k - k % 2)) * 8 + 16)
        on.tensor_scalar(w[0], raw[k % 2][:, 0:ncols], 1.0, None, ALU.mult).then_inc(split_hi, 1)
        v.wait_ge(split_hi, base + (k + 1))
        on.tensor_tensor(w[1], raw[k % 2][:, 0:ncols], w[0].bitcast(F32), ALU.subtract).then_inc(prep_done, 1)

    def cut(w, at, n):
        return [t[:, at:at + n] for t in w]

    def mix_sync(sp, c):
        with sp.Fori(0, E_OUT // 2) as i:
            base = i * c.per + c.pair0
            odd, even = i * 2 + 1, (i * 2 + 2) % E_OUT
            load_unit(sp, base, 0, c.win[bass.ds(odd, 1)].rearrange("a p n -> (a p) n"), RAW)
            load_unit(sp, base, 1, c.wout[bass.ds(odd, 1)].rearrange("a p n -> (a p) n"), RAW)
            if not c.gelu:
                for k in range(2):
                    load_unit(sp, base, 2 + k, w_ffn[:, bass.ds(i * (2 * FU) + k * FU, FU)], FU)
            load_unit(sp, base, c.per - 2, c.win[bass.ds(even, 1)].rearrange("a p n -> (a p) n"), RAW)
            load_unit(sp, base, c.per - 1, c.wout[bass.ds(even, 1)].rearrange("a p n -> (a p) n"), RAW)

    def mix_order(c):
        if c.gelu:
            start = [("x", k) for k in range(4)]
        else:
            start = [("w", 0)] + [("x", k) for k in range(4)] + [("w", 1)]
        start += [("u", 0), ("x", 4), ("x", 5), ("u", 1), ("x", 6), ("x", 7)]
        for u in range(2, NU + 2):
            start += [("u", u)] if u < NU else []
            start.append(("d", u - 2))
            if c.gelu:
                start += {2: [("l", 0)], 3: [("g", 0)], 5: [("g", 1)], 6: [("e", 0)], 7: [("g", 2)]}.get(u, [])
            if u < NU and u % HC == 2 and u >= HC + 2 and u != HC + 2:
                start.append(("c", u // HC - 1))
            elif u == 2 * HC:
                start.append(("c", 0))
        return start + [("c", 2 * NG - 1)]

    def mix_tensor(pe, c):
        def transposed_x(k):
            g, ch = divmod(k, DC)
            if c.gelu and ch == 0:
                pe.wait_ge(A5.s["x_done"], (g + 1) * GB + C1)
            pe.wait_ge(c.s["g_evac"], k + 1)
            for j in range(GB):
                last = nc.tensor.transpose(ps[:, 4 + k % 2, j * S:(j + 1) * S], X[:, g * GB + j, ch * P:(ch + 1) * P], ident[:, :])
            last.then_inc(c.s["g_full"], 1)

        def logits():
            rh, rl = (t[:, 32:48].rearrange("p (k n) -> p k n", k=DC) for t in (rw_h, rw_l))
            pe.wait_ge(c.s["g_evac"], NG * DC + 2)
            for t in range(B):
                for i in range(DC):
                    last = split3(nc, ps[:, 4, t * 8:(t + 1) * 8], c.XT[0][:, i, t * S:(t + 1) * S],
                                  c.XT[1][:, i, t * S:(t + 1) * S], rh[:, i, :], rl[:, i, :], i == 0, i == DC - 1)
            last.then_inc(c.s["logits"], 1)

        def up(i, u):
            e2, r = divmod(u, NG * HC)
            g, ch = divmod(r, HC)
            first = type(i) is int
            if first and ch == 0 and e2 == 0:
                pe.wait_ge(c.s["g_evac"], (g + 1) * DC + 2)
            if first and u == 0:
                pe.wait_ge(prep_done, c.first + 1)
            elif r == 0:
                pe.wait_ge(prep_done, i * c.per + (c.pair0 + 2 * e2))
            wh, wl = (t[:, 0:RAW].rearrange("p (k n) -> p k n", k=DC) for t in c.slots[e2])
            pe.wait_ge(c.s["lo_ready"], i * NU + u + 1)
            for k in range(DC):
                last = split3(nc, ps[:, u % 2, :], wh[:, k, ch * P:(ch + 1) * P], wl[:, k, ch * P:(ch + 1) * P],
                              c.XT[0][:, k, g * GT:(g + 1) * GT], c.XT[1][:, k, g * GT:(g + 1) * GT], k == 0, k == DC - 1)
            last.then_inc(c.s["u_full"], 1)

        def down(i, u):
            e2 = u // (NG * HC)
            q, ch = divmod(u, HC)
            if type(i) is int and u == 0:
                pe.wait_ge(prep_done, c.pair0)
            pe.wait_ge(c.s["lo_ready"], i * NU + u + 3)
            if ch == 0:
                pe.wait_ge(c.s["comb_done"], i * (2 * B) + GB * (q + 1))
            wh, wl = (t[:, RAW:2 * RAW].rearrange("p (k n) -> p k n", k=HC) for t in c.slots[e2])
            for j in range(GB):
                acc = ps[:, (2, 6)[q % 2] + j // 2, (j % 2) * D:(j % 2 + 1) * D]
                last = split3(nc, acc, c.hT[0][:, ch, j * S:(j + 1) * S], c.hT[1][:, ch, j * S:(j + 1) * S],
                              wh[:, ch, :], wl[:, ch, :], ch == 0 and j % 2 == 0, ch == HC - 1 and j % 2 == 1,
                              skip_group_check=True)
            if ch == HC - 1:
                last.then_inc(c.s["d_full"], 1)

        for kind, k in mix_order(c):
            if kind == "x":
                transposed_x(k)
            elif kind == "u":
                up(0, k)
            elif kind == "d":
                down(0, k)
            elif kind == "l":
                logits()
        with pe.Fori(1, E_OUT // 2) as i:
            for u in range(NU + 2):
                if u < NU:
                    up(i, u)
                if u >= 2:
                    down(i, u - 2)

    def mix_scalar(act, c):
        def hidden(i, u):
            e2, ch = u // (NG * HC), u % HC
            if c.gelu and u == 0:
                act.wait_ge(c.s["b1_ready"], i + 1)
            act.wait_ge(c.s["u_full"], i * NU + u + 1)
            if c.gelu:
                bias = c.b1[:, e2, ch:ch + 1]
                nc.scalar.activation(c.h32[:, u % 2, :], ps[:, u % 2, :], ACT.Gelu, bias=bias)
                nc.scalar.activation(c.hT[0][:, ch, :], ps[:, u % 2, :], ACT.Gelu, bias=bias).then_inc(c.s["hi_ready"], 1)
            else:
                nc.scalar.activation(c.hT[0][:, ch, :], ps[:, u % 2, :], ACT.Relu).then_inc(c.s["hi_ready"], 1)

        for kind, k in mix_order(c):
            if kind == "x":
                g, ch = divmod(k, DC)
                act.wait_ge(c.s["g_full"], k + 1)
                nc.scalar.activation(c.XT[0][:, ch, g * GT:(g + 1) * GT], ps[:, 4 + k % 2, :], ACT.Identity).then_inc(c.s["xt_hi"], 1)
            elif kind == "u":
                hidden(0, k)
            elif kind == "e":
                act.wait_ge(c.s["step"], NG_STEPS)
                nc.scalar.activation(c.ex[:, :, :], c.lg[:, :, :], ACT.Exp, scale=2.0).then_inc(c.s["ex_ready"], 1)
        with act.Fori(1, E_OUT // 2) as i:
            for u in range(NU):
                hidden(i, u)

    def mix_pool(pool, c):
        if c.gelu:
            pool.wait_ge(c.s["step"], 4)
            nc.gpsimd.tensor_tensor(c.t2[:, :], c.t1[:, :], mhalf[:, :], ALU.pow).then_inc(c.s["rstd_ready"], 1)
        for g in range(NG):
            own = slice(g * GB, (g + 1) * GB)
            pool.wait_ge(c.s["ln_var"], g + 1)
            nc.gpsimd.tensor_tensor(rstd[:, own], veps[:, own], mhalf[:, own], ALU.pow).then_inc(c.s["rstd_ready"], 1)

    def gate_scale(v, c, n, part):
        def step(ins):
            n[0] += 1
            ins.then_inc(c.s["step"], 1)
            v.wait_ge(c.s["step"], n[0])

        def over(t):
            return t[:, :].unsqueeze(2).broadcast_to([P, B, E_OUT])

        def across(row):
            return row.unsqueeze(1).broadcast_to([P, B, row.shape[1]])
        if part == 0:
            v.wait_ge(c.s["logits"], 1)
            step(nc.vector.tensor_tensor(c.lg[:, :, :], ps[:, 4, 0:B * E_OUT].rearrange("p (b e) -> p b e", b=B), across(row_gb), ALU.add))
            step(nc.vector.tensor_tensor(c.ex[:, :, :], c.lg[:, :, :], c.lg[:, :, :], ALU.mult))
            step(nc.vector.reduce_sum(c.t1[:, :], c.ex[:, :, :], AX.X))
            step(nc.vector.tensor_scalar(c.t1[:, :], c.t1[:, :], 1.0 / E_OUT, 2.0 ** -23, ALU.mult, ALU.add))
        elif part == 1:
            v.wait_ge(c.s["rstd_ready"], 1)
            step(nc.vector.tensor_tensor(c.lg[:, :, :], c.lg[:, :, :], over(c.t2), ALU.mult))
            step(nc.vector.tensor_tensor(c.lg[:, :, :], c.lg[:, :, :], across(row_rms), ALU.mult))
            step(nc.vector.reduce_max(c.t1[:, :], c.lg[:, :, :], AX.X))
            step(nc.vector.tensor_tensor(c.lg[:, :, :], c.lg[:, :, :], over(c.t1), ALU.subtract))
            assert n[0] == NG_STEPS
        else:
            v.wait_ge(c.s["ex_ready"], 1)
            step(nc.vector.reduce_sum(c.t1[:, :], c.ex[:, :, :], AX.X))
            step(nc.vector.reciprocal(c.t2[:, :], c.t1[:, :]))
            step(nc.vector.tensor_scalar(c.t1[:, :], c.t2[:, :], 1e-6, None, ALU.add))
            step(nc.vector.reciprocal(c.t1[:, :], c.t1[:, :]))
            step(nc.vector.tensor_tensor(ng[:, :], c.t1[:, :], c.t2[:, :], ALU.mult))
            v.wait_ge(b2_loaded, 16)
            step(nc.vector.reduce_sum(b2sum[:, :], b2rows[:, :, :].rearrange("p e d -> p d e"), AX.X))

    def mix_vector_start(v, c):
        v.sem_inc(c.s["g_evac"], 2)
        v.sem_inc(c.s["lo_ready"], 2)
        v.sem_inc(c.s["comb_done"], 2 * GB)

        mix_biases(c, 0)
        for k in range(4 if c.gelu else 0):
            mix_transposed_x(v, c, k)

    def mix_transposed_x(v, c, k):
        g, ch = divmod(k, DC)
        tok = slice(g * GT, (g + 1) * GT)
        v.wait_ge(c.s["xt_hi"], k + 1)
        nc.vector.tensor_tensor(c.XT[1][:, ch, tok], ps[:, 4 + k % 2, :], c.XT[0][:, ch, tok].bitcast(F32),
                                ALU.subtract).then_inc(c.s["g_evac"], 1)

    def mix_biases(c, i):
        if c.gelu:
            nc.vector.tensor_scalar(c.b1[:, :, :].rearrange("p a b -> p (a b)"), col_b1[:, bass.ds(i * (2 * HC), 2 * HC)],
                                    1.0, None, ALU.mult).then_inc(c.s["b1_ready"], 1)

    def mix_vector(v, c, beside=None, following=None):
        n = [0]

        def hidden(i, u):
            ch = u % HC
            v.wait_ge(c.s["hi_ready"], i * NU + u + 1)
            if c.gelu:
                last = nc.vector.tensor_tensor(c.hT[1][:, ch, :], c.h32[:, u % 2, :], c.hT[0][:, ch, :].bitcast(F32), ALU.subtract)
            else:
                last = nc.vector.scalar_tensor_tensor(c.hT[1][:, ch, :], ps[:, u % 2, :], 0.0,
                                                      c.hT[0][:, ch, :].bitcast(F32), ALU.max, ALU.subtract)
            last.then_inc(c.s["lo_ready"], 1)

        def combine(i, q):
            e2, g = divmod(q, NG)
            if c.gelu and type(i) is int and i + e2 == 0:
                for t in range(g * GB, (g + 1) * GB):
                    n[0] += 1
                    nc.vector.scalar_tensor_tensor(X[:, t, :], b2sum[:, :], ng[:, t:t + 1], X[:, t, :], ALU.mult, ALU.add).then_inc(c.s["step"], 1)
                v.wait_ge(c.s["step"], n[0])
            v.wait_ge(c.s["d_full"], i * (2 * NG) + q + 1)
            for j in range(GB):
                t = g * GB + j
                gate = ng[:, t:t + 1] if c.gelu else gates[:, t, bass.ds(i * 2 + e2, 1)]
                acc = ps[:, (2, 6)[q % 2] + j // 2, (j % 2) * D:(j % 2 + 1) * D]
                nc.vector.scalar_tensor_tensor(X[:, t, :], acc, gate, X[:, t, :], ALU.mult, ALU.add).then_inc(c.s["comb_done"], 1)

        def weights(i, u):
            base = i * c.per + c.pair0
            if u in (3, 5):
                k = (u - 3) // 2
                split_unit(v, base, k, cut(c.slots[1], k * RAW, RAW), RAW)
            if u in (8, 12) and not c.gelu:
                k = (u - 8) // 4
                split_unit(v, base, 2 + k, [t[:, bass.ds(i * (2 * FU) + k * FU, FU)] for t in wF], FU)
            if u in (20, 24):
                k = (u - 20) // 4
                split_unit(v, base, c.per - 2 + k, cut(c.slots[0], k * RAW, RAW), RAW)

        def stats_of(g):
            seqs = range(g * GB, (g + 1) * GB)
            v.wait_ge(c.s["comb_done"], (E_OUT - 1) * B + (g + 1) * GB + 2 * GB)
            for t in seqs:
                n[0] += 1
                nc.vector.bn_stats(stats[:, t, :], X[:, t, :]).then_inc(c.s["step"], 1)
            v.wait_ge(c.s["step"], n[0])
            for t in seqs:
                n[0] += 1
                nc.vector.bn_aggr(mv[:, t, :], stats[:, t, :]).then_inc(c.s["step"], 1)
            v.wait_ge(c.s["step"], n[0])
            own = slice(g * GB, (g + 1) * GB)
            nc.vector.tensor_scalar(veps[:, own].unsqueeze(2), mv[:, own, 1:2], LN_EPS, None, ALU.add).then_inc(c.s["ln_var"], 1)

        def normalise(g):
            v.wait_ge(c.s["rstd_ready"], g + (2 if c.gelu else 1))
            for t in range(g * GB, (g + 1) * GB):
                nc.vector.tensor_scalar(X[:, t, :], X[:, t, :], mv[:, t, 0:1], rstd[:, t:t + 1],
                                        ALU.subtract, ALU.mult).then_inc(c.s["x_done"], 1)

        for kind, k in mix_order(c):
            if kind == "w":
                split_unit(v, c.first, k, cut(c.slots[0], k * RAW, RAW), RAW)
            elif kind == "x" and not (c.gelu and k < 4):
                mix_transposed_x(v, c, k)
            elif kind == "u":
                hidden(0, k)
                weights(0, k)
            elif kind == "g":
                gate_scale(v, c, n, k)
            elif kind == "c":
                combine(0, k)
        if beside:
            beside()
        with v.Fori(1, E_OUT // 2 - 1) as i:
            mix_biases(c, i)
            for u in range(NU):
                hidden(i, u)
                if u >= HC + 2 and u % HC == 2:
                    combine(i, u // HC - 1)
                weights(i, u)
            combine(i, 2 * NG - 1)
        i = E_OUT // 2 - 1
        mix_biases(c, i)
        for u in range(NU):
            hidden(i, u)
            q = u // HC - 1
            if u >= HC + 2 and u % HC == 2:
                combine(i, q)
                if q >= NG:
                    stats_of(q - NG)
            if u % HC == 3 and q >= NG:
                normalise(q - NG)
            weights(i, u)
        combine(i, 2 * NG - 1)
        stats_of(NG - 1)
        if following:
            following()
        normalise(NG - 1)
        v.wait_ge(c.s["x_done"], B)

    F3 = Stage()
    m = r2.again()
    F3.Xs = m.place("f3Xs", [P, GB, D], F32)
    F3.XT = pair(m, "f3XT", [P, DC, GT])
    F3.gs = m.place("f3gs", [P, 2, GT], F32)
    F3.tt = m.place("f3tt", [P, 2, GT], F32)
    F3.h32 = m.place("f3h32", [P, 2, GT], F32)
    F3.hT = pair(m, "f3hT", [P, 3, GT])
    F3.r = m.place("f3r", [P, GB, D], F32)
    m2 = Region(nc, M2.end, r2.end - M2.end)
    F3.sel32 = m2.place("f3sel32", [R_N, FC - SC, P], F32)
    F3.sel = r1b.place("f3sel", [R_N, FC - SC, P], F32R)
    F3.combT = pair(m, "f3combT", [R_N, GT])
    F3.lg = m.place("f3lg", [P, GB, R_N], F32)
    F3.pr = m.place("f3pr", [P, GB, R_N + 6], F32)
    F3.mr = m.place("f3mr", [P, GB, R_N + 6], F32)
    F3.comb = m.place("f3comb", [P, GB, R_N], F32)
    F3.top = m.place("f3top", [P, GB, 8], F32)
    F3.t1 = m.place("f3t1", [P, GB], F32)
    F3.t2 = m.place("f3t2", [P, GB], F32)
    F3.s = signals("f3", "xs_loaded xt_hi g_full g_evac soft_exp comb_ready gu_full sg_ready t_done hi_ready h_ready "
                         "d_full r_done ln_var rstd_ready x_done sel_pool sel_ready")
    assert m.at <= V45_at
    FG = 2 + FC - SC + DC
    F_LINKS = 18 + 2 * GB

    def ffn_order(first, last):
        order = [("l", 0), ("e", 0)]
        if not first:
            order.append(("a", 0))
        order.append(("r", 0))
        for c in range(FC + 1):
            if c < FC:
                order += [("u", c)] + ([("s", c)] if c >= SC else []) + [("t", c)]
            if c == SC - 1:
                order.append(("c", 0))
            if 2 <= c < FC:
                order.append(("d", c - 2))
            if c == FC and not last:
                order += [("x", k) for k in range(DC)]
            if c == FC:
                order.append(("d", c - 2))
            if c >= 1:
                order.append(("h", c - 1))
            if not first and c in (3, 4):
                order.append(("mn"[c - 3], 0))
        return order + [("d", FC - 1)]

    def ffn_groups(eng, steps):
        steps(0, ffn_order(True, False))
        with eng.Fori(1, NG - 1) as g:
            steps(g, ffn_order(False, False))
        steps(NG - 1, ffn_order(False, True))

    def ffn_full(g, k):
        return g * FG + (DC + k + 1)

    def ffn_evac(g, k):
        return g * FG + (DC + k + 3)

    FL, FT, FX = 0, 1, 2 + FC - SC

    def ffn_sync(sp):
        s = F3.s
        with sp.Fori(1, NG) as g:
            sp.wait_ge(s["xt_hi"], g * DC + C1)
            sp.dma_start(F3.Xs[:, :, :], X[:, bass.ds(g * GB, GB), :]).then_inc(s["xs_loaded"], 16)

    def ffn_selector_pool(pool):
        s = F3.s
        nc.gpsimd.memset(F3.sel32[:, :, :], 0.0).then_inc(s["sel_pool"], 1)
        pool.wait_ge(s["sel_pool"], 1)
        sel = F3.sel32[:, :, :].rearrange("e c (a m) -> e c a m", a=2)
        nc.gpsimd.affine_select(out=sel, in_=sel, compare_op=ALU.not_equal, fill=1.0, base=0,
                                pattern=[[-2, FC - SC], [-1, 2], [0, R_MID]], channel_multiplier=1).then_inc(s["sel_pool"], 1)

    def ffn_pool(pool):
        s = F3.s
        nc.gpsimd.memset(V45[:, :, :, :], 0.0).then_inc(v45_made, 1)
        with pool.Fori(0, NG) as g:
            pool.wait_ge(s["ln_var"], g + 1)
            nc.gpsimd.tensor_tensor(rstd[:, 0:GB], veps[:, 0:GB], mhalf[:, 0:GB], ALU.pow).then_inc(s["rstd_ready"], 1)

    def ffn_tensor(pe):
        s = F3.s
        wgu = [t[:, 0:2 * DC * FC * P].rearrange("p (k n) -> p k n", k=DC) for t in wF]
        wd = [t[:, 2 * DC * FC * P:].rearrange("p (k n) -> p k n", k=FC) for t in wF]
        rh, rl = (t[:, 0:32].rearrange("p (k n) -> p k n", k=DC) for t in (rw_h, rw_l))

        def g_fill(g, k):
            pe.wait_ge(s["g_evac"], ffn_evac(g, k - 2))
            return ps[:, 4 + k % 2, :]

        def up(g, c):
            pe.wait_ge(s["sg_ready"], g * FC + c + 1)
            pe.wait_ge(s["t_done"], g * FC + c + 1)
            for part in range(2):
                at = (part * FC + c) * P
                for k in range(DC):
                    last = split3(nc, ps[:, 2 * part + c % 2, :], wgu[0][:, k, at:at + P], wgu[1][:, k, at:at + P],
                                  F3.XT[0][:, k, :], F3.XT[1][:, k, :], k == 0, k == DC - 1)
            last.then_inc(s["gu_full"], 1)

        def spread(g, c):
            bank = g_fill(g, c)
            if c == SC:
                pe.wait_ge(s["g_evac"], ffn_evac(g, FT))
            nc.tensor.matmul(bank, F3.sel[:, c - SC, :], F3.combT[0][:, :], start=True, stop=False)
            nc.tensor.matmul(bank, F3.sel[:, c - SC, :], F3.combT[1][:, :], start=False, stop=True).then_inc(s["g_full"], 1)

        def down(g, c):
            pe.wait_ge(s["h_ready"], g * FC + c + 1 + C1)
            if c == 0:
                pe.wait_ge(s["r_done"], g * GB + C1)
            for j in range(GB):
                acc = ps[:, 6 + j // 2, (j % 2) * D:(j % 2 + 1) * D]
                last = split3(nc, acc, F3.hT[0][:, c % 3, j * S:(j + 1) * S], F3.hT[1][:, c % 3, j * S:(j + 1) * S],
                              wd[0][:, c, :], wd[1][:, c, :], c == 0 and j % 2 == 0, c == FC - 1 and j % 2 == 1,
                              skip_group_check=True)
            if c == FC - 1:
                last.then_inc(s["d_full"], 1)

        def transposed_x(g, ch):
            src = X if type(g) is int and g < 0 else F3.Xs
            if src is F3.Xs:
                pe.wait_ge(s["xs_loaded"], (g + 1) * 16)
            bank = g_fill(g, FX + ch)
            for j in range(GB):
                last = nc.tensor.transpose(bank[:, j * S:(j + 1) * S], src[:, j, ch * P:(ch + 1) * P], ident[:, :])
            last.then_inc(s["g_full"], 1)

        def logits(g):
            bank = g_fill(g, FL)
            pe.wait_ge(s["g_evac"], ffn_evac(g, -1))
            for j in range(GB):
                for i in range(DC):
                    last = split3(nc, bank[:, j * R_N:(j + 1) * R_N], F3.XT[0][:, i, j * S:(j + 1) * S],
                                  F3.XT[1][:, i, j * S:(j + 1) * S], rh[:, i, :], rl[:, i, :], i == 0, i == DC - 1)
            last.then_inc(s["g_full"], 1)

        def gates_transposed(g):
            bank = g_fill(g, FT)
            pe.wait_ge(s["comb_ready"], g + 1)
            for j in range(GB):
                last = nc.tensor.transpose(bank[0:R_N, j * S:(j + 1) * S], F3.comb[:, j, :], ident[:, :])
            last.then_inc(s["g_full"], 1)

        def steps(g, order):
            for kind, c in order:
                if kind == "x":
                    transposed_x(g, c)
                elif kind == "l":
                    logits(g)
                elif kind == "u":
                    up(g, c)
                elif kind == "c":
                    gates_transposed(g)
                elif kind == "s":
                    spread(g, c)
                elif kind == "d":
                    down(g, c)

        pe.wait_ge(s["sel_ready"], 1)
        for ch in range(DC):
            transposed_x(-1, ch)
        ffn_groups(pe, steps)

    def ffn_scalar(act):
        s = F3.s
        act.sem_inc(s["sg_ready"], 2)
        act.sem_inc(s["xt_hi"], C1)

        def transposed_x(g, ch):
            act.wait_ge(s["g_full"], ffn_full(g, FX + ch))
            nc.scalar.activation(F3.XT[0][:, ch, :], ps[:, 4 + ch % 2, :], ACT.Identity).then_inc(s["xt_hi"], 1)

        def steps(g, order):
            for kind, c in order:
                if kind == "x":
                    transposed_x(g, c)
                elif kind == "e":
                    act.wait_ge(s["g_evac"], ffn_evac(g, FL))
                    nc.scalar.activation(F3.pr[:, :, 0:R_N], F3.lg[:, :, :], ACT.Exp).then_inc(s["soft_exp"], 1)
                elif kind == "u":
                    act.wait_ge(s["gu_full"], g * FC + c + 1)
                    nc.scalar.activation(F3.gs[:, c % 2, :], ps[:, c % 2, :], ACT.Silu).then_inc(s["sg_ready"], 1)
                elif kind == "h":
                    if c < SC:
                        act.wait_ge(s["t_done"], g * FC + c + 3)
                    else:
                        act.wait_ge(s["g_evac"], ffn_evac(g, c))
                    nc.scalar.activation(F3.hT[0][:, c % 3, :], F3.h32[:, c % 2, :], ACT.Identity).then_inc(s["hi_ready"], 1)

        for ch in range(DC):
            transposed_x(-1, ch)
        ffn_groups(act, steps)

    def ffn_selector(v):
        v.wait_ge(F3.s["sel_pool"], 2)
        nc.vector.tensor_copy(F3.sel[:, :, :], F3.sel32[:, :, :]).then_inc(F3.s["sel_ready"], 1)

    def ffn_transposed_x(v, g, ch):
        s = F3.s
        v.wait_ge(s["xt_hi"], (g + 1) * DC + ch + 1 + C1)
        nc.vector.tensor_tensor(F3.XT[1][:, ch, :], ps[:, 4 + ch % 2, :], F3.XT[0][:, ch, :].bitcast(F32),
                                ALU.subtract).then_inc(s["g_evac"], 1)

    def ffn_vector_start(v):
        s = F3.s
        v.sem_inc(s["g_evac"], 2)
        v.sem_inc(s["t_done"], 2)
        v.sem_inc(s["r_done"], C1)
        v.sem_inc(s["h_ready"], C1)
        for ch in range(DC):
            ffn_transposed_x(v, -1, ch)
        nc.vector.memset(F3.pr[:, :, R_N:], -1.0).then_inc(s["sel_ready"], 1)
        v.wait_ge(s["sel_ready"], 2)

    def ffn_vector(v, link, following):
        s = F3.s

        def over(t, n):
            return t.unsqueeze(2).broadcast_to([P, GB, n])

        def logits(g):
            v.wait_ge(s["g_full"], ffn_full(g, FL))
            lgp = ps[:, 4, 0:GB * R_N].rearrange("p (b e) -> p b e", b=GB)
            link(nc.vector.reduce_max(F3.t1[:, :], lgp, AX.X))
            nc.vector.tensor_tensor(F3.lg[:, :, :], lgp, over(F3.t1[:, :], R_N), ALU.subtract).then_inc(s["g_evac"], 1)

        def router(g):
            v.wait_ge(s["soft_exp"], g + 1)
            probs = F3.pr[:, :, 0:R_N]
            link(nc.vector.reduce_sum(F3.t1[:, :], probs, AX.X))
            link(nc.vector.reciprocal(F3.t2[:, :], F3.t1[:, :]))
            link(nc.vector.tensor_tensor(probs, probs, over(F3.t2[:, :], R_N), ALU.mult), alone=True)
            for j in range(GB):
                (link if j == GB - 1 else link.note)(nc.vector.max(F3.top[:, j, :], F3.pr[:, j, 0:R_N]))
            link(nc.vector.tensor_tensor(F3.t1[:, :].unsqueeze(2), F3.top[:, :, 0:1], F3.top[:, :, 1:2], ALU.add))
            link(nc.vector.tensor_scalar(F3.t1[:, :], F3.t1[:, :], 1e-9, None, ALU.add))
            link(nc.vector.reciprocal(F3.t2[:, :], F3.t1[:, :]))
            link(nc.vector.memset(F3.top[:, :, 2:8], -1.0), alone=True)
            for j in range(GB):
                (link if j == GB - 1 else link.note)(
                    nc.vector.match_replace(F3.mr[:, j, :], F3.top[:, j, :], F3.pr[:, j, :], -2.0))
            link(nc.vector.scalar_tensor_tensor(F3.comb[:, :, :], F3.mr[:, :, 0:R_N], -2.0, probs, ALU.is_equal, ALU.mult))
            nc.vector.tensor_tensor(F3.comb[:, :, :], F3.comb[:, :, :], over(F3.t2[:, :], R_N), ALU.mult).then_inc(s["comb_ready"], 1)

        def product(g, c):
            v.wait_ge(s["sg_ready"], g * FC + c + 3)
            v.wait_ge(s["h_ready"], g * FC + max(c - 1, 0) + C1)
            dst = F3.h32 if c < SC else F3.tt
            nc.vector.tensor_tensor(dst[:, c % 2, :], F3.gs[:, c % 2, :], ps[:, 2 + c % 2, :], ALU.mult).then_inc(s["t_done"], 1)
            if c >= SC:
                v.wait_ge(s["g_full"], ffn_full(g, c))
                v.wait_ge(s["t_done"], g * FC + c + 3)
                nc.vector.tensor_tensor(F3.h32[:, c % 2, :], F3.tt[:, c % 2, :], ps[:, 4 + c % 2, :], ALU.mult).then_inc(s["g_evac"], 1)
                v.wait_ge(s["g_evac"], ffn_evac(g, c))

        def gates_transposed(g):
            v.wait_ge(s["g_full"], ffn_full(g, FT))
            src = ps[0:R_N, 4 + FT % 2, :]
            link(nc.vector.tensor_copy(F3.combT[0][:, :], src))
            nc.vector.tensor_tensor(F3.combT[1][:, :], src, F3.combT[0][:, :].bitcast(F32), ALU.subtract).then_inc(s["g_evac"], 1)

        def residual(g):
            v.wait_ge(s["d_full"], g + 1)
            for j in range(GB):
                acc = ps[:, 6 + j // 2, (j % 2) * D:(j % 2 + 1) * D]
                nc.vector.tensor_tensor(F3.r[:, j, :], acc, X[:, g * GB + j, :], ALU.add).then_inc(s["r_done"], 1)
            v.wait_ge(s["r_done"], (g + 1) * GB + C1)

        def norm_stats(g):
            for j in range(GB):
                bn = nc.vector.bn_stats(stats[:, j, :], F3.r[:, j, :])
                if j == GB - 1:
                    link(bn, alone=True)
                else:
                    link.note(bn)
            for j in range(GB):
                (link if j == GB - 1 else link.note)(nc.vector.bn_aggr(mv[:, j, :], stats[:, j, :]))
            nc.vector.tensor_scalar(veps[:, 0:GB].unsqueeze(2), mv[:, 0:GB, 1:2], LN_EPS, None, ALU.add).then_inc(s["ln_var"], 1)

        def norm(g):
            v.wait_ge(s["rstd_ready"], g + 1)
            for j in range(GB):
                nc.vector.tensor_scalar(X[:, g * GB + j, :], F3.r[:, j, :], mv[:, j, 0:1], rstd[:, j:j + 1],
                                        ALU.subtract, ALU.mult).then_inc(s["x_done"], 1)
            v.wait_ge(s["x_done"], (g + 1) * GB)

        def steps(g, order):
            if type(g) is not int:
                link.begin(g, 1, F_LINKS)
            for kind, c in order:
                if kind == "x":
                    ffn_transposed_x(v, g, c)
                elif kind == "l":
                    logits(g)
                elif kind == "a":
                    residual(g - 1)
                elif kind == "r":
                    router(g)
                elif kind == "t":
                    product(g, c)
                    if type(g) is int and g == 0 and 4 <= c < 8:
                        k = c - 4
                        n, at = (768, k * 768) if k < 2 else (256, 1536 + (k - 2) * 256)
                        split_unit(v, U_A4, k, cut(wA4, at, n), n)
                elif kind == "c":
                    gates_transposed(g)
                elif kind == "h":
                    v.wait_ge(s["hi_ready"], g * FC + c + 1)
                    nc.vector.tensor_tensor(F3.hT[1][:, c % 3, :], F3.h32[:, c % 2, :], F3.hT[0][:, c % 3, :].bitcast(F32),
                                            ALU.subtract).then_inc(s["h_ready"], 1)
                elif kind == "m":
                    norm_stats(g - 1)
                elif kind == "n":
                    norm(g - 1)
            if type(g) is not int:
                link.end(NG - 1)

        ffn_groups(v, steps)
        residual(NG - 1)
        following()
        norm_stats(NG - 1)
        norm(NG - 1)

    class Link:

        def __init__(self, v):
            self.v, self.total, self.g, self.per, self.k = v, 0, 0, 0, 0

        def begin(self, g, first, per):
            self.total += self.k - first * per
            self.g, self.per, self.k = g, per, 0

        def note(self, ins):
            self.k += 1
            ins.then_inc(chain, 1)

        def __call__(self, ins, alone=False):
            self.note(ins)
            self.v.wait_ge(chain, self.g * self.per + (self.total + self.k))
            if alone:
                self.v.sem_inc(waited, 1)

        def end(self, beyond):
            assert self.k == self.per, (self.k, self.per)
            self.total += self.per * beyond
            self.g, self.per, self.k = 0, 0, 0

    block = nc.Block()
    with block as block:
        @block.sync
        def _(sp):
            def load_x(g):
                own = slice(g * GB, (g + 1) * GB)
                sp.dma_start(X[:, own, :], x_in[own].rearrange("b s d -> s b d")).then_inc(x_loaded, 16)

            def load_a1(k):
                sp.dma_start(raw[k % 2][:, :], w_a1[:, k * RAW:(k + 1) * RAW]).then_inc(raw_loaded[k % 2], 16)

            load_x(0)
            load_a1(0)
            load_a1(1)
            sp.dma_start(cols[:, :], cols_in).then_inc(small_loaded, 16)
            sp.dma_start(rows[:, :], rows_in.partition_broadcast(P)).then_inc(small_loaded, 16)
            sp.dma_start(bv1[:, :], bv_in.partition_broadcast(P)).then_inc(small_loaded, 16)
            sp.wait_ge(x_loaded, 16)
            attn_first_loads(sp, A1)
            for k in range(2, 8):
                sp.wait_ge(prep_done, k - 1)
                load_a1(k)
                if k >= 8 - (NG - 1):
                    load_x(k - (8 - NG))
            sp.wait_ge(x_loaded, 16 * NG)
            attn_sync(sp, A1)
            load_unit(sp, U_E0, 0, w_e1i[0], RAW)
            load_unit(sp, U_E0, 1, w_e1o[0], RAW)
            mix_sync(sp, M2)
            for k in range(4):
                n, at = (768, k * 768) if k < 2 else (256, 1536 + (k - 2) * 256)
                load_unit(sp, U_A4, k, w_a4[:, at:at + n], n)
            sp.wait_ge(stage_done, 2)
            ffn_sync(sp)
            for k in range(2):
                load_unit(sp, U_A5, k, w_a5[:, k * 768:(k + 1) * 768], 768)
            sp.wait_ge(stage_done, 3)
            attn_first_loads(sp, A4)
            attn_sync(sp, A4)
            load_unit(sp, U_E6, 0, w_e6i[0], RAW)
            load_unit(sp, U_E6, 1, w_e6o[0], RAW)
            attn_load_ctx(sp, 0, A5.ctxg[:, :], A5.s["ctx_loaded"])
            sp.wait_ge(stage_done, 4)
            sp.dma_start(b2rows[:, :, :].rearrange("p e d -> p (e d)"), b2_in.partition_broadcast(P)).then_inc(b2_loaded, 16)
            attn_first_loads(sp, A5)
            attn_sync(sp, A5)
            mix_sync(sp, M6)
            for g in range(NG):
                own = slice(g * GB, (g + 1) * GB)
                sp.wait_ge(M6.s["x_done"], (g + 1) * GB)
                sp.dma_start(out[own].rearrange("b s d -> s b d"), X[:, own, :]).then_inc(out_stored, 16)
            sp.wait_ge(out_stored, 16 * NG)

        @block.gpsimd
        def _(pool):
            nc.gpsimd.memset(ident[:, :], 0.0).then_inc(consts_pool, 1)
            pool.wait_ge(consts_pool, 1)
            nc.gpsimd.affine_select(out=ident[:, :], in_=ident[:, :], compare_op=ALU.not_equal, fill=1.0, base=0,
                                    pattern=[[-1, P]], channel_multiplier=1).then_inc(consts_pool, 1)
            nc.gpsimd.memset(head8[:, :, :], 1.0).then_inc(consts_pool, 1)
            nc.gpsimd.memset(causal[:, :, :], 0.0).then_inc(consts_pool, 1)
            nc.gpsimd.memset(band[:, :, :], 0.0).then_inc(consts_pool, 1)
            pool.wait_ge(consts_pool, 5)
            nc.gpsimd.affine_select(out=causal[:, :, :], in_=causal[:, :, :], compare_op=ALU.is_ge, fill=NEG, base=0,
                                    pattern=[[0, QH], [-1, S]], channel_multiplier=1).then_inc(consts_pool, 1)
            nc.gpsimd.affine_select(out=head8[:, :, :], in_=head8[:, :, :], compare_op=ALU.is_ge, fill=0.0, base=0,
                                    pattern=[[-64, 2], [-16, 4]], channel_multiplier=1).then_inc(consts_pool, 1)
            nc.gpsimd.affine_select(out=band[:, :, :], in_=band[:, :, :], compare_op=ALU.is_ge, fill=NEG, base=8,
                                    pattern=[[0, QH], [-1, S]], channel_multiplier=1).then_inc(consts_pool, 1)
            pool.wait_ge(consts_pool, 8)
            nc.gpsimd.affine_select(out=head8[:, :, :], in_=head8[:, :, :], compare_op=ALU.is_ge, fill=0.0, base=15,
                                    pattern=[[64, 2], [16, 4]], channel_multiplier=-1).then_inc(consts_pool, 1)
            nc.gpsimd.affine_select(out=band[:, :, :], in_=band[:, :, :], compare_op=ALU.is_ge, fill=NEG, base=8,
                                    pattern=[[0, QH], [1, S]], channel_multiplier=-1).then_inc(consts_pool, 1)
            pool.wait_ge(consts_dve, 5)
            pool.wait_ge(small_loaded, 48)
            attn_pool(pool, A1, {})
            pool.wait_ge(stage_done, 1)
            ffn_selector_pool(pool)
            mix_pool(pool, M2)
            pool.wait_ge(stage_done, 2)
            ffn_pool(pool)
            pool.wait_ge(stage_done, 3)

            def split_a5():
                for k in range(2):
                    split_unit(pool, U_A5, k, cut(wA5, k * 768, 768), 768, nc.gpsimd)

            def split_e6():
                for k in range(2):
                    split_unit(pool, U_E6, k, cut(slots6[0], k * RAW, RAW), RAW, nc.gpsimd)

            attn_pool(pool, A4, {("q", 0): split_a5})
            attn_pool(pool, A5, {("q", 0): split_e6})
            mix_pool(pool, M6)

        @block.tensor
        def _(pe):
            pe.wait_ge(consts_pool, 2)
            pe.wait_ge(x_loaded, 16)
            attn_tensor(pe, A1)
            pe.wait_ge(stage_done, 1)
            mix_tensor(pe, M2)
            pe.wait_ge(M2.s["x_done"], GB)
            ffn_tensor(pe)
            pe.wait_ge(F3.s["x_done"], GB)
            attn_tensor(pe, A4)
            pe.wait_ge(A4.s["x_done"], GB + C1)
            attn_tensor(pe, A5)
            mix_tensor(pe, M6)

        @block.scalar
        def _(act):
            attn_scalar(act, A1)
            mix_scalar(act, M2)
            ffn_scalar(act)
            attn_scalar(act, A4)
            attn_scalar(act, A5)
            mix_scalar(act, M6)

        @block.vector
        def _(v):
            link = Link(v)

            def constants():
                nc.vector.memset(mhalf[:, :], -0.5).then_inc(consts_dve, 1)
                v.wait_ge(consts_pool, 10)
                nc.vector.tensor_copy(identb[:, :], ident[:, :]).then_inc(consts_dve, 1)
                nc.vector.tensor_tensor(head[:, :], head8[:, 0, :], head8[:, 1, :], ALU.add).then_inc(consts_dve, 1)
                nc.vector.tensor_copy(rw_h[:, :], col_rw).then_inc(consts_dve, 1)
                v.wait_ge(consts_dve, 4)
                nc.vector.tensor_tensor(rw_l[:, :], col_rw, rw_h[:, :].bitcast(F32), ALU.subtract).then_inc(consts_dve, 1)

            def split_a1(k):
                split_unit(v, U_A1, k, cut(wA1, k * RAW, RAW), RAW)

            split_a1(0)
            split_a1(1)
            attn_vector_start(v, A1)
            v.wait_ge(small_loaded, 48)
            attn_vector(v, A1, link, {("q", 1): constants, ("q", 0): lambda: split_a1(2), ("q", 2): lambda: split_a1(3),
                                      ("q", 4): lambda: split_a1(4), ("q", 6): lambda: split_a1(5),
                                      ("k", 0): lambda: split_a1(6), ("k", 2): lambda: split_a1(7)})
            v.sem_inc(stage_done, 1)
            mix_vector_start(v, M2)
            mix_vector(v, M2, lambda: ffn_selector(v), lambda: ffn_vector_start(v))
            v.sem_inc(stage_done, 1)
            ffn_vector(v, link, lambda: attn_vector_start(v, A4))
            v.sem_inc(stage_done, 1)
            attn_vector(v, A4, link, {}, lambda: attn_vector_start(v, A5))
            v.sem_inc(stage_done, 1)

            def start_m6():
                v.wait_ge(prep_done, U_PAIR6)
                mix_vector_start(v, M6)

            attn_vector(v, A5, link, {}, start_m6)
            v.sem_inc(stage_done, 1)
            mix_vector(v, M6)
            v.sem_inc(stage_done, 1)


def kernel(**inputs):
    import numpy as np
    import concourse.bacc as bacc
    from concourse import mybir as mb
    from concourse.bass_utils import run_bass_kernel_spmd as run

    a = {k: np.asarray(v) for k, v in inputs.items()}

    def chunked(w):
        k, n = w.shape
        return w.reshape(k // 128, 128, n).transpose(1, 0, 2).reshape(128, -1)

    def heads(w):
        return w.transpose(1, 0, 2).reshape(256, -1)

    def experts(w):
        return np.stack([chunked(e) for e in w])

    x = {}
    x["x"] = a["x"]
    x["ctxT"] = a["ctx_512"].transpose(2, 0, 1).reshape(128, -1)
    x["itokT"] = a["itok_BxS2xS_0_7"].transpose(2, 0, 1).reshape(128, -1)
    x["w_a1"] = np.concatenate([chunked(heads(a[f"L0_attn_W_{n}"])) for n in "QKV"]
                               + [chunked(a["L0_attn_W_O"].reshape(-1, 256))], 1)
    x["w_e1i"] = experts(a["L0_xattn_proj_in"].transpose(0, 2, 1))
    x["w_e1o"] = experts(a["L0_xattn_proj_out"].transpose(0, 2, 1))
    gu = [heads(a[f"L0_ffn_w{n}"]) for n in ("g_s", "g_r", "u_s", "u_r")]
    down = [a[f"L0_ffn_wd_{n}"].reshape(-1, 256) for n in "sr"]
    x["w_ffn"] = np.concatenate([chunked(np.concatenate(gu, 1)), chunked(np.concatenate(down, 0))], 1)
    x["w_a4"] = np.concatenate([chunked(a["L1_attn_Wqkv"]), chunked(a["L1_attn_Wproj"])], 1)
    x["w_a5"] = np.concatenate([chunked(a[f"L1_xattn_W{n}"]) for n in "qkvo"], 1)
    x["w_e6i"] = experts(a["L1_ffn_w1"])
    x["w_e6o"] = experts(a["L1_ffn_w2"])
    x["cols"] = np.concatenate([a["L0_attn_b_Q"].reshape(-1, 128).T, a["L0_attn_b_K"].reshape(-1, 128).T,
                                a["L1_xattn_bq"].reshape(-1, 128).T, a["L1_xattn_bk"].reshape(-1, 128).T,
                                a["L1_ffn_b1"].reshape(-1, 128).T, chunked(a["L0_ffn_router_w"]),
                                chunked(a["L1_ffn_gate_w"].T)], 1)
    x["rows"] = np.concatenate([a["L0_attn_b_O"], a["L1_attn_bproj"], a["L1_xattn_bv"], a["L1_xattn_bo"],
                                a["L1_ffn_gate_b"], a["L1_ffn_rms_w"]])
    x["bv"] = a["L0_attn_b_V"].reshape(-1)
    x["b2"] = a["L1_ffn_b2"].reshape(-1)
    nc = bacc.Bacc("TRN2", target_bir_lowering=False, num_devices=1)
    arrays, args = {}, []
    for name, v in x.items():
        v = np.ascontiguousarray(v)
        arrays[f"in_{name}"] = v
        args.append(nc.dram_tensor(f"in_{name}", v.shape, mb.dt.from_np(v.dtype), kind="ExternalInput").ap())
    args.append(nc.dram_tensor("out_0", (16, 128, 256), mb.dt.float32, kind="ExternalOutput").ap())
    program(nc, *args)
    r = run(nc, [arrays], core_ids=[0])
    return r.results[0]["out_0"]
```
